# Optimizing a Trainium2 kernel written in Bass

```python
import numpy as np
import jax
import jax.numpy as jnp

def _softmax(x, axis=-1):
    return jax.nn.softmax(x, axis=axis)

def _gelu(x):
    return jax.nn.gelu(x, approximate=True)

def _silu(x):
    return jax.nn.silu(x)

def _sigmoid(x):
    return jax.nn.sigmoid(x)

def _layernorm(x, axis=-1, eps=1e-05):
    m = jnp.mean(x, axis=axis, keepdims=True)
    v = jnp.var(x, axis=axis, keepdims=True)
    return (x - m) / jnp.sqrt(v + eps)

def _scatter_add(tgt, idx, src, axis=0):
    return tgt.at[idx].add(src)

def _segment_sum(src, seg, n):
    return jax.ops.segment_sum(src, seg, n)
kernel_name = 'mk_macaron_d4_jaxref_r8_4f9ed2'

def setup_inputs(seed: int=0):
    np.random.seed(seed)
    _w = jnp.asarray

    def _L0_attn_setup():
        import jax, jax.numpy as jnp
        import numpy as np
        B, N, E, H = (1, 512, 256, 16)
        D = E // H
        DEGREE = 4
        LN_EPS = 1e-05
        ROPE_BASE = 10000.0

        def rope_cos_sin(n, d):
            inv_freq = 1.0 / ROPE_BASE ** (jnp.arange(0, d, 2, dtype=jnp.float32) / d)
            t = jnp.arange(n, dtype=jnp.float32)[:, None] * inv_freq[None, :]
            return (jnp.cos(t), jnp.sin(t))

        def apply_rope(x, cos, sin):
            x1, x2 = jnp.split(x, 2, axis=-1)
            c = cos[None, :, None, :]
            s = sin[None, :, None, :]
            return jnp.concatenate([x1 * c - x2 * s, x1 * s + x2 * c], axis=-1)

        def layernorm(x, scale, bias, eps=LN_EPS):
            m = jnp.mean(x, axis=-1, keepdims=True)
            v = jnp.var(x, axis=-1, keepdims=True)
            return (x - m) * jax.lax.rsqrt(v + eps) * scale + bias

        def polynomial_attention(q, k, v, degree, is_causal):
            a = jnp.einsum('bhnd,bhmd->bhnm', q, k) ** degree
            if is_causal:
                a = jnp.tril(a)
            denom = jnp.sum(a, axis=-1, keepdims=True)
            return jnp.einsum('bhnm,bhmd->bhnd', a / denom, v)
        key = jax.random.key(seed)
        k0, k1, k2 = jax.random.split(key, 3)
        x = jax.random.normal(k0, (B, N, E), dtype=jnp.float32)
        w_qkv = jax.random.normal(k1, (E, 3 * E), dtype=jnp.float32) * (1.0 / np.sqrt(E))
        w_out = jax.random.normal(k2, (E, E), dtype=jnp.float32) * (1.0 / np.sqrt(E))
        ln_scale = jnp.ones((D,), dtype=jnp.float32)
        ln_bias = jnp.zeros((D,), dtype=jnp.float32)
        return {'x': x, 'w_qkv': w_qkv, 'w_out': w_out, 'ln_scale': ln_scale, 'ln_bias': ln_bias}
    _L0_attn_in = _L0_attn_setup()

    def _L0_ffn_setup():
        import jax, jax.numpy as jnp
        import numpy as np
        HIDDEN = 256
        INTER = 688
        LUT_SIZE = 16

        def _ghost_linear(x, idx, lut):
            w = lut[idx]
            return jnp.einsum('bsh,oh->bso', x, w)
        key = jax.random.key(seed)
        k_x, k_lut, k_g, k_u, k_d = jax.random.split(key, 5)
        x = jax.random.normal(k_x, (2, 512, HIDDEN), dtype=jnp.float32)
        lut = jax.random.normal(k_lut, (LUT_SIZE,), dtype=jnp.float32) * 0.02
        gate_idx = jax.random.randint(k_g, (INTER, HIDDEN), 0, LUT_SIZE, dtype=jnp.int32)
        up_idx = jax.random.randint(k_u, (INTER, HIDDEN), 0, LUT_SIZE, dtype=jnp.int32)
        down_idx = jax.random.randint(k_d, (HIDDEN, INTER), 0, LUT_SIZE, dtype=jnp.int32)
        return {'x': x, 'lut': lut, 'gate_idx': gate_idx, 'up_idx': up_idx, 'down_idx': down_idx}
    _L0_ffn_in = _L0_ffn_setup()

    def _L1_attn_setup():
        import jax, jax.numpy as jnp
        import numpy as np
        H, DH, DR = (16, 128, 64)
        DN = DH - DR
        EPS = 1e-06

        def rmsnorm(x, w):
            return x * jax.lax.rsqrt(jnp.mean(x * x, axis=-1, keepdims=True) + EPS) * w

        def apply_rope(x, f):
            B, S, Hh, dr = x.shape
            xp = x.reshape(B, S, Hh, dr // 2, 2)
            x0, x1 = (xp[..., 0], xp[..., 1])
            cos, sin = (f[..., 0], f[..., 1])
            r0 = x0 * cos - x1 * sin
            r1 = x0 * sin + x1 * cos
            return jnp.stack([r0, r1], axis=-1).reshape(B, S, Hh, dr)
        key = jax.random.key(seed)
        ks = jax.random.split(key, 6)
        B, S, D, DL = (2, 256, 256, 64)
        x = jax.random.normal(ks[0], (B, S, D), jnp.float32)
        pos = jnp.arange(S, dtype=jnp.float32)[:, None]
        inv = 1.0 / 10000.0 ** (jnp.arange(0, DR, 2, dtype=jnp.float32) / DR)
        theta = pos * inv
        freqs = jnp.stack([jnp.cos(theta), jnp.sin(theta)], axis=-1)
        sc = lambda k, sh: jax.random.normal(k, sh, jnp.float32) * 0.02
        wq_w = sc(ks[1], (H * DH, D))
        wq_b = jnp.zeros((H * DH,), jnp.float32)
        wkv_a_w = sc(ks[2], (DL, D))
        wkv_b_w = sc(ks[3], (2 * H * DH, DL))
        norm_w = jnp.ones((DL,), jnp.float32)
        out_w = sc(ks[4], (D, H * DH))
        out_b = jnp.zeros((D,), jnp.float32)
        return dict(x=x, freqs=freqs, wq_w=wq_w, wq_b=wq_b, wkv_a_w=wkv_a_w, wkv_b_w=wkv_b_w, norm_w=norm_w, out_w=out_w, out_b=out_b)
    _L1_attn_in = _L1_attn_setup()

    def _L1_ffn_setup():
        import jax, jax.numpy as jnp
        import numpy as np
        E = 8
        TOP_K = 2
        D = 256
        DE = 176
        DS = 352
        B, S = (2, 256)
        key = jax.random.key(seed)
        ks = jax.random.split(key, 8)
        std = 0.02
        return {'x': jax.random.normal(ks[0], (B, S, D), jnp.float32), 'W_router': jax.random.normal(ks[1], (D, E), jnp.float32) * std, 'We_gate': jax.random.normal(ks[2], (E, D, DE), jnp.float32) * std, 'We_up': jax.random.normal(ks[3], (E, D, DE), jnp.float32) * std, 'We_down': jax.random.normal(ks[4], (E, DE, D), jnp.float32) * std, 'Ws_gate': jax.random.normal(ks[5], (D, DS), jnp.float32) * std, 'Ws_up': jax.random.normal(ks[6], (D, DS), jnp.float32) * std, 'Ws_down': jax.random.normal(ks[7], (DS, D), jnp.float32) * std}
    _L1_ffn_in = _L1_ffn_setup()

    def _L2_attn_setup():
        import jax, jax.numpy as jnp
        import numpy as np
        H = 256
        NH = 16
        D = 128
        K = 4

        def _causal_depthwise_conv(x, w, b):
            S = x.shape[1]
            xp = jnp.pad(x, ((0, 0), (K - 1, 0), (0, 0)))
            y = b
            for j in range(K):
                y = y + xp[:, j:j + S, :] * w[:, j]
            return y

        def _forward(x, Wq, Wk, Wv, Wa, ba, Wb, bb, Wg, Wo, qcw, qcb, kcw, kcb, vcw, vcb, ln_w, ln_b):
            B, S, _ = x.shape
            q = _causal_depthwise_conv(x @ Wq, qcw, qcb)
            k = _causal_depthwise_conv(x @ Wk, kcw, kcb)
            v = _causal_depthwise_conv(x @ Wv, vcw, vcb)
            q = jax.nn.silu(q).reshape(B, S, NH, D)
            k = jax.nn.silu(k).reshape(B, S, NH, D) * D ** (-0.5)
            v = jax.nn.silu(v).reshape(B, S, NH, D)
            alpha = jax.nn.sigmoid(x @ Wa + ba)
            beta = jax.nn.sigmoid(x @ Wb + bb)
            qt = jnp.moveaxis(q, 1, 0)
            kt = jnp.moveaxis(k, 1, 0)
            vt = jnp.moveaxis(v, 1, 0)
            at = jnp.moveaxis(alpha, 1, 0)
            bt = jnp.moveaxis(beta, 1, 0)

            def step(St, inp):
                q_, k_, v_, a_, b_ = inp
                sk = jnp.einsum('bhij,bhj->bhi', St, k_)
                err = sk - v_
                Sn = a_[..., None, None] * St - b_[..., None, None] * err[..., None] * k_[..., None, :]
                o_ = jnp.einsum('bhij,bhj->bhi', Sn, q_)
                return (Sn, o_)
            S0 = jnp.zeros((B, NH, D, D), dtype=x.dtype)
            _, o = jax.lax.scan(step, S0, (qt, kt, vt, at, bt))
            o = jnp.moveaxis(o, 0, 1)
            mu = jnp.mean(o, axis=-1, keepdims=True)
            var = jnp.mean(jnp.square(o - mu), axis=-1, keepdims=True)
            o = (o - mu) * jax.lax.rsqrt(var + 1e-05) * ln_w + ln_b
            g = jax.nn.sigmoid(x @ Wg).reshape(B, S, NH, D)
            o = (o * g).reshape(B, S, NH * D)
            return o @ Wo
        key = jax.random.key(seed)
        ks = jax.random.split(key, 18)
        s = 0.02
        B, S = (2, 256)
        return {'x': jax.random.normal(ks[0], (B, S, H), dtype=jnp.float32), 'Wq': jax.random.normal(ks[1], (H, NH * D), dtype=jnp.float32) * s, 'Wk': jax.random.normal(ks[2], (H, NH * D), dtype=jnp.float32) * s, 'Wv': jax.random.normal(ks[3], (H, NH * D), dtype=jnp.float32) * s, 'Wa': jax.random.normal(ks[4], (H, NH), dtype=jnp.float32) * s, 'ba': jax.random.normal(ks[5], (NH,), dtype=jnp.float32) * s, 'Wb': jax.random.normal(ks[6], (H, NH), dtype=jnp.float32) * s, 'bb': jax.random.normal(ks[7], (NH,), dtype=jnp.float32) * s, 'Wg': jax.random.normal(ks[8], (H, NH * D), dtype=jnp.float32) * s, 'Wo': jax.random.normal(ks[9], (NH * D, H), dtype=jnp.float32) * s, 'qcw': jax.random.normal(ks[10], (NH * D, K), dtype=jnp.float32) * s, 'qcb': jax.random.normal(ks[11], (NH * D,), dtype=jnp.float32) * s, 'kcw': jax.random.normal(ks[12], (NH * D, K), dtype=jnp.float32) * s, 'kcb': jax.random.normal(ks[13], (NH * D,), dtype=jnp.float32) * s, 'vcw': jax.random.normal(ks[14], (NH * D, K), dtype=jnp.float32) * s, 'vcb': jax.random.normal(ks[15], (NH * D,), dtype=jnp.float32) * s, 'ln_w': jnp.ones((D,), dtype=jnp.float32), 'ln_b': jnp.zeros((D,), dtype=jnp.float32)}
    _L2_attn_in = _L2_attn_setup()

    def _L2_ffn_setup():
        import jax, jax.numpy as jnp
        import numpy as np
        E = 64
        K = 6
        CAP = 64
        SCALE = 1.0
        H = 256
        I = 96
        SI = I * 2
        B, S = (2, 128)

        def _moe(x, gate_w, gate_up_proj, down_proj, shared_gate_w, shared_up_w, shared_down_w):
            b, s, h = x.shape
            T = b * s
            xf = x.reshape(T, h)
            scores = jax.nn.softmax(xf @ gate_w.T, axis=-1)
            topk_w, topk_idx = jax.lax.top_k(scores, K)
            topk_w = topk_w * SCALE
            flat_e = topk_idx.reshape(-1)
            order = jnp.argsort(flat_e)
            sorted_e = flat_e[order]
            sorted_tok = (order // K).astype(jnp.int32)
            sorted_w = topk_w.reshape(-1)[order]
            counts = jnp.zeros((E,), jnp.int32).at[flat_e].add(1)
            offsets = jnp.cumsum(counts) - counts
            pos = jnp.arange(T * K, dtype=jnp.int32) - offsets[sorted_e]
            buf_tok = jnp.full((E, CAP), T, jnp.int32).at[sorted_e, pos].set(sorted_tok, mode='drop')
            buf_w = jnp.zeros((E, CAP), x.dtype).at[sorted_e, pos].set(sorted_w, mode='drop')
            xp = jnp.concatenate([xf, jnp.zeros((1, h), x.dtype)], axis=0)
            gx = xp[buf_tok]
            gu = jnp.einsum('ech,ehi->eci', gx, gate_up_proj)
            g, u = jnp.split(gu, 2, axis=-1)
            hid = jax.nn.silu(g) * u
            eo = jnp.einsum('eci,eih->ech', hid, down_proj) * buf_w[..., None]
            routed = jnp.zeros((T + 1, h), x.dtype).at[buf_tok.reshape(-1)].add(eo.reshape(-1, h))[:T]
            shared = jax.nn.silu(xf @ shared_gate_w.T) * (xf @ shared_up_w.T) @ shared_down_w.T
            return (routed + shared).reshape(b, s, h)
        key = jax.random.key(seed)
        ks = jax.random.split(key, 7)
        x = jax.random.normal(ks[0], (B, S, H), jnp.float32)
        gate_w = jax.random.normal(ks[1], (E, H), jnp.float32) * 0.02
        gate_up_proj = jax.random.normal(ks[2], (E, H, 2 * I), jnp.float32) * 0.02
        down_proj = jax.random.normal(ks[3], (E, I, H), jnp.float32) * 0.02
        shared_gate_w = jax.random.normal(ks[4], (SI, H), jnp.float32) * 0.02
        shared_up_w = jax.random.normal(ks[5], (SI, H), jnp.float32) * 0.02
        shared_down_w = jax.random.normal(ks[6], (H, SI), jnp.float32) * 0.02
        return dict(x=x, gate_w=gate_w, gate_up_proj=gate_up_proj, down_proj=down_proj, shared_gate_w=shared_gate_w, shared_up_w=shared_up_w, shared_down_w=shared_down_w)
    _L2_ffn_in = _L2_ffn_setup()

    def _L3_attn_setup():
        import jax, jax.numpy as jnp
        import numpy as np
        B, T, DIM = (2, 512, 256)
        H, HKV = (16, 4)
        HD = DIM // H
        NREP = H // HKV
        R = 16
        TOPK = 64
        THETA = 10000.0

        def _rope(x, cos, sin):
            half = HD // 2
            xr = x.reshape(*x.shape[:-1], half, 2)
            a, b = (xr[..., 0], xr[..., 1])
            ra = a * cos - b * sin
            rb = a * sin + b * cos
            return jnp.stack([ra, rb], axis=-1).reshape(x.shape)
        key = jax.random.key(seed)
        ks = jax.random.split(key, 9)
        s = 0.02
        return {'x': jax.random.normal(ks[0], (B, T, DIM), jnp.float32), 'wq': jax.random.normal(ks[1], (DIM, H * HD), jnp.float32) * s, 'wk': jax.random.normal(ks[2], (DIM, HKV * HD), jnp.float32) * s, 'wv': jax.random.normal(ks[3], (DIM, HKV * HD), jnp.float32) * s, 'wo': jax.random.normal(ks[4], (DIM, DIM), jnp.float32) * s, 'wiq': jax.random.normal(ks[5], (DIM, HD), jnp.float32) * s, 'wik': jax.random.normal(ks[6], (DIM, HD), jnp.float32) * s, 'cwa': jax.random.normal(ks[7], (HD,), jnp.float32) * s, 'cwb': jax.random.normal(ks[8], (HD,), jnp.float32) * s}
    _L3_attn_in = _L3_attn_setup()

    def _L3_ffn_setup():
        import jax, jax.numpy as jnp
        import numpy as np
        BLOCK = 64

        def dequant4bit(q, scale):
            return (q.astype(jnp.float32) - 7.5) * jnp.repeat(scale, BLOCK, axis=1)
        key = jax.random.key(seed)
        ks = jax.random.split(key, 11)
        B, S, D, H, R = (4, 256, 256, 1024, 16)
        return {'x1': jax.random.normal(ks[0], (B, S, D), jnp.float32), 'w_up_q': jax.random.randint(ks[1], (H, D), 0, 16, dtype=jnp.int32), 'w_up_scale': jax.random.uniform(ks[2], (H, D // BLOCK), jnp.float32) * 0.02, 'b_up': jax.random.normal(ks[3], (H,), jnp.float32) * 0.01, 'w_up_lora_a': jax.random.normal(ks[4], (D, R), jnp.float32) * 0.02, 'w_up_lora_b': jax.random.normal(ks[5], (R, H), jnp.float32) * 0.02, 'w_down_q': jax.random.randint(ks[6], (D, H), 0, 16, dtype=jnp.int32), 'w_down_scale': jax.random.uniform(ks[7], (D, H // BLOCK), jnp.float32) * 0.02, 'b_down': jax.random.normal(ks[8], (D,), jnp.float32) * 0.01, 'w_down_lora_a': jax.random.normal(ks[9], (H, R), jnp.float32) * 0.02, 'w_down_lora_b': jax.random.normal(ks[10], (R, D), jnp.float32) * 0.02}
    _L3_ffn_in = _L3_ffn_setup()
    _d = {'L0_attn_x': _L0_attn_in['x'], 'L0_attn_w_qkv': _L0_attn_in['w_qkv'], 'L0_attn_w_out': _L0_attn_in['w_out'], 'L0_attn_ln_scale': _L0_attn_in['ln_scale'], 'L0_attn_ln_bias': _L0_attn_in['ln_bias'], 'L0_ffn_lut': _L0_ffn_in['lut'], 'L0_ffn_gate_idx': _L0_ffn_in['gate_idx'], 'L0_ffn_up_idx': _L0_ffn_in['up_idx'], 'L0_ffn_down_idx': _L0_ffn_in['down_idx'], 'L1_attn_freqs': _L1_attn_in['freqs'], 'L1_attn_wq_w': _L1_attn_in['wq_w'], 'L1_attn_wq_b': _L1_attn_in['wq_b'], 'L1_attn_wkv_a_w': _L1_attn_in['wkv_a_w'], 'L1_attn_wkv_b_w': _L1_attn_in['wkv_b_w'], 'L1_attn_norm_w': _L1_attn_in['norm_w'], 'L1_attn_out_w': _L1_attn_in['out_w'], 'L1_attn_out_b': _L1_attn_in['out_b'], 'L1_ffn_W_router': _L1_ffn_in['W_router'], 'L1_ffn_We_gate': _L1_ffn_in['We_gate'], 'L1_ffn_We_up': _L1_ffn_in['We_up'], 'L1_ffn_We_down': _L1_ffn_in['We_down'], 'L1_ffn_Ws_gate': _L1_ffn_in['Ws_gate'], 'L1_ffn_Ws_up': _L1_ffn_in['Ws_up'], 'L1_ffn_Ws_down': _L1_ffn_in['Ws_down'], 'L2_attn_Wq': _L2_attn_in['Wq'], 'L2_attn_Wk': _L2_attn_in['Wk'], 'L2_attn_Wv': _L2_attn_in['Wv'], 'L2_attn_Wa': _L2_attn_in['Wa'], 'L2_attn_ba': _L2_attn_in['ba'], 'L2_attn_Wb': _L2_attn_in['Wb'], 'L2_attn_bb': _L2_attn_in['bb'], 'L2_attn_Wg': _L2_attn_in['Wg'], 'L2_attn_Wo': _L2_attn_in['Wo'], 'L2_attn_qcw': _L2_attn_in['qcw'], 'L2_attn_qcb': _L2_attn_in['qcb'], 'L2_attn_kcw': _L2_attn_in['kcw'], 'L2_attn_kcb': _L2_attn_in['kcb'], 'L2_attn_vcw': _L2_attn_in['vcw'], 'L2_attn_vcb': _L2_attn_in['vcb'], 'L2_attn_ln_w': _L2_attn_in['ln_w'], 'L2_attn_ln_b': _L2_attn_in['ln_b'], 'L2_ffn_gate_w': _L2_ffn_in['gate_w'], 'L2_ffn_gate_up_proj': _L2_ffn_in['gate_up_proj'], 'L2_ffn_down_proj': _L2_ffn_in['down_proj'], 'L2_ffn_shared_gate_w': _L2_ffn_in['shared_gate_w'], 'L2_ffn_shared_up_w': _L2_ffn_in['shared_up_w'], 'L2_ffn_shared_down_w': _L2_ffn_in['shared_down_w'], 'L3_attn_wq': _L3_attn_in['wq'], 'L3_attn_wk': _L3_attn_in['wk'], 'L3_attn_wv': _L3_attn_in['wv'], 'L3_attn_wo': _L3_attn_in['wo'], 'L3_attn_wiq': _L3_attn_in['wiq'], 'L3_attn_wik': _L3_attn_in['wik'], 'L3_attn_cwa': _L3_attn_in['cwa'], 'L3_attn_cwb': _L3_attn_in['cwb'], 'L3_ffn_w_up_q': _L3_ffn_in['w_up_q'], 'L3_ffn_w_up_scale': _L3_ffn_in['w_up_scale'], 'L3_ffn_b_up': _L3_ffn_in['b_up'], 'L3_ffn_w_up_lora_a': _L3_ffn_in['w_up_lora_a'], 'L3_ffn_w_up_lora_b': _L3_ffn_in['w_up_lora_b'], 'L3_ffn_w_down_q': _L3_ffn_in['w_down_q'], 'L3_ffn_w_down_scale': _L3_ffn_in['w_down_scale'], 'L3_ffn_b_down': _L3_ffn_in['b_down'], 'L3_ffn_w_down_lora_a': _L3_ffn_in['w_down_lora_a'], 'L3_ffn_w_down_lora_b': _L3_ffn_in['w_down_lora_b']}
    _x0 = _d['L0_attn_x']
    _d['L0_attn_x'] = jax.random.normal(jax.random.fold_in(jax.random.key(seed), 1), (4, 256, 256), dtype=_x0.dtype)
    del _x0
    return _d

def reference(L0_attn_x, L0_attn_w_qkv, L0_attn_w_out, L0_attn_ln_scale, L0_attn_ln_bias, L0_ffn_lut, L0_ffn_gate_idx, L0_ffn_up_idx, L0_ffn_down_idx, L1_attn_freqs, L1_attn_wq_w, L1_attn_wq_b, L1_attn_wkv_a_w, L1_attn_wkv_b_w, L1_attn_norm_w, L1_attn_out_w, L1_attn_out_b, L1_ffn_W_router, L1_ffn_We_gate, L1_ffn_We_up, L1_ffn_We_down, L1_ffn_Ws_gate, L1_ffn_Ws_up, L1_ffn_Ws_down, L2_attn_Wq, L2_attn_Wk, L2_attn_Wv, L2_attn_Wa, L2_attn_ba, L2_attn_Wb, L2_attn_bb, L2_attn_Wg, L2_attn_Wo, L2_attn_qcw, L2_attn_qcb, L2_attn_kcw, L2_attn_kcb, L2_attn_vcw, L2_attn_vcb, L2_attn_ln_w, L2_attn_ln_b, L2_ffn_gate_w, L2_ffn_gate_up_proj, L2_ffn_down_proj, L2_ffn_shared_gate_w, L2_ffn_shared_up_w, L2_ffn_shared_down_w, L3_attn_wq, L3_attn_wk, L3_attn_wv, L3_attn_wo, L3_attn_wiq, L3_attn_wik, L3_attn_cwa, L3_attn_cwb, L3_ffn_w_up_q, L3_ffn_w_up_scale, L3_ffn_b_up, L3_ffn_w_up_lora_a, L3_ffn_w_up_lora_b, L3_ffn_w_down_q, L3_ffn_w_down_scale, L3_ffn_b_down, L3_ffn_w_down_lora_a, L3_ffn_w_down_lora_b):

    def _L0_attn_ref(x, w_qkv, w_out, ln_scale, ln_bias):
        import jax, jax.numpy as jnp
        import numpy as np
        B, N, E, H = (1, 512, 256, 16)
        D = E // H
        DEGREE = 4
        LN_EPS = 1e-05
        ROPE_BASE = 10000.0

        def rope_cos_sin(n, d):
            inv_freq = 1.0 / ROPE_BASE ** (jnp.arange(0, d, 2, dtype=jnp.float32) / d)
            t = jnp.arange(n, dtype=jnp.float32)[:, None] * inv_freq[None, :]
            return (jnp.cos(t), jnp.sin(t))

        def apply_rope(x, cos, sin):
            x1, x2 = jnp.split(x, 2, axis=-1)
            c = cos[None, :, None, :]
            s = sin[None, :, None, :]
            return jnp.concatenate([x1 * c - x2 * s, x1 * s + x2 * c], axis=-1)

        def layernorm(x, scale, bias, eps=LN_EPS):
            m = jnp.mean(x, axis=-1, keepdims=True)
            v = jnp.var(x, axis=-1, keepdims=True)
            return (x - m) * jax.lax.rsqrt(v + eps) * scale + bias

        def polynomial_attention(q, k, v, degree, is_causal):
            a = jnp.einsum('bhnd,bhmd->bhnm', q, k) ** degree
            if is_causal:
                a = jnp.tril(a)
            denom = jnp.sum(a, axis=-1, keepdims=True)
            return jnp.einsum('bhnm,bhmd->bhnd', a / denom, v)
        b, n, e = x.shape
        proj = x @ w_qkv
        q, k, v = jnp.split(proj, 3, axis=-1)
        q = q.reshape(b, n, H, D)
        k = k.reshape(b, n, H, D)
        v = v.reshape(b, n, H, D)
        cos, sin = rope_cos_sin(n, D)
        q = apply_rope(q, cos, sin)
        k = apply_rope(k, cos, sin)
        q = q.transpose(0, 2, 1, 3)
        k = k.transpose(0, 2, 1, 3)
        v = v.transpose(0, 2, 1, 3)
        q = layernorm(q, ln_scale, ln_bias)
        k = layernorm(k, ln_scale, ln_bias)
        out = polynomial_attention(q, k, v, DEGREE, True)
        out = out.transpose(0, 2, 1, 3).reshape(b, n, e)
        out = out @ w_out
        return out

    def _L0_ffn_ref(x, lut, gate_idx, up_idx, down_idx):
        import jax, jax.numpy as jnp
        import numpy as np
        HIDDEN = 256
        INTER = 688
        LUT_SIZE = 16

        def _ghost_linear(x, idx, lut):
            w = lut[idx]
            return jnp.einsum('bsh,oh->bso', x, w)
        gate = _ghost_linear(x, gate_idx, lut)
        up = _ghost_linear(x, up_idx, lut)
        h = jax.nn.silu(gate) * up
        return _ghost_linear(h, down_idx, lut)

    def _L1_attn_ref(x, freqs, wq_w, wq_b, wkv_a_w, wkv_b_w, norm_w, out_w, out_b):
        import jax, jax.numpy as jnp
        import numpy as np
        H, DH, DR = (16, 128, 64)
        DN = DH - DR
        EPS = 1e-06

        def rmsnorm(x, w):
            return x * jax.lax.rsqrt(jnp.mean(x * x, axis=-1, keepdims=True) + EPS) * w

        def apply_rope(x, f):
            B, S, Hh, dr = x.shape
            xp = x.reshape(B, S, Hh, dr // 2, 2)
            x0, x1 = (xp[..., 0], xp[..., 1])
            cos, sin = (f[..., 0], f[..., 1])
            r0 = x0 * cos - x1 * sin
            r1 = x0 * sin + x1 * cos
            return jnp.stack([r0, r1], axis=-1).reshape(B, S, Hh, dr)
        B, S, D = x.shape
        lat = rmsnorm(x @ wkv_a_w.T, norm_w)
        kv = lat @ wkv_b_w.T
        q = (x @ wq_w.T + wq_b).reshape(B, S, H, DH)
        q = jnp.concatenate([q[..., :DN], apply_rope(q[..., DN:], freqs[:H])], axis=-1)
        k, v = jnp.split(kv, 2, axis=-1)
        k = k.reshape(B, S, H, DH)
        v = v.reshape(B, S, H, DH)
        k = jnp.concatenate([k[..., :DN], apply_rope(k[..., DN:], freqs[:H])], axis=-1)
        scale = 1.0 / jnp.sqrt(jnp.float32(DH))
        scores = jnp.einsum('bqhd,bkhd->bhqk', q, k) * scale
        mask = jnp.tril(jnp.ones((S, S), dtype=bool))
        scores = jnp.where(mask, scores, jnp.float32(-jnp.inf))
        attn = jax.nn.softmax(scores, axis=-1)
        o = jnp.einsum('bhqk,bkhd->bqhd', attn, v).reshape(B, S, H * DH)
        return o @ out_w.T + out_b

    def _L1_ffn_ref(x, W_router, We_gate, We_up, We_down, Ws_gate, Ws_up, Ws_down):
        import jax, jax.numpy as jnp
        import numpy as np
        E = 8
        TOP_K = 2
        D = 256
        DE = 176
        DS = 352
        B, S = (2, 256)
        b, s, d = x.shape
        shared = jax.nn.silu(x @ Ws_gate) * (x @ Ws_up) @ Ws_down
        scores = jax.nn.softmax(x @ W_router, axis=-1)
        topk_vals, topk_idx = jax.lax.top_k(scores, TOP_K)
        onehot = jax.nn.one_hot(topk_idx, E, dtype=x.dtype)
        combine = jnp.einsum('bsk,bske->bse', topk_vals, onehot)
        combine = combine.reshape(b * s, E)
        xf = x.reshape(b * s, d)
        h = jax.nn.silu(jnp.einsum('td,edh->eth', xf, We_gate)) * jnp.einsum('td,edh->eth', xf, We_up)
        y_all = jnp.einsum('eth,ehd->etd', h, We_down)
        routed = jnp.einsum('etd,te->td', y_all, combine)
        return routed.reshape(b, s, d) + shared

    def _L2_attn_ref(x, Wq, Wk, Wv, Wa, ba, Wb, bb, Wg, Wo, qcw, qcb, kcw, kcb, vcw, vcb, ln_w, ln_b):
        import jax, jax.numpy as jnp
        import numpy as np
        H = 256
        NH = 16
        D = 128
        K = 4

        def _causal_depthwise_conv(x, w, b):
            S = x.shape[1]
            xp = jnp.pad(x, ((0, 0), (K - 1, 0), (0, 0)))
            y = b
            for j in range(K):
                y = y + xp[:, j:j + S, :] * w[:, j]
            return y

        def _forward(x, Wq, Wk, Wv, Wa, ba, Wb, bb, Wg, Wo, qcw, qcb, kcw, kcb, vcw, vcb, ln_w, ln_b):
            B, S, _ = x.shape
            q = _causal_depthwise_conv(x @ Wq, qcw, qcb)
            k = _causal_depthwise_conv(x @ Wk, kcw, kcb)
            v = _causal_depthwise_conv(x @ Wv, vcw, vcb)
            q = jax.nn.silu(q).reshape(B, S, NH, D)
            k = jax.nn.silu(k).reshape(B, S, NH, D) * D ** (-0.5)
            v = jax.nn.silu(v).reshape(B, S, NH, D)
            alpha = jax.nn.sigmoid(x @ Wa + ba)
            beta = jax.nn.sigmoid(x @ Wb + bb)
            qt = jnp.moveaxis(q, 1, 0)
            kt = jnp.moveaxis(k, 1, 0)
            vt = jnp.moveaxis(v, 1, 0)
            at = jnp.moveaxis(alpha, 1, 0)
            bt = jnp.moveaxis(beta, 1, 0)

            def step(St, inp):
                q_, k_, v_, a_, b_ = inp
                sk = jnp.einsum('bhij,bhj->bhi', St, k_)
                err = sk - v_
                Sn = a_[..., None, None] * St - b_[..., None, None] * err[..., None] * k_[..., None, :]
                o_ = jnp.einsum('bhij,bhj->bhi', Sn, q_)
                return (Sn, o_)
            S0 = jnp.zeros((B, NH, D, D), dtype=x.dtype)
            _, o = jax.lax.scan(step, S0, (qt, kt, vt, at, bt))
            o = jnp.moveaxis(o, 0, 1)
            mu = jnp.mean(o, axis=-1, keepdims=True)
            var = jnp.mean(jnp.square(o - mu), axis=-1, keepdims=True)
            o = (o - mu) * jax.lax.rsqrt(var + 1e-05) * ln_w + ln_b
            g = jax.nn.sigmoid(x @ Wg).reshape(B, S, NH, D)
            o = (o * g).reshape(B, S, NH * D)
            return o @ Wo
        return _forward(x, Wq, Wk, Wv, Wa, ba, Wb, bb, Wg, Wo, qcw, qcb, kcw, kcb, vcw, vcb, ln_w, ln_b)

    def _L2_ffn_ref(x, gate_w, gate_up_proj, down_proj, shared_gate_w, shared_up_w, shared_down_w):
        import jax, jax.numpy as jnp
        import numpy as np
        E = 64
        K = 6
        CAP = 64
        SCALE = 1.0
        H = 256
        I = 96
        SI = I * 2
        B, S = (2, 128)

        def _moe(x, gate_w, gate_up_proj, down_proj, shared_gate_w, shared_up_w, shared_down_w):
            b, s, h = x.shape
            T = b * s
            xf = x.reshape(T, h)
            scores = jax.nn.softmax(xf @ gate_w.T, axis=-1)
            topk_w, topk_idx = jax.lax.top_k(scores, K)
            topk_w = topk_w * SCALE
            flat_e = topk_idx.reshape(-1)
            order = jnp.argsort(flat_e)
            sorted_e = flat_e[order]
            sorted_tok = (order // K).astype(jnp.int32)
            sorted_w = topk_w.reshape(-1)[order]
            counts = jnp.zeros((E,), jnp.int32).at[flat_e].add(1)
            offsets = jnp.cumsum(counts) - counts
            pos = jnp.arange(T * K, dtype=jnp.int32) - offsets[sorted_e]
            buf_tok = jnp.full((E, CAP), T, jnp.int32).at[sorted_e, pos].set(sorted_tok, mode='drop')
            buf_w = jnp.zeros((E, CAP), x.dtype).at[sorted_e, pos].set(sorted_w, mode='drop')
            xp = jnp.concatenate([xf, jnp.zeros((1, h), x.dtype)], axis=0)
            gx = xp[buf_tok]
            gu = jnp.einsum('ech,ehi->eci', gx, gate_up_proj)
            g, u = jnp.split(gu, 2, axis=-1)
            hid = jax.nn.silu(g) * u
            eo = jnp.einsum('eci,eih->ech', hid, down_proj) * buf_w[..., None]
            routed = jnp.zeros((T + 1, h), x.dtype).at[buf_tok.reshape(-1)].add(eo.reshape(-1, h))[:T]
            shared = jax.nn.silu(xf @ shared_gate_w.T) * (xf @ shared_up_w.T) @ shared_down_w.T
            return (routed + shared).reshape(b, s, h)
        return _moe(x, gate_w, gate_up_proj, down_proj, shared_gate_w, shared_up_w, shared_down_w)

    def _L3_attn_ref(x, wq, wk, wv, wo, wiq, wik, cwa, cwb):
        import jax, jax.numpy as jnp
        import numpy as np
        B, T, DIM = (2, 512, 256)
        H, HKV = (16, 4)
        HD = DIM // H
        NREP = H // HKV
        R = 16
        TOPK = 64
        THETA = 10000.0

        def _rope(x, cos, sin):
            half = HD // 2
            xr = x.reshape(*x.shape[:-1], half, 2)
            a, b = (xr[..., 0], xr[..., 1])
            ra = a * cos - b * sin
            rb = a * sin + b * cos
            return jnp.stack([ra, rb], axis=-1).reshape(x.shape)
        Bx, Tx, C = x.shape
        half = HD // 2
        freqs = 1.0 / THETA ** (jnp.arange(half, dtype=jnp.float32) / half)
        ang = jnp.arange(Tx, dtype=jnp.float32)[:, None] * freqs[None, :]
        cos, sin = (jnp.cos(ang), jnp.sin(ang))
        q = (x @ wq).reshape(Bx, Tx, H, HD).transpose(0, 2, 1, 3)
        k = (x @ wk).reshape(Bx, Tx, HKV, HD).transpose(0, 2, 1, 3)
        v = (x @ wv).reshape(Bx, Tx, HKV, HD).transpose(0, 2, 1, 3)
        q = _rope(q, cos, sin)
        k = _rope(k, cos, sin)
        nb = Tx // R
        kb = k.reshape(Bx, HKV, nb, R, HD)
        vb = v.reshape(Bx, HKV, nb, R, HD)
        wa = jax.nn.softmax(kb @ cwa, axis=-1)
        wb_ = jax.nn.softmax(kb @ cwb, axis=-1)
        w = 0.5 * (wa + wb_)
        ck = jnp.einsum('bhnr,bhnrd->bhnd', w, kb)
        cv = jnp.einsum('bhnr,bhnrd->bhnd', w, vb)
        qi = x @ wiq
        ki_mean = (x @ wik).mean(axis=1)
        scores = jnp.einsum('btd,bd->bt', qi, ki_mean)
        block_scores = scores[:, :nb]
        if nb > TOPK:
            idx = jax.lax.top_k(block_scores, TOPK)[1]
            ck = jnp.take_along_axis(ck, idx[:, None, :, None], axis=2)
            cv = jnp.take_along_axis(cv, idx[:, None, :, None], axis=2)
        k_rep = jnp.repeat(ck, NREP, axis=1)
        v_rep = jnp.repeat(cv, NREP, axis=1)
        att = jax.nn.softmax(jnp.einsum('bhtd,bhsd->bhts', q, k_rep) / jnp.sqrt(jnp.float32(HD)), axis=-1)
        out = jnp.einsum('bhts,bhsd->bhtd', att, v_rep)
        out = out.transpose(0, 2, 1, 3).reshape(Bx, Tx, C)
        return out @ wo

    def _L3_ffn_ref(x1, w_up_q, w_up_scale, b_up, w_up_lora_a, w_up_lora_b, w_down_q, w_down_scale, b_down, w_down_lora_a, w_down_lora_b):
        import jax, jax.numpy as jnp
        import numpy as np
        BLOCK = 64

        def dequant4bit(q, scale):
            return (q.astype(jnp.float32) - 7.5) * jnp.repeat(scale, BLOCK, axis=1)
        w_up = dequant4bit(w_up_q, w_up_scale).T
        y1 = x1 @ w_up + b_up + x1 @ w_up_lora_a @ w_up_lora_b
        x2 = jax.nn.relu(y1)
        w_down = dequant4bit(w_down_q, w_down_scale).T
        y2 = x2 @ w_down + b_down + x2 @ w_down_lora_a @ w_down_lora_b
        return y2
    x = L0_attn_x
    x = x + 0.5 * _L0_ffn_ref(_layernorm(x, axis=-1), L0_ffn_lut, L0_ffn_gate_idx, L0_ffn_up_idx, L0_ffn_down_idx)
    x = x + _L0_attn_ref(_layernorm(x, axis=-1), L0_attn_w_qkv, L0_attn_w_out, L0_attn_ln_scale, L0_attn_ln_bias)
    x = x + 0.5 * _L0_ffn_ref(_layernorm(x, axis=-1), L0_ffn_lut, L0_ffn_gate_idx, L0_ffn_up_idx, L0_ffn_down_idx)
    x = x + 0.5 * _L1_ffn_ref(_layernorm(x, axis=-1), L1_ffn_W_router, L1_ffn_We_gate, L1_ffn_We_up, L1_ffn_We_down, L1_ffn_Ws_gate, L1_ffn_Ws_up, L1_ffn_Ws_down)
    x = x + _L1_attn_ref(_layernorm(x, axis=-1), L1_attn_freqs, L1_attn_wq_w, L1_attn_wq_b, L1_attn_wkv_a_w, L1_attn_wkv_b_w, L1_attn_norm_w, L1_attn_out_w, L1_attn_out_b)
    x = x + 0.5 * _L1_ffn_ref(_layernorm(x, axis=-1), L1_ffn_W_router, L1_ffn_We_gate, L1_ffn_We_up, L1_ffn_We_down, L1_ffn_Ws_gate, L1_ffn_Ws_up, L1_ffn_Ws_down)
    x = x + 0.5 * _L2_ffn_ref(_layernorm(x, axis=-1), L2_ffn_gate_w, L2_ffn_gate_up_proj, L2_ffn_down_proj, L2_ffn_shared_gate_w, L2_ffn_shared_up_w, L2_ffn_shared_down_w)
    x = x + _L2_attn_ref(_layernorm(x, axis=-1), L2_attn_Wq, L2_attn_Wk, L2_attn_Wv, L2_attn_Wa, L2_attn_ba, L2_attn_Wb, L2_attn_bb, L2_attn_Wg, L2_attn_Wo, L2_attn_qcw, L2_attn_qcb, L2_attn_kcw, L2_attn_kcb, L2_attn_vcw, L2_attn_vcb, L2_attn_ln_w, L2_attn_ln_b)
    x = x + 0.5 * _L2_ffn_ref(_layernorm(x, axis=-1), L2_ffn_gate_w, L2_ffn_gate_up_proj, L2_ffn_down_proj, L2_ffn_shared_gate_w, L2_ffn_shared_up_w, L2_ffn_shared_down_w)
    x = x + 0.5 * _L3_ffn_ref(_layernorm(x, axis=-1), L3_ffn_w_up_q, L3_ffn_w_up_scale, L3_ffn_b_up, L3_ffn_w_up_lora_a, L3_ffn_w_up_lora_b, L3_ffn_w_down_q, L3_ffn_w_down_scale, L3_ffn_b_down, L3_ffn_w_down_lora_a, L3_ffn_w_down_lora_b)
    x = x + _L3_attn_ref(_layernorm(x, axis=-1), L3_attn_wq, L3_attn_wk, L3_attn_wv, L3_attn_wo, L3_attn_wiq, L3_attn_wik, L3_attn_cwa, L3_attn_cwb)
    x = x + 0.5 * _L3_ffn_ref(_layernorm(x, axis=-1), L3_ffn_w_up_q, L3_ffn_w_up_scale, L3_ffn_b_up, L3_ffn_w_up_lora_a, L3_ffn_w_up_lora_b, L3_ffn_w_down_q, L3_ffn_w_down_scale, L3_ffn_b_down, L3_ffn_w_down_lora_a, L3_ffn_w_down_lora_b)
    return x

_drawn_inputs = setup_inputs


def setup_inputs(seed=0):
    import zlib

    import numpy as np

    out = dict(_drawn_inputs(seed))
    spreads = {'L0_attn_ln_scale': (1.0, 0.2),
     'L0_attn_ln_bias': (0.0, 0.1),
     'L1_attn_wq_b': (0.0, 0.8),
     'L1_attn_norm_w': (1.0, 0.6),
     'L1_attn_out_b': (0.0, 0.1),
     'L2_attn_ln_w': (1.0, 0.6),
     'L2_attn_ln_b': (0.0, 0.1)}
    factors = {'L1_attn_freqs': 64.0,
     'L1_attn_wq_w': 8.0,
     'L1_ffn_W_router': 8.0,
     'L1_ffn_We_gate': 8.0,
     'L1_ffn_We_up': 8.0,
     'L1_ffn_We_down': 8.0,
     'L1_ffn_Ws_gate': 3.106,
     'L1_ffn_Ws_up': 3.069,
     'L1_ffn_Ws_down': 3.078,
     'L2_attn_Wq': 8.0,
     'L2_attn_Wk': 8.0,
     'L2_attn_Wv': 8.0,
     'L2_attn_Wa': 8.0,
     'L2_attn_ba': 23.693,
     'L2_attn_Wb': 8.0,
     'L2_attn_bb': 33.11,
     'L2_attn_Wg': 8.0,
     'L2_attn_qcw': 8.0,
     'L2_attn_qcb': 8.0,
     'L2_attn_kcw': 8.0,
     'L2_attn_kcb': 8.0,
     'L2_attn_vcw': 8.0,
     'L2_attn_vcb': 8.0,
     'L2_ffn_gate_w': 8.0,
     'L2_ffn_gate_up_proj': 8.0,
     'L2_ffn_down_proj': 8.0,
     'L2_ffn_shared_gate_w': 4.22,
     'L2_ffn_shared_up_w': 4.173,
     'L2_ffn_shared_down_w': 4.175,
     'L3_attn_wq': 64.0,
     'L3_attn_wk': 64.0,
     'L3_attn_cwa': 64.0,
     'L3_attn_cwb': 64.0,
     'L3_ffn_b_up': 30.566,
     'L3_ffn_w_up_lora_a': 2.847,
     'L3_ffn_w_up_lora_b': 2.813,
     'L3_ffn_b_down': 35.3,
     'L3_ffn_w_down_lora_a': 2.785,
     'L3_ffn_w_down_lora_b': 2.911,
     'L3_attn_wv': 8.0,
     'L3_attn_wo': 8.0}
    for name, (base, spread) in spreads.items():
        noise = np.random.default_rng([zlib.crc32(name.encode()), seed]).standard_normal(out[name].shape)
        drawn = base * np.exp(spread * noise) if base else spread * noise
        out[name] = jnp.asarray(drawn.astype(out[name].dtype))
    for name, factor in factors.items():
        out[name] = (out[name] * factor).astype(out[name].dtype)
    return out
```

```python
from contextlib import ExitStack

import concourse.bass as bass
from concourse import mybir

ALU = mybir.AluOpType
ACT = mybir.ActivationFunctionType
F32 = mybir.dt.float32
I32 = mybir.dt.int32
BF16 = mybir.dt.bfloat16
AX_X = mybir.AxisListType.X

P = 128
BATCH, SEQ, D = 4, 256, 256
TOKENS = BATCH * SEQ
TILES = TOKENS // P
KC = D // P
HALF = 512
HALVES = TOKENS // HALF
NORM_EPS = 1e-5


class Stage:

    def __init__(self, nc, name):
        self.nc, self.name, self.ctx, self.sems = nc, name, ExitStack(), []
        self.seen = nc.next_id()

    def __enter__(self):
        return self

    def sb(self, name, shape, dt=F32):
        return self.ctx.enter_context(self.nc.sbuf_tensor(f"{self.name}_{name}_{self.seen}", shape, dt))

    def ps(self, name, shape, dt=F32):
        return self.ctx.enter_context(self.nc.psum_tensor(f"{self.name}_{name}_{self.seen}", shape, dt))

    def sem(self, name):
        s = self.nc.alloc_semaphore(f"{self.name}_{name}_{self.seen}")
        self.sems.append(s)
        return s

    def block(self):
        self.blocks = ExitStack()
        return self.blocks.enter_context(self.nc.Block())

    def __exit__(self, *failed):
        if failed[0] is None:
            self.blocks.close()
            self.nc.clear_and_free_semaphores(self.sems)
            self.nc.all_engine_barrier()
            self.ctx.close()


class Core:

    def __init__(self, nc, ctx):
        def sb(name, shape, dt=F32):
            return ctx.enter_context(nc.sbuf_tensor(name, shape, dt))

        self.x = sb("x", [P, TILES, D])
        self.xnT = sb("xnT", [P, KC, TOKENS])
        self.ident = sb("ident", [P, P])
        self.ones = sb("ones", [P, P])
        self.before = sb("before", [P, P])
        self.upto = sb("upto", [P, P])
        self.after = sb("after", [P, P])
        self.norm_eps = sb("norm_eps", [P, 1])
        self.half_col = sb("half_col", [P, 1])


def start_stage(nc, core, x_in):
    with Stage(nc, "start") as st:
        loaded = st.sem("loaded")
        filled = st.sem("filled")
        shaped = st.sem("shaped")
        block = st.block()

        @block.sync
        def _(sp):
            sp.dma_start(core.x[:], x_in.rearrange("(t p) d -> p t d", p=P)).then_inc(loaded, 16)
            sp.wait_ge(loaded, 16)

        @block.gpsimd
        def _(pool):
            pool.memset(core.ident[:], 0.0).then_inc(filled, 1)
            for m in (core.ones, core.before, core.upto, core.after):
                pool.memset(m[:], 1.0).then_inc(filled, 1)
            pool.memset(core.norm_eps[:], NORM_EPS).then_inc(filled, 1)
            pool.memset(core.half_col[:], 0.5).then_inc(filled, 1)
            pool.wait_ge(filled, 7)
            pool.affine_select(out=core.ident[:], in_=core.ident[:], compare_op=ALU.not_equal, fill=1.0,
                               base=0, pattern=[[-1, P]], channel_multiplier=1).then_inc(shaped, 1)
            pool.affine_select(out=core.before[:], in_=core.before[:], compare_op=ALU.is_gt, fill=0.0,
                               base=0, pattern=[[1, P]], channel_multiplier=-1).then_inc(shaped, 1)
            pool.affine_select(out=core.upto[:], in_=core.upto[:], compare_op=ALU.is_ge, fill=0.0,
                               base=0, pattern=[[1, P]], channel_multiplier=-1).then_inc(shaped, 1)
            pool.affine_select(out=core.after[:], in_=core.after[:], compare_op=ALU.is_gt, fill=0.0,
                               base=0, pattern=[[-1, P]], channel_multiplier=1).then_inc(shaped, 1)
            pool.wait_ge(shaped, 4)


def end_stage(nc, core, out):
    with Stage(nc, "end") as st:
        stored = st.sem("stored")
        block = st.block()

        @block.sync
        def _(sp):
            sp.dma_start(out.rearrange("(t p) d -> p t d", p=P), core.x[:]).then_inc(stored, 16)
            sp.wait_ge(stored, 16)


def norm_stage(nc, core, kept=None):
    with Stage(nc, "norm") as st:
        stats = st.sb("stats", [P, TILES, 6])
        mean_var = st.sb("mean_var", [P, TILES, 2])
        sd = st.sb("sd", [P, TILES])
        rstd = st.sb("rstd", [P, TILES])
        xn = st.sb("xn", [P, TILES, D]) if kept is None else kept
        turn = st.ps("turn", [P, KC, HALVES, HALF])
        stats_done = st.sem("stats_done")
        mean_var_done = st.sem("mean_var_done")
        sd_done = st.sem("sd_done")
        rstd_done = st.sem("rstd_done")
        xn_ready = st.sem("xn_ready")
        turned = st.sem("turned")
        per_half = TILES // HALVES
        block = st.block()

        @block.vector
        def _(dve):
            for t in range(TILES):
                dve.bn_stats(stats[:, t, :], core.x[:, t, :]).then_inc(stats_done, 1)
            for t in range(TILES):
                dve.wait_ge(stats_done, t + 1)
                dve.bn_aggr(mean_var[:, t, :], stats[:, t, :]).then_inc(mean_var_done, 1)
            dve.wait_ge(sd_done, 1)
            dve.reciprocal(rstd[:], sd[:]).then_inc(rstd_done, 1)
            dve.wait_ge(rstd_done, 1)
            for t in range(TILES):
                dve.tensor_scalar(xn[:, t, :], core.x[:, t, :], mean_var[:, t, 0:1], rstd[:, t:t + 1],
                                  ALU.subtract, ALU.mult).then_inc(xn_ready, 1)
            for h in range(HALVES):
                dve.wait_ge(turned, KC * per_half * (h + 1))
                dve.tensor_copy(core.xnT[:, 1, h * HALF:(h + 1) * HALF], turn[:, 1, h, :])

        @block.scalar
        def _(act):
            act.wait_ge(mean_var_done, TILES)
            act.activation(sd[:], mean_var[:, :, 1], ACT.Sqrt, bias=core.norm_eps[:]).then_inc(sd_done, 1)
            for h in range(HALVES):
                act.wait_ge(turned, KC * per_half * (h + 1))
                act.copy(core.xnT[:, 0, h * HALF:(h + 1) * HALF], turn[:, 0, h, :])

        @block.tensor
        def _(pe):
            for t in range(TILES):
                pe.wait_ge(xn_ready, t + 1)
                for c in range(KC):
                    pe.transpose(turn[:, c, t // per_half, (t % per_half) * P:(t % per_half + 1) * P],
                                 xn[:, t, c * P:(c + 1) * P], core.ident[:]).then_inc(turned, 1)


def gated_units_stage(nc, core, name, F, units, in_weights, out_weights, token_weights):
    with Stage(nc, name) as st:
        w_in = [st.sb(f"w_in{b}", [P, KC, 2, F]) for b in range(2)]
        w_out = [st.sb(f"w_out{b}", [F, D]) for b in range(2)]
        gate = [st.sb(f"gate{h}", [F, HALF]) for h in range(HALVES)]
        hidden = [st.sb(f"hidden{b}", [F, TOKENS]) for b in range(2)]
        ps_gate = [st.ps(f"ps_gate{h}", [P, HALF]) for h in range(HALVES)]
        ps_up = [st.ps(f"ps_up{h}", [P, HALF]) for h in range(HALVES)]
        BANKS, PER = 4, TILES // 4
        ps_down = [st.ps(f"ps_down{q}", [P, PER, D]) for q in range(BANKS)]
        w_loaded = [st.sem(f"w_loaded{b}") for b in range(2)]
        up_done = st.sem("up_done")
        silu_done = st.sem("silu_done")
        hidden_ready = st.sem("hidden_ready")
        down_bank = st.sem("down_bank")
        added = st.sem("added")
        block = st.block()
        pairs = units // 2

        def over_pairs(eng, unit, lead):
            unit(0, 0, True)
            unit(1, 1, lead == 0)
            if pairs > 1:
                with eng.Fori(1, pairs) as i:
                    unit(2 * i, 0, False)
                    unit(2 * i + 1, 1, False)

        @block.sync
        def _(sp):
            def load(u, b, first):
                if not first:
                    sp.wait_ge(down_bank, BANKS * (u - 1))
                sp.dma_start(w_in[b][:], in_weights[bass.ds(u, 1)].rearrange("a p c g f -> (a p) c g f"))\
                    .then_inc(w_loaded[b], 16)
                sp.dma_start(w_out[b][:], out_weights[bass.ds(u, 1)].rearrange("a f d -> (a f) d"))\
                    .then_inc(w_loaded[b], 16)

            over_pairs(sp, load, 0)

        @block.tensor
        def _(pe):
            def up(u, i, b, first):
                pe.wait_ge(w_loaded[b], 32 * (i + 1))
                for h in range(HALVES):
                    if not first:
                        pe.wait_ge(hidden_ready, 2 * (u - 1) + h + 1)
                    for g, bank in ((0, ps_gate[h]), (1, ps_up[h])):
                        for c in range(KC):
                            mm = pe.matmul(bank[0:F, :], w_in[b][:, c, g, :],
                                           core.xnT[:, c, h * HALF:(h + 1) * HALF],
                                           start=(c == 0), stop=(c == KC - 1))
                    mm.then_inc(up_done, 1)

            def down(u, b, first):
                pe.wait_ge(hidden_ready, 2 * u + 2)
                for q in range(BANKS):
                    if not first:
                        pe.wait_ge(added, BANKS * (u - 1) + q + 1)
                    for r in range(PER):
                        t = q * PER + r
                        mm = pe.matmul(ps_down[q][:, r, :], hidden[b][:, t * P:(t + 1) * P], w_out[b][:],
                                       start=True, stop=True)
                    mm.then_inc(down_bank, 1)

            up(0, 0, 0, True)
            up(1, 0, 1, False)
            down(0, 0, True)
            if pairs > 1:
                with pe.Fori(1, pairs) as i:
                    up(2 * i, i, 0, False)
                    down(2 * i - 1, 1, False)
                    up(2 * i + 1, i, 1, False)
                    down(2 * i, 0, False)
            down(units - 1, 1, False)

        @block.scalar
        def _(act):
            def silu(u, b, first):
                for h in range(HALVES):
                    act.wait_ge(up_done, 2 * u + h + 1)
                    if not first:
                        act.wait_ge(hidden_ready, 2 * (u - 1) + h + 1)
                    act.activation(gate[h][:], ps_gate[h][0:F, :], ACT.Silu).then_inc(silu_done, 1)

            over_pairs(act, silu, 1)

        @block.vector
        def _(dve):
            def mix(u, b, first):
                if not first:
                    dve.wait_ge(down_bank, BANKS * (u - 1))
                for h in range(HALVES):
                    dve.wait_ge(silu_done, 2 * u + h + 1)
                    dve.tensor_tensor(hidden[b][:, h * HALF:(h + 1) * HALF], gate[h][:], ps_up[h][0:F, :],
                                      ALU.mult).then_inc(hidden_ready, 1)

            def add(u, b, first):
                for q in range(BANKS):
                    dve.wait_ge(down_bank, BANKS * u + q + 1)
                    if not first:
                        dve.wait_ge(added, BANKS * (u - 1) + q + 1)
                    if token_weights is None:
                        last = dve.scalar_tensor_tensor(
                            out=core.x[:, q * PER:(q + 1) * PER, :], in0=ps_down[q][:], scalar=0.5,
                            in1=core.x[:, q * PER:(q + 1) * PER, :], op0=ALU.mult, op1=ALU.add)
                    else:
                        for t in range(q * PER, (q + 1) * PER):
                            last = dve.scalar_tensor_tensor(
                                out=core.x[:, t, :], in0=ps_down[q][:, t % PER, :],
                                scalar=token_weights[:, t, bass.ds(u, 1)],
                                in1=core.x[:, t, :], op0=ALU.mult, op1=ALU.add)
                    last.then_inc(added, 1)

            mix(0, 0, True)
            mix(1, 1, True)
            add(0, 0, True)
            if pairs > 1:
                with dve.Fori(1, pairs) as i:
                    mix(2 * i, 0, False)
                    add(2 * i - 1, 1, False)
                    mix(2 * i + 1, 1, False)
                    add(2 * i, 0, False)
            add(units - 1, 1, False)


LUT = 16
F0, UNITS0 = 86, 8


def l0_decode_stage(nc, core, lut, in_idx, out_idx, in_w, out_w):
    IN = KC * 2 * F0
    N = IN + D
    with Stage(nc, "decode") as st:
        table = st.sb("table", [P, LUT])
        idx = st.sb("idx", [P, UNITS0, N], I32)
        term = [st.sb(f"term{b}", [P, N]) for b in range(2)]
        w = st.sb("w", [P, UNITS0, N])
        table_loaded = st.sem("table_loaded")
        idx_loaded = [st.sem(f"idx_loaded{u}") for u in range(UNITS0)]
        term_done = st.sem("term_done")
        w_done = st.sem("w_done")
        stored = st.sem("stored")
        block = st.block()

        zeroed = st.sem("zeroed")

        @block.gpsimd
        def _(pool):
            pool.memset(idx[64:P, :, IN:N], 0).then_inc(zeroed, 1)

        @block.sync
        def _(sp):
            sp.dma_start(table[:], lut.partition_broadcast(P)).then_inc(table_loaded, 16)
            sp.wait_ge(zeroed, 1)
            for u in range(UNITS0):
                sp.dma_start(idx[:, u, 0:IN], in_idx[u]).then_inc(idx_loaded[u], 16)
                sp.dma_start(idx[0:F0, u, IN:N], out_idx[u]).then_inc(idx_loaded[u], 16)
            for u in range(UNITS0):
                sp.wait_ge(w_done, LUT * (u + 1))
                sp.dma_start(in_w[u].rearrange("p c g f -> p (c g f)"), w[:, u, 0:IN]).then_inc(stored, 16)
                sp.dma_start(out_w[u], w[0:F0, u, IN:N]).then_inc(stored, 16)
            sp.wait_ge(stored, 32 * UNITS0)

        @block.vector
        def _(dve):
            dve.wait_ge(table_loaded, 16)
            for u in range(UNITS0):
                dve.wait_ge(idx_loaded[u], 32)
                dve.tensor_scalar(w[:, u, :], idx[:, u, :], 0.0, table[:, 0:1],
                                  ALU.is_equal, ALU.mult).then_inc(w_done, 1)
                for j in range(1, LUT):
                    n = u * (LUT - 1) + j - 1
                    if n >= 2:
                        dve.wait_ge(w_done, u * LUT + j - 1 if j > 1 else u * LUT)
                    dve.tensor_scalar(term[n % 2][:], idx[:, u, :], float(j), table[:, j:j + 1],
                                      ALU.is_equal, ALU.mult).then_inc(term_done, 1)
                    dve.wait_ge(term_done, n + 1)
                    dve.wait_ge(w_done, u * LUT + j)
                    dve.tensor_tensor(w[:, u, :], w[:, u, :], term[n % 2][:], ALU.add).then_inc(w_done, 1)


HEAD = 16
HALF_HEAD = HEAD // 2
HEADS = D // HEAD


def rope_qkv_stage(nc, core, name, weights, angles, heads, qk, v_cols, v_view):
    N = heads * HEAD
    with Stage(nc, name) as st:
        w = st.sb("w", [P, KC, N + v_cols])
        angle = st.sb("angle", [P, 2, 2, HALF_HEAD])
        raw = [st.sb(f"raw{b}", [P, N]) for b in range(2)]
        by_cos = [st.sb(f"by_cos{b}", [P, N]) for b in range(2)]
        by_sin = [st.sb(f"by_sin{b}", [P, N]) for b in range(2)]
        ps_qk = [st.ps(f"ps_qk{b}", [P, HALF]) for b in range(2)]
        ps_v = [st.ps(f"ps_v{b}", [P, HALF]) for b in range(2)]
        loaded = st.sem("loaded")
        projected = st.sem("projected")
        raw_ready = st.sem("raw_ready")
        v_ready = st.sem("v_ready")
        cos_ready = st.sem("cos_ready")
        sin_ready = st.sem("sin_ready")
        turned = st.sem("turned")
        block = st.block()

        def pairs(ap):
            return ap.rearrange("p (h e j) -> p h e j", e=2, j=HALF_HEAD)

        def factor(t, which):
            return angle[:, t % 2, which, :].unsqueeze(1).broadcast_to([P, heads * 2, HALF_HEAD])

        @block.sync
        def _(sp):
            sp.dma_start(w[:], weights.rearrange("(c p) n -> p c n", p=P)).then_inc(loaded, 16)
            sp.dma_start(angle[:], angles).then_inc(loaded, 16)

        @block.tensor
        def _(pe):
            pe.wait_ge(loaded, 32)
            for t in range(TILES):
                if t >= 2:
                    pe.wait_ge(raw_ready, t - 1)
                    pe.wait_ge(v_ready, t - 1)
                for bank, lo, hi in ((ps_qk[t % 2], 0, N), (ps_v[t % 2], N, N + v_cols)):
                    for c in range(KC):
                        mm = pe.matmul(bank[:, 0:hi - lo], core.xnT[:, c, t * P:(t + 1) * P], w[:, c, lo:hi],
                                       start=(c == 0), stop=(c == KC - 1))
                mm.then_inc(projected, 1)

        @block.scalar
        def _(act):
            for t in range(TILES):
                act.wait_ge(projected, t + 1)
                if t >= 2:
                    act.wait_ge(cos_ready, t - 1)
                    act.wait_ge(sin_ready, t - 1)
                act.copy(raw[t % 2][:], ps_qk[t % 2][:, 0:N]).then_inc(raw_ready, 1)
                width = v_view(t).shape[-1]
                act.copy(v_view(t), ps_v[t % 2][:, 0:v_cols].rearrange("p (h d) -> p h d", d=width))\
                    .then_inc(v_ready, 1)

        @block.gpsimd
        def _(pool):
            pool.wait_ge(loaded, 32)
            for t in range(TILES):
                pool.wait_ge(raw_ready, t + 1)
                if t >= 2:
                    pool.wait_ge(turned, 2 * (t - 1))
                pool.tensor_tensor(by_sin[t % 2][:].rearrange("p (n j) -> p n j", j=HALF_HEAD),
                                   raw[t % 2][:].rearrange("p (n j) -> p n j", j=HALF_HEAD),
                                   factor(t, 1), ALU.mult).then_inc(sin_ready, 1)

        @block.vector
        def _(dve):
            dve.wait_ge(loaded, 32)

            def cosines(t):
                dve.wait_ge(raw_ready, t + 1)
                if t >= 2:
                    dve.wait_ge(turned, 2 * (t - 1))
                dve.tensor_tensor(by_cos[t % 2][:].rearrange("p (n j) -> p n j", j=HALF_HEAD),
                                  raw[t % 2][:].rearrange("p (n j) -> p n j", j=HALF_HEAD),
                                  factor(t, 0), ALU.mult).then_inc(cos_ready, 1)

            def turn(t):
                dve.wait_ge(cos_ready, t + 1)
                dve.wait_ge(sin_ready, t + 1)
                c, s, o = pairs(by_cos[t % 2][:]), pairs(by_sin[t % 2][:]), pairs(qk[:, t, :])
                dve.tensor_tensor(o[:, :, 0, :], c[:, :, 0, :], s[:, :, 1, :], ALU.subtract).then_inc(turned, 1)
                dve.tensor_tensor(o[:, :, 1, :], s[:, :, 0, :], c[:, :, 1, :], ALU.add).then_inc(turned, 1)

            cosines(0)
            for t in range(1, TILES):
                cosines(t)
                turn(t - 1)
            turn(TILES - 1)


def turn_stage(nc, core, name, src, chunks, dst):
    with Stage(nc, name) as st:
        banks = [st.ps(f"bank{b}", [P, 4, P]) for b in range(4)]
        turned = st.sem("turned")
        copied = [st.sem(f"copied{e}") for e in range(2)]
        block = st.block()

        @block.tensor
        def _(pe):
            for t in range(TILES):
                if t >= 4:
                    pe.wait_ge(copied[t % 2], (t - 4) // 2 + 1)
                for c in range(chunks):
                    tr = pe.transpose(banks[t % 4][:, c, :], src[:, t, c * P:(c + 1) * P], core.ident[:])
                tr.then_inc(turned, 1)

        @block.scalar
        def _(act):
            for t in range(0, TILES, 2):
                act.wait_ge(turned, t + 1)
                act.copy(dst[:, :, t * P:(t + 1) * P], banks[t % 4][:, 0:chunks, :]).then_inc(copied[0], 1)

        @block.vector
        def _(dve):
            for t in range(1, TILES, 2):
                dve.wait_ge(turned, t + 1)
                dve.tensor_copy(dst[:, :, t * P:(t + 1) * P], banks[t % 4][:, 0:chunks, :])\
                    .then_inc(copied[1], 1)


def project_stage(nc, core, name, oT, weights):
    with Stage(nc, name) as st:
        w = st.sb("w", [P, KC, D])
        banks = [st.ps(f"bank{q}", [P, 2, D]) for q in range(4)]
        loaded = st.sem("loaded")
        projected = st.sem("projected")
        block = st.block()

        @block.sync
        def _(sp):
            sp.dma_start(w[:], weights.rearrange("(c p) n -> p c n", p=P)).then_inc(loaded, 16)

        @block.tensor
        def _(pe):
            pe.wait_ge(loaded, 16)
            for t in range(TILES):
                for c in range(KC):
                    mm = pe.matmul(banks[t // 2][:, t % 2, :], oT[:, c, t * P:(t + 1) * P], w[:, c, :],
                                   start=(c == 0), stop=(c == KC - 1))
                mm.then_inc(projected, 1)

        @block.vector
        def _(dve):
            for q in range(4):
                dve.wait_ge(projected, 2 * q + 2)
                dve.tensor_tensor(core.x[:, 2 * q:2 * q + 2, :], core.x[:, 2 * q:2 * q + 2, :],
                                  banks[q][:], ALU.add)


def l0_head_norm_stage(nc, core, qk, scale, bias):
    PER = 2
    STEPS = TILES // PER
    ROWS = PER * 2 * HEADS
    with Stage(nc, "head_norm") as st:
        gain = st.sb("gain", [P, HEAD])
        shift = st.sb("shift", [P, HEAD])
        total = [st.sb(f"total{b}", [P, ROWS]) for b in range(STEPS)]
        squares = [st.sb(f"squares{b}", [P, ROWS, HEAD]) for b in range(2)]
        spread = [st.sb(f"spread{b}", [P, ROWS]) for b in range(STEPS)]
        sd = [st.sb(f"sd{b}", [P, ROWS]) for b in range(STEPS)]
        rstd = [st.sb(f"rstd{b}", [P, ROWS]) for b in range(STEPS)]
        loaded = st.sem("loaded")
        total_ready = st.sem("total_ready")
        mean_ready = st.sem("mean_ready")
        centred = st.sem("centred")
        squared = st.sem("squared")
        spread_ready = st.sem("spread_ready")
        sd_ready = st.sem("sd_ready")
        rstd_ready = st.sem("rstd_ready")
        scaled = st.sem("scaled")
        gained = st.sem("gained")
        block = st.block()

        def heads(s):
            return qk[:, s * PER:(s + 1) * PER, :].rearrange("p t (h d) -> p (t h) d", d=HEAD)

        def across(ap):
            return ap.unsqueeze(2).broadcast_to([P, ROWS, HEAD])

        def along(ap):
            return ap.unsqueeze(1).broadcast_to([P, ROWS, HEAD])

        @block.sync
        def _(sp):
            sp.dma_start(gain[:], scale.partition_broadcast(P)).then_inc(loaded, 16)
            sp.dma_start(shift[:], bias.partition_broadcast(P)).then_inc(loaded, 16)

        @block.vector
        def _(dve):
            def centre(s):
                dve.tensor_reduce(total[s][:], heads(s), AX_X, ALU.add).then_inc(total_ready, 1)
                dve.wait_ge(total_ready, s + 1)
                dve.tensor_scalar(total[s][:], total[s][:], 1.0 / HEAD, None, ALU.mult).then_inc(mean_ready, 1)
                dve.wait_ge(mean_ready, s + 1)
                dve.tensor_tensor(heads(s), heads(s), across(total[s][:]), ALU.subtract).then_inc(centred, 1)

            def finish(s):
                dve.wait_ge(squared, s + 1)
                dve.tensor_reduce(spread[s][:], squares[s % 2][:], AX_X, ALU.add).then_inc(spread_ready, 1)
                dve.wait_ge(sd_ready, s + 1)
                dve.reciprocal(rstd[s][:], sd[s][:]).then_inc(rstd_ready, 1)
                dve.wait_ge(rstd_ready, s + 1)
                dve.tensor_tensor(heads(s), heads(s), across(rstd[s][:]), ALU.mult).then_inc(scaled, 1)

            centre(0)
            for s in range(STEPS):
                if s + 1 < STEPS:
                    centre(s + 1)
                finish(s)

        @block.scalar
        def _(act):
            for s in range(STEPS):
                act.wait_ge(centred, s + 1)
                if s >= 2:
                    act.wait_ge(spread_ready, s - 1)
                act.activation(squares[s % 2][:], heads(s), ACT.Square).then_inc(squared, 1)
                act.wait_ge(spread_ready, s + 1)
                act.activation(sd[s][:], spread[s][:], ACT.Sqrt, bias=core.norm_eps[:],
                               scale=1.0 / HEAD).then_inc(sd_ready, 1)

        @block.gpsimd
        def _(pool):
            pool.wait_ge(loaded, 32)
            for s in range(STEPS):
                pool.wait_ge(scaled, s + 1)
                pool.tensor_tensor(heads(s), heads(s), along(gain[:]), ALU.mult).then_inc(gained, 1)
                pool.wait_ge(gained, s + 1)
                pool.tensor_tensor(heads(s), heads(s), along(shift[:]), ALU.add)


def l0_attention(nc, core, weights, angles, head_rows, scale, bias, w_out):
    VA = HEAD + 1
    GROUP = P // HEAD
    with ExitStack() as ctx:
        def sb(name, shape):
            return ctx.enter_context(nc.sbuf_tensor(f"l0a_{name}", shape, F32))

        v1 = sb("v1", [P, TILES, HEADS, VA])
        qkT = sb("qkT", [P, 2 * KC, TOKENS])
        with nc.sbuf_tensor("l0a_qk", [P, TILES, 2 * D], F32) as qk:
            rope_qkv_stage(nc, core, "l0_qkv", weights, angles, 2 * HEADS, qk, D,
                           lambda t: v1[:, t, :, 0:HEAD])
            l0_head_norm_stage(nc, core, qk, scale, bias)
            turn_stage(nc, core, "l0_turn", qk, 2 * KC, qkT)
        o = sb("o", [P, TILES, D])
        with Stage(nc, "l0_heads") as st:
            rows = st.sb("rows", [P, GROUP])
            causal = st.sb("causal", [P, 3 * P])
            own_k = [st.sb(f"own_k{b}", [P, GROUP, SEQ]) for b in range(2)]
            NB = 4
            squares = [st.sb(f"squares{b}", [P, 3 * P]) for b in range(NB)]
            masked = [st.sb(f"masked{b}", [P, 3 * P]) for b in range(NB)]
            fourth = [st.sb(f"fourth{b}", [P, 3 * P]) for b in range(NB)]
            inverse = st.sb("inverse", [P, TILES, HEADS])
            ps_s = [st.ps(f"ps_s{b}", [P, HALF]) for b in range(NB)]
            ps_o = [st.ps(f"ps_o{b}", [P, HALF]) for b in range(4)]
            rows_loaded = st.sem("rows_loaded")
            causal_ready = st.sem("causal_ready")
            ones_ready = st.sem("ones_ready")
            own_ready = st.sem("own_ready")
            scored = st.sem("scored")
            squared = st.sem("squared")
            mask_done = st.sem("mask_done")
            fourth_ready = st.sem("fourth_ready")
            summed = st.sem("summed")
            inverse_ready = st.sem("inverse_ready")
            o_ready = st.sem("o_ready")
            ALL = BATCH * HEADS
            LAG = 3
            block = st.block()

            @block.sync
            def _(sp):
                sp.dma_start(rows[:], head_rows).then_inc(rows_loaded, 16)

            @block.gpsimd
            def _(pool):
                pool.tensor_copy(causal[:, 0:P], core.upto[:]).then_inc(causal_ready, 1)
                pool.memset(causal[:, P:2 * P], 1.0).then_inc(causal_ready, 1)
                pool.tensor_copy(causal[:, 2 * P:3 * P], core.upto[:]).then_inc(causal_ready, 1)
                pool.memset(v1[:, :, :, HEAD:VA], 1.0).then_inc(ones_ready, 1)
                pool.wait_ge(rows_loaded, 16)
                for n in range(BATCH * KC):
                    b, g = n // KC, n % KC
                    if n >= 2:
                        pool.wait_ge(scored, GROUP * (n - 1))
                    pool.tensor_tensor(
                        own_k[n % 2][:],
                        qkT[:, KC + g, b * SEQ:(b + 1) * SEQ].unsqueeze(1).broadcast_to([P, GROUP, SEQ]),
                        rows[:].unsqueeze(2).broadcast_to([P, GROUP, SEQ]), ALU.mult).then_inc(own_ready, 1)

            @block.tensor
            def _(pe):
                def scores(n):
                    b, h = n // HEADS, n % HEADS
                    g, e = h // GROUP, h % GROUP
                    pe.wait_ge(own_ready, n // GROUP + 1)
                    if n >= NB:
                        pe.wait_ge(squared, n - NB + 1)
                    k = own_k[(n // GROUP) % 2]
                    q = qkT[:, g, b * SEQ:(b + 1) * SEQ]
                    pe.matmul(ps_s[n % NB][:, 0:2 * P], k[:, e, 0:P], q, start=True, stop=True)
                    pe.matmul(ps_s[n % NB][:, 2 * P:3 * P], k[:, e, P:2 * P], q[:, P:2 * P],
                              start=True, stop=True).then_inc(scored, 1)

                def values(n):
                    b, h = n // HEADS, n % HEADS
                    pe.wait_ge(fourth_ready, n + 1)
                    if h == 0 and b >= 2:
                        pe.wait_ge(o_ready, 2 * (b - 1))
                    a = fourth[n % NB]
                    out0, out1 = (ps_o[2 * (b % 2) + j][:, h * VA:(h + 1) * VA] for j in range(2))
                    pe.matmul(out0, a[:, 0:P], v1[:, 2 * b, h, :], start=True, stop=True)
                    pe.matmul(out1, a[:, P:2 * P], v1[:, 2 * b, h, :], start=True, stop=False)
                    pe.matmul(out1, a[:, 2 * P:3 * P], v1[:, 2 * b + 1, h, :], start=False, stop=True)\
                        .then_inc(summed, 1)

                pe.wait_ge(ones_ready, 1)
                for n in range(ALL + LAG):
                    if n < ALL:
                        scores(n)
                    if n >= LAG:
                        values(n - LAG)

            @block.scalar
            def _(act):
                for n in range(ALL + 1):
                    if n < ALL:
                        act.wait_ge(scored, n + 1)
                        if n >= NB:
                            act.wait_ge(mask_done, n - NB + 1)
                        act.activation(squares[n % NB][:], ps_s[n % NB][:, 0:3 * P], ACT.Square)\
                            .then_inc(squared, 1)
                    if n >= 1:
                        m = n - 1
                        act.wait_ge(mask_done, m + 1)
                        if m >= NB:
                            act.wait_ge(summed, m - NB + 1)
                        act.activation(fourth[m % NB][:], masked[m % NB][:], ACT.Square)\
                            .then_inc(fourth_ready, 1)

            @block.vector
            def _(dve):
                def norm(b):
                    dve.wait_ge(summed, HEADS * (b + 1))
                    for j in range(2):
                        t = 2 * b + j
                        bank = ps_o[2 * (b % 2) + j][:, 0:HEADS * VA].rearrange("p (h d) -> p h d", d=VA)
                        dve.reciprocal(inverse[:, t, :], bank[:, :, HEAD]).then_inc(inverse_ready, 1)
                        dve.wait_ge(inverse_ready, t + 1)
                        dve.tensor_tensor(o[:, t, :].rearrange("p (h d) -> p h d", d=HEAD), bank[:, :, 0:HEAD],
                                          inverse[:, t, :].unsqueeze(2).broadcast_to([P, HEADS, HEAD]),
                                          ALU.mult).then_inc(o_ready, 1)

                dve.wait_ge(causal_ready, 3)
                for n in range(ALL):
                    dve.wait_ge(squared, n + 1)
                    if n >= NB:
                        dve.wait_ge(fourth_ready, n - NB + 1)
                    dve.tensor_tensor(masked[n % NB][:], squares[n % NB][:], causal[:], ALU.mult)\
                        .then_inc(mask_done, 1)
                    if n % HEADS == LAG + 2 and n >= HEADS:
                        norm(n // HEADS - 1)
                norm(BATCH - 1)

        oT = sb("oT", [P, KC, TOKENS])
        turn_stage(nc, core, "l0_turn_o", o, KC, oT)
        project_stage(nc, core, "l0_project", oT, w_out)


EXPERTS1, TOP1 = 8, 2
F1, UNITS1, UNITS_PER_EXPERT1 = 88, 20, 2


def route_stage(nc, core, name, router, experts, top, repeat=1, weights=None, slot_of=None, parts=None):
    E = experts
    with Stage(nc, name) as st:
        w = st.sb("w", [P, KC, E])
        score = st.sb("score", [P, TILES, E])
        peak = st.sb("peak", [P, TILES])
        total = st.sb("total", [P, TILES])
        best = st.sb("best", [P, TILES, 8])
        above = st.sb("above", [P, TILES, E])
        equal = st.sb("equal", [P, TILES, E])
        count = [st.sb(f"count{b}", [P, TILES, E]) for b in range(2)]
        n_above = st.sb("n_above", [P, TILES])
        chosen = st.sb("chosen", [P, TILES, E])
        ps = st.ps("ps", [P, TILES, E])
        ps_rank = st.ps("ps_rank", [P, TILES, E])
        loaded = st.sem("loaded")
        logits_ready = st.sem("logits_ready")
        shifted = st.sem("shifted")
        exp_ready = st.sem("exp_ready")
        step_done = st.sem("step_done")
        chosen_ready = st.sem("chosen_ready")
        rank_ready = st.sem("rank_ready")
        block = st.block()

        def across(ap):
            return ap.unsqueeze(2).broadcast_to([P, TILES, E])

        @block.sync
        def _(sp):
            sp.dma_start(w[:], router.rearrange("(c p) n -> p c n", p=P)).then_inc(loaded, 16)

        @block.tensor
        def _(pe):
            pe.wait_ge(loaded, 16)
            for t in range(TILES):
                for c in range(KC):
                    mm = pe.matmul(ps[:, t, :], core.xnT[:, c, t * P:(t + 1) * P], w[:, c, :],
                                   start=(c == 0), stop=(c == KC - 1))
            mm.then_inc(logits_ready, 1)
            if slot_of is not None:
                pe.wait_ge(chosen_ready, 1)
                for t in range(TILES):
                    for s in range(t):
                        pe.matmul(ps_rank[:, t, :], core.ones[:], chosen[:, s, :], start=(s == 0), stop=False)
                    mm = pe.matmul(ps_rank[:, t, :], core.before[:], chosen[:, t, :], start=(t == 0), stop=True)
                mm.then_inc(rank_ready, 1)

        @block.scalar
        def _(act):
            act.wait_ge(shifted, 1)
            act.activation(score[:], score[:], ACT.Exp).then_inc(exp_ready, 1)

        @block.vector
        def _(dve):
            steps = [0]

            def link(ins):
                steps[0] += 1
                ins.then_inc(step_done, 1)
                dve.wait_ge(step_done, steps[0])

            dve.wait_ge(logits_ready, 1)
            link(dve.tensor_reduce(peak[:], ps[:], AX_X, ALU.max))
            dve.tensor_tensor(score[:], ps[:], across(peak[:]), ALU.subtract).then_inc(shifted, 1)
            dve.wait_ge(exp_ready, 1)
            link(dve.tensor_reduce(total[:], score[:], AX_X, ALU.add))
            link(dve.reciprocal(total[:], total[:]))
            link(dve.tensor_tensor(score[:], score[:], across(total[:]), ALU.mult))
            for t in range(TILES):
                last = dve.max(best[:, t, :], score[:, t, :])
                if t < TILES - 1:
                    last.then_inc(step_done, 1)
                    steps[0] += 1
            link(last)
            least = best[:, :, top - 1].unsqueeze(2).broadcast_to([P, TILES, E])
            link(dve.tensor_tensor(above[:], score[:], least, ALU.is_gt))
            link(dve.tensor_tensor(equal[:], score[:], least, ALU.is_equal))
            link(dve.tensor_reduce(n_above[:], above[:], AX_X, ALU.add))
            src, n, b = equal, 1, 0
            while n < E:
                dst = count[b]
                link(dve.tensor_copy(dst[:, :, 0:n], src[:, :, 0:n]))
                link(dve.tensor_tensor(dst[:, :, n:E], src[:, :, n:E], src[:, :, 0:E - n], ALU.add))
                src, n, b = dst, 2 * n, 1 - b
            link(dve.tensor_tensor(src[:], src[:], across(n_above[:]), ALU.add))
            link(dve.scalar_tensor_tensor(out=chosen[:], in0=src[:], scalar=float(top), in1=equal[:],
                                          op0=ALU.is_le, op1=ALU.mult))
            dve.tensor_tensor(chosen[:], chosen[:], above[:], ALU.add).then_inc(chosen_ready, 1)
            dve.wait_ge(chosen_ready, 1)
            link(dve.scalar_tensor_tensor(out=score[:], in0=score[:], scalar=0.5, in1=chosen[:],
                                          op0=ALU.mult, op1=ALU.mult))
            if slot_of is not None:
                rest = above
                for k in range(3):
                    link(dve.tensor_copy(parts[:, :, :, k], score[:] if k == 0 else rest[:]))
                    if k < 2:
                        link(dve.tensor_tensor(rest[:], score[:] if k == 0 else rest[:], parts[:, :, :, k],
                                               ALU.subtract))
                dve.wait_ge(rank_ready, 1)
                link(dve.scalar_tensor_tensor(out=equal[:], in0=ps_rank[:], scalar=1.0, in1=chosen[:],
                                              op0=ALU.add, op1=ALU.mult))
                dve.tensor_scalar(slot_of[:], equal[:], 1.0, None, ALU.subtract)
            else:
                dve.memset(weights[:, :, E * repeat:], 0.5)
                for r in range(repeat):
                    dve.tensor_copy(
                        weights[:, :, 0:E * repeat].rearrange("p t (e r) -> p t e r", r=repeat)[:, :, :, r],
                        score[:])


HEADS1 = 16
DH1 = 128
LATENT = 64
ROPE1 = 64
RMS_EPS = 1e-6
MASKED = -1e30


def l1_latent_stage(nc, core, weights, norm_w, latT):
    with Stage(nc, "latent") as st:
        w = st.sb("w", [P, KC, LATENT])
        gain = st.sb("gain", [P, LATENT])
        eps = st.sb("eps", [P, 1])
        squares = st.sb("squares", [P, TILES, LATENT])
        lat = st.sb("lat", [P, TILES, LATENT])
        total = st.sb("total", [P, TILES])
        rms = st.sb("rms", [P, TILES])
        inverse = st.sb("inverse", [P, TILES])
        ps = st.ps("ps", [P, TILES, LATENT])
        turn = st.ps("turn", [P, HALVES, HALF])
        loaded = st.sem("loaded")
        eps_ready = st.sem("eps_ready")
        projected = st.sem("projected")
        squared = st.sem("squared")
        total_ready = st.sem("total_ready")
        rms_ready = st.sem("rms_ready")
        step_done = st.sem("step_done")
        lat_ready = st.sem("lat_ready")
        turned = st.sem("turned")
        block = st.block()

        @block.sync
        def _(sp):
            sp.dma_start(w[:], weights.rearrange("(c p) n -> p c n", p=P)).then_inc(loaded, 16)
            sp.dma_start(gain[:], norm_w.partition_broadcast(P)).then_inc(loaded, 16)

        @block.gpsimd
        def _(pool):
            pool.memset(eps[:], RMS_EPS).then_inc(eps_ready, 1)

        @block.tensor
        def _(pe):
            pe.wait_ge(loaded, 32)
            for t in range(TILES):
                for c in range(KC):
                    mm = pe.matmul(ps[:, t, :], core.xnT[:, c, t * P:(t + 1) * P], w[:, c, :],
                                   start=(c == 0), stop=(c == KC - 1))
            mm.then_inc(projected, 1)
            pe.wait_ge(lat_ready, 1)
            for t in range(TILES):
                tr = pe.transpose(turn[0:LATENT, t // 4, (t % 4) * P:(t % 4 + 1) * P], lat[:, t, :], core.ident[:])
            tr.then_inc(turned, 1)

        @block.scalar
        def _(act):
            act.wait_ge(projected, 1)
            act.activation(squares[:], ps[:], ACT.Square).then_inc(squared, 1)
            act.wait_ge(total_ready, 1)
            act.wait_ge(eps_ready, 1)
            act.activation(rms[:], total[:], ACT.Sqrt, bias=eps[:], scale=1.0 / LATENT).then_inc(rms_ready, 1)

        @block.vector
        def _(dve):
            dve.wait_ge(squared, 1)
            dve.tensor_reduce(total[:], squares[:], AX_X, ALU.add).then_inc(total_ready, 1)
            dve.wait_ge(rms_ready, 1)
            dve.reciprocal(inverse[:], rms[:]).then_inc(step_done, 1)
            dve.wait_ge(step_done, 1)
            dve.tensor_tensor(lat[:], ps[:], inverse[:].unsqueeze(2).broadcast_to([P, TILES, LATENT]),
                              ALU.mult).then_inc(step_done, 1)
            dve.wait_ge(step_done, 2)
            dve.wait_ge(loaded, 32)
            dve.tensor_tensor(lat[:], lat[:], gain[:].unsqueeze(1).broadcast_to([P, TILES, LATENT]),
                              ALU.mult).then_inc(lat_ready, 1)
            dve.wait_ge(turned, 1)
            dve.tensor_copy(latT[:], turn[0:LATENT, :, :].rearrange("p h n -> p (h n)"))


def wide_project_stage(nc, core, name, oT, weights, bias, heads):
    with Stage(nc, name) as st:
        w = st.sb("w", [P, heads, D])
        row = st.sb("row", [P, D])
        banks = [st.ps(f"bank{q}", [P, 2, D]) for q in range(4)]
        PARTS = 4
        loaded = [st.sem(f"loaded{i}") for i in range(PARTS)]
        bias_loaded = st.sem("bias_loaded")
        projected = st.sem("projected")
        bias_added = st.sem("bias_added")
        block = st.block()
        per = heads // PARTS

        @block.sync
        def _(sp):
            for i in range(PARTS):
                sp.dma_start(w[:, i * per:(i + 1) * per, :],
                             weights[i * per:(i + 1) * per].rearrange("h p d -> p h d")).then_inc(loaded[i], 16)
            if bias is not None:
                sp.dma_start(row[:], bias.partition_broadcast(P)).then_inc(bias_loaded, 16)

        @block.tensor
        def _(pe):
            for t in range(TILES):
                for h in range(heads):
                    if t == 0 and h % per == 0:
                        pe.wait_ge(loaded[h // per], 16)
                    mm = pe.matmul(banks[t // 2][:, t % 2, :], oT[:, h, t * P:(t + 1) * P], w[:, h, :],
                                   start=(h == 0), stop=(h == heads - 1))
                mm.then_inc(projected, 1)

        @block.vector
        def _(dve):
            if bias is not None:
                dve.wait_ge(bias_loaded, 16)
                dve.tensor_tensor(core.x[:], core.x[:], row[:].unsqueeze(1).broadcast_to([P, TILES, D]),
                                  ALU.add).then_inc(bias_added, 1)
                dve.wait_ge(bias_added, 1)
            for q in range(4):
                dve.wait_ge(projected, 2 * q + 2)
                dve.tensor_tensor(core.x[:, 2 * q:2 * q + 2, :], core.x[:, 2 * q:2 * q + 2, :],
                                  banks[q][:], ALU.add)


def l1_attention(nc, core, wkv_a, norm_w, wq, wkv, columns, signs, w_out, b_out):
    SCALE = 1.0 / float(DH1) ** 0.5
    X0, X1 = P - ROPE1, P - ROPE1 // 2
    with ExitStack() as ctx:
        latT = ctx.enter_context(nc.sbuf_tensor("l1a_latT", [LATENT, TOKENS], F32))
        oT = ctx.enter_context(nc.sbuf_tensor("l1a_oT", [P, HEADS1, TOKENS], F32))
        l1_latent_stage(nc, core, wkv_a, norm_w, latT)
        with Stage(nc, "l1_heads") as st:
            w_q = [st.sb(f"w_q{b}", [P, KC, DH1]) for b in range(2)]
            w_kv = [st.sb(f"w_kv{b}", [LATENT, 2 * DH1]) for b in range(2)]
            sign = st.sb("sign", [P, 1])
            column = [st.sb(f"column{b}", [P, 3]) for b in range(2)]
            derived = [st.sb(f"derived{b}", [P, 3]) for b in range(2)]
            mask = st.sb("mask", [P, 3 * P])
            o_head = [st.sb(f"o_head{b}", [P, TOKENS]) for b in range(2)]
            qT = [st.sb(f"qT{b}", [P, TOKENS]) for b in range(2)]
            kT = [st.sb(f"kT{b}", [P, TOKENS]) for b in range(2)]
            cross = [st.sb(f"cross{i}", [P, TOKENS]) for i in range(2)]
            v = [st.sb(f"v{b}", [P, TILES, DH1]) for b in range(2)]
            logit = [st.sb(f"logit{b}", [P, 3 * P]) for b in range(2)]
            peak = st.sb("peak", [P, BATCH, 2])
            shift = st.sb("shift", [P, BATCH, 2])
            total = st.sb("total", [P, BATCH, 2])
            inverse = st.sb("inverse", [P, BATCH, 2])
            e = [st.sb(f"e{b}", [P, 3 * P]) for b in range(2)]
            prob = [st.sb(f"prob{b}", [P, 3 * P]) for b in range(2)]
            probT = [st.sb(f"probT{b}", [P, 3 * P]) for b in range(2)]
            ps_p = [st.ps(f"ps_p{b}", [P, HALF]) for b in range(2)]
            ps_s = [st.ps(f"ps_s{b}", [P, HALF]) for b in range(2)]
            ps_t = [st.ps(f"ps_t{b}", [P, HALF]) for b in range(2)]
            ps_o = [st.ps(f"ps_o{b}", [P, HALF]) for b in range(2)]

            small_loaded = st.sem("small_loaded")
            sine_ready = st.sem("sine_ready")
            derived_ready = st.sem("derived_ready")
            o_stored = [st.sem(f"o_stored{b}") for b in range(2)]
            mask_step = st.sem("mask_step")
            w_loaded = [st.sem(f"w_loaded{b}") for b in range(2)]
            projected = st.sem("projected")
            plain_done = st.sem("plain_done")
            cross_done = st.sem("cross_done")
            qk_ready = st.sem("qk_ready")
            scored = st.sem("scored")
            masked = st.sem("masked")
            peak_ready = st.sem("peak_ready")
            shift_ready = st.sem("shift_ready")
            exp_done = st.sem("exp_done")
            inverse_ready = st.sem("inverse_ready")
            prob_ready = st.sem("prob_ready")
            turned = st.sem("turned")
            probT_ready = st.sem("probT_ready")
            summed = st.sem("summed")
            o_copied = st.sem("o_copied")
            block = st.block()

            def over_heads(eng, prologue, step):
                prologue()
                step(0, 0, True, True)
                with eng.Fori(1, HEADS1 // 2) as i:
                    step(2 * i - 1, 1, False, True)
                    step(2 * i, 0, False, True)
                step(HEADS1 - 1, 1, False, False)

            @block.sync
            def _(sp):
                sp.dma_start(sign[:], signs).then_inc(small_loaded, 16)

                def load(h, b, first):
                    if not first:
                        sp.wait_ge(projected, 6 * (h - 1))
                    sp.dma_start(column[b][:], columns[bass.ds(h, 1)].rearrange("a p n -> (a p) n"))\
                        .then_inc(w_loaded[b], 16)
                    sp.dma_start(w_q[b][:], wq[bass.ds(h, 1)].rearrange("a p c n -> (a p) c n"))\
                        .then_inc(w_loaded[b], 16)
                    sp.dma_start(w_kv[b][:], wkv[bass.ds(h, 1)].rearrange("a p n -> (a p) n"))\
                        .then_inc(w_loaded[b], 16)

                load(0, 0, True)
                load(1, 1, True)
                with sp.Fori(1, HEADS1 // 2) as i:
                    load(2 * i, 0, False)
                    load(2 * i + 1, 1, False)

            @block.tensor
            def _(pe):
                def project_q(p, i, b, first):
                    pe.wait_ge(w_loaded[b], 48 * (i + 1))
                    for h in range(HALVES):
                        if not first:
                            pe.wait_ge(plain_done, 6 * (p - 1) + 5 + h)
                        for c in range(KC):
                            mm = pe.matmul(ps_p[h][:], w_q[b][:, c, :], core.xnT[:, c, h * HALF:(h + 1) * HALF],
                                           start=(c == 0), stop=(c == KC - 1))
                        mm.then_inc(projected, 1)

                def project_k(p, b):
                    for h in range(HALVES):
                        pe.wait_ge(plain_done, 6 * p + h + 1)
                        pe.wait_ge(cross_done, 4 * p + h + 1)
                        pe.matmul(ps_p[h][:], w_kv[b][:, 0:DH1], latT[:, h * HALF:(h + 1) * HALF],
                                  start=True, stop=True).then_inc(projected, 1)

                def project_v(p, b):
                    for h in range(HALVES):
                        pe.wait_ge(plain_done, 6 * p + h + 3)
                        pe.wait_ge(cross_done, 4 * p + h + 3)
                        for j in range(4):
                            t = 4 * h + j
                            mm = pe.matmul(ps_p[h][:, j * DH1:(j + 1) * DH1], latT[:, t * P:(t + 1) * P],
                                           w_kv[b][:, DH1:2 * DH1], start=True, stop=True)
                        mm.then_inc(projected, 1)

                def scores(h, b, n, first):
                    if n == 0:
                        pe.wait_ge(qk_ready, 2 * h + 2)
                    if not (first and n < 2):
                        pe.wait_ge(masked, BATCH * h + n - 1)
                    q, k = qT[b][:, n * SEQ:(n + 1) * SEQ], kT[b][:, n * SEQ:(n + 1) * SEQ]
                    pe.matmul(ps_s[n % 2][:, 0:P], q[:, 0:P], k[:, 0:P], start=True, stop=True)
                    pe.matmul(ps_s[n % 2][:, P:3 * P], q[:, P:2 * P], k, start=True, stop=True)\
                        .then_inc(scored, 1)

                def turn(h, n, first):
                    pe.wait_ge(prob_ready, BATCH * h + n + 1)
                    if not (first and n < 2):
                        pe.wait_ge(probT_ready, BATCH * h + n - 1)
                    for j in range(3):
                        tr = pe.transpose(ps_t[n % 2][:, j * P:(j + 1) * P], prob[n % 2][:, j * P:(j + 1) * P],
                                          core.ident[:])
                    tr.then_inc(turned, 1)

                def values(h, b, n, first):
                    pe.wait_ge(probT_ready, BATCH * h + n + 1)
                    if not first and n % 2 == 0:
                        pe.wait_ge(o_copied, 2 * (h - 1) + n // 2 + 1)
                    out = ps_o[n // 2][:, (n % 2) * SEQ:(n % 2 + 1) * SEQ]
                    pe.matmul(out, v[b][:, 2 * n, :], probT[n % 2][:, 0:2 * P], start=True, stop=False)
                    pe.matmul(out[:, P:2 * P], v[b][:, 2 * n + 1, :], probT[n % 2][:, 2 * P:3 * P],
                              start=False, stop=True).then_inc(summed, 1)

                def prologue():
                    project_q(0, 0, 0, True)
                    project_k(0, 0)
                    project_v(0, 0)

                def step(h, b, first, more):
                    nb = 1 - b
                    i = (h + 1) // 2 if isinstance(h, int) else h_half[0]
                    scores(h, b, 0, first)
                    scores(h, b, 1, first)
                    if more:
                        project_q(h + 1, i, nb, False)
                    turn(h, 0, first)
                    scores(h, b, 2, first)
                    if more:
                        project_k(h + 1, nb)
                    turn(h, 1, first)
                    values(h, b, 0, first)
                    scores(h, b, 3, first)
                    if more:
                        project_v(h + 1, nb)
                    turn(h, 2, first)
                    values(h, b, 1, first)
                    turn(h, 3, first)
                    values(h, b, 2, first)
                    values(h, b, 3, first)

                h_half = [0]
                prologue()
                step(0, 0, True, True)
                with pe.Fori(1, HEADS1 // 2) as i:
                    h_half[0] = i
                    step(2 * i - 1, 1, False, True)
                    step(2 * i, 0, False, True)
                step(HEADS1 - 1, 1, False, False)

            @block.scalar
            def _(act):
                def plain(p, b, which, first):
                    dst = (qT, kT)[which][b]
                    if not first:
                        act.wait_ge(summed, BATCH * (p - 1))
                    if which == 0:
                        act.wait_ge(derived_ready, 2 * p + 2)
                    for h in range(HALVES):
                        act.wait_ge(projected, 6 * p + 2 * which + h + 1)
                        out = dst[:, h * HALF:(h + 1) * HALF]
                        if which == 0:
                            act.activation(out, ps_p[h][:], ACT.Identity, bias=derived[b][:, 2:3],
                                           scale=column[b][:, 1:2]).then_inc(plain_done, 1)
                        else:
                            act.activation(out, ps_p[h][:], ACT.Copy, scale=column[b][:, 1:2])\
                                .then_inc(plain_done, 1)

                def copy_v(p, b, first):
                    if not first:
                        act.wait_ge(summed, BATCH * (p - 1))
                    for h in range(HALVES):
                        act.wait_ge(projected, 6 * p + 4 + h + 1)
                        act.copy(v[b][:, 4 * h:4 * h + 4, :].rearrange("p t n -> p (t n)"), ps_p[h][:])\
                            .then_inc(plain_done, 1)

                def exps(h, n, first):
                    act.wait_ge(shift_ready, BATCH * h + n + 1)
                    if not (first and n < 2):
                        act.wait_ge(prob_ready, BATCH * h + n - 1)
                    for j, (lo, hi) in enumerate(((0, P), (P, 3 * P))):
                        last = act.activation(e[n % 2][:, lo:hi], logit[n % 2][:, lo:hi], ACT.Exp,
                                              bias=shift[:, n, j:j + 1], scale=SCALE,
                                              accum_out=total[:, n, j:j + 1])
                        last.then_inc(exp_done, 1)

                def copy_o(h, b, i, j):
                    if i is not None:
                        act.wait_ge(o_stored[b], 16 * i)
                    act.wait_ge(summed, BATCH * h + 2 * j + 2)
                    act.copy(o_head[b][:, 2 * j * SEQ:2 * (j + 1) * SEQ], ps_o[j][:]).then_inc(o_copied, 1)

                def prologue():
                    plain(0, 0, 0, True)
                    plain(0, 0, 1, True)
                    copy_v(0, 0, True)

                def step(h, b, first, more):
                    exps(h, 0, first)
                    exps(h, 1, first)
                    if more:
                        plain(h + 1, 1 - b, 0, first)
                    exps(h, 2, first)
                    if more:
                        plain(h + 1, 1 - b, 1, first)
                    exps(h, 3, first)
                    if more:
                        copy_v(h + 1, 1 - b, first)
                    for j in range(2):
                        copy_o(h, b, stored_before[0], j)
                    act.wait_ge(o_copied, 2 * h + 2)
                    act.dma_start(oT[:, bass.ds(h, 1), :].rearrange("p a n -> p (a n)"), o_head[b][:])\
                        .then_inc(o_stored[b], 16)

                stored_before = [None]
                prologue()
                step(0, 0, True, True)
                with act.Fori(1, HEADS1 // 2) as i:
                    stored_before[0] = i - 1
                    step(2 * i - 1, 1, False, True)
                    stored_before[0] = i
                    step(2 * i, 0, False, True)
                stored_before[0] = HEADS1 // 2 - 1
                step(HEADS1 - 1, 1, False, False)
                for b in range(2):
                    act.wait_ge(o_stored[b], 16 * (HEADS1 // 2))

            @block.vector
            def _(dve):
                def sines_of(p, b, which, first):
                    if not first:
                        dve.wait_ge(qk_ready, 2 * (p - 1) + which + 1)
                    for h in range(HALVES):
                        dve.wait_ge(plain_done, 6 * p + 2 * which + h + 1)
                        for src, dst in ((X1, X0), (X0, X1)):
                            rows, to = slice(src, src + ROPE1 // 2), slice(dst, dst + ROPE1 // 2)
                            out = cross[which][to, h * HALF:(h + 1) * HALF]
                            if which == 0:
                                last = dve.tensor_scalar(out, ps_p[h][rows, :], derived[b][rows, 0:1],
                                                         derived[b][rows, 1:2], ALU.mult, ALU.add)
                            else:
                                last = dve.tensor_scalar(out, ps_p[h][rows, :], derived[b][rows, 0:1],
                                                         None, ALU.mult)
                        last.then_inc(cross_done, 1)

                def mask_max(h, n, first):
                    dve.wait_ge(scored, BATCH * h + n + 1)
                    if not (first and n < 2):
                        dve.wait_ge(exp_done, 2 * (BATCH * h + n - 1))
                    dve.tensor_tensor(logit[n % 2][:], ps_s[n % 2][:, 0:3 * P], mask[:], ALU.add)\
                        .then_inc(masked, 1)
                    dve.wait_ge(masked, BATCH * h + n + 1)
                    for j, (lo, hi) in enumerate(((0, P), (P, 3 * P))):
                        last = dve.tensor_reduce(peak[:, n, j:j + 1], logit[n % 2][:, lo:hi], AX_X, ALU.max)
                        last.then_inc(peak_ready, 1)
                    dve.wait_ge(peak_ready, 2 * (BATCH * h + n + 1))
                    dve.tensor_scalar(shift[:, n, :], peak[:, n, :], -SCALE, None, ALU.mult)\
                        .then_inc(shift_ready, 1)

                def invert(h, n):
                    dve.wait_ge(exp_done, 2 * (BATCH * h + n + 1))
                    dve.reciprocal(inverse[:, n, :], total[:, n, :]).then_inc(inverse_ready, 1)

                def copy_probT(h, n, first):
                    dve.wait_ge(turned, BATCH * h + n + 1)
                    if not (first and n < 2):
                        dve.wait_ge(summed, BATCH * h + n - 1)
                    dve.tensor_copy(probT[n % 2][:], ps_t[n % 2][:, 0:3 * P]).then_inc(probT_ready, 1)

                def prologue():
                    dve.wait_ge(mask_step, 3)
                    sines_of(0, 0, 0, True)
                    sines_of(0, 0, 1, True)

                def step(h, b, first, more):
                    mask_max(h, 0, first)
                    mask_max(h, 1, first)
                    invert(h, 0)
                    invert(h, 1)
                    if more:
                        sines_of(h + 1, 1 - b, 0, False)
                    copy_probT(h, 0, first)
                    mask_max(h, 2, first)
                    if more:
                        sines_of(h + 1, 1 - b, 1, False)
                    invert(h, 2)
                    copy_probT(h, 1, first)
                    mask_max(h, 3, first)
                    invert(h, 3)
                    copy_probT(h, 2, first)
                    copy_probT(h, 3, first)

                over_heads(dve, prologue, step)

            @block.gpsimd
            def _(pool):
                def derive(p, b, i, first):
                    pool.wait_ge(w_loaded[b], 48 * (i + 1))
                    if not first:
                        pool.wait_ge(cross_done, 4 * (p - 1))
                        pool.wait_ge(plain_done, 6 * (p - 1))
                    pool.tensor_tensor(derived[b][:, 0:1], column[b][:, 2:3], sign[:], ALU.mult)\
                        .then_inc(sine_ready, 1)
                    pool.wait_ge(sine_ready, p + 1)
                    pool.tensor_tensor(derived[b][:, 1:2], column[b][:, 0:1], derived[b][:, 0:1], ALU.mult)\
                        .then_inc(derived_ready, 1)
                    pool.tensor_tensor(derived[b][:, 2:3], column[b][:, 0:1], column[b][:, 1:2], ALU.mult)\
                        .then_inc(derived_ready, 1)

                def add_sines(p, b, which):
                    pool.wait_ge(plain_done, 6 * p + 2 * which + 2)
                    pool.wait_ge(cross_done, 4 * p + 2 * which + 2)
                    dst = (qT, kT)[which][b]
                    pool.tensor_tensor(dst[:], dst[:], cross[which][:], ALU.add)\
                        .then_inc(qk_ready, 1)

                def normalise(h, n, first):
                    pool.wait_ge(inverse_ready, BATCH * h + n + 1)
                    if not (first and n < 2):
                        pool.wait_ge(turned, BATCH * h + n - 1)
                    for j, (lo, hi) in enumerate(((0, P), (P, 3 * P))):
                        last = pool.tensor_tensor(prob[n % 2][:, lo:hi], e[n % 2][:, lo:hi],
                                                  inverse[:, n, j:j + 1].broadcast_to([P, hi - lo]), ALU.mult)
                    last.then_inc(prob_ready, 1)

                def prologue():
                    pool.memset(mask[:], 0.0).then_inc(mask_step, 1)
                    pool.wait_ge(mask_step, 1)
                    for lo in (0, 2 * P):
                        pool.affine_select(out=mask[:, lo:lo + P], in_=mask[:, lo:lo + P], compare_op=ALU.is_ge,
                                           fill=MASKED, base=0, pattern=[[-1, P]], channel_multiplier=1)\
                            .then_inc(mask_step, 1)
                    for c in cross:
                        pool.memset(c[0:X0, :], 0.0).then_inc(mask_step, 1)
                        pool.wait_ge(mask_step, 4 + cross.index(c))
                    pool.wait_ge(small_loaded, 16)
                    derive(0, 0, 0, True)
                    derive(1, 1, 0, True)
                    add_sines(0, 0, 0)
                    add_sines(0, 0, 1)

                def step(h, b, first, more):
                    normalise(h, 0, first)
                    normalise(h, 1, first)
                    if more:
                        add_sines(h + 1, 1 - b, 0)
                    normalise(h, 2, first)
                    if more:
                        add_sines(h + 1, 1 - b, 1)
                    normalise(h, 3, first)

                prologue()
                step(0, 0, True, True)
                with pool.Fori(1, HEADS1 // 2) as i:
                    derive(2 * i, 0, i, False)
                    step(2 * i - 1, 1, False, True)
                    derive(2 * i + 1, 1, i, False)
                    step(2 * i, 0, False, True)
                step(HEADS1 - 1, 1, False, False)
        wide_project_stage(nc, core, "l1_project", oT, w_out, b_out, HEADS1)


F2, SHARED2 = 96, 2
EXPERTS2, TOP2, CAPACITY2 = 64, 6, 64
HEADS2 = 16
DH2 = 128
TAPS = 4
CHUNKS2 = SEQ // P
LOG_A, NEG_B, B, NEG_BG, TO_END, FROM_START = range(6)
COLUMNS = 6


def l2_decay_stage(nc, core, weights, bias, table_out):
    with Stage(nc, "decay") as st:
        w = st.sb("w", [P, KC, 2 * HEADS2])
        row = st.sb("row", [P, 2 * HEADS2])
        z = st.sb("z", [P, TILES, 2 * HEADS2])
        size = st.sb("size", [P, TILES, HEADS2])
        log_a = st.sb("log_a", [P, TILES, HEADS2])
        b = st.sb("b", [P, TILES, HEADS2])
        sums = st.sb("sums", [P, 3, TILES, HEADS2])
        ps = st.ps("ps", [P, TILES, 2 * HEADS2])
        ps_sums = st.ps("ps_sums", [P, 3, TILES, HEADS2])
        table = st.sb("table", [P, HEADS2, COLUMNS, TILES])
        table_ready = st.sem("table_ready")
        stored = st.sem("stored")
        loaded = st.sem("loaded")
        projected = st.sem("projected")
        z_ready = st.sem("z_ready")
        b_ready = st.sem("b_ready")
        act_step = st.sem("act_step")
        log_ready = st.sem("log_ready")
        summed = st.sem("summed")
        exp_ready = st.sem("exp_ready")
        step_done = st.sem("step_done")
        block = st.block()

        @block.sync
        def _(sp):
            sp.dma_start(w[:], weights.rearrange("(c p) n -> p c n", p=P)).then_inc(loaded, 16)
            sp.dma_start(row[:], bias.partition_broadcast(P)).then_inc(loaded, 16)
            sp.wait_ge(table_ready, COLUMNS)
            sp.dma_start(table_out, table[:]).then_inc(stored, 16)
            sp.wait_ge(stored, 16)

        @block.tensor
        def _(pe):
            pe.wait_ge(loaded, 32)
            for t in range(TILES):
                for c in range(KC):
                    mm = pe.matmul(ps[:, t, :], core.xnT[:, c, t * P:(t + 1) * P], w[:, c, :],
                                   start=(c == 0), stop=(c == KC - 1))
            mm.then_inc(projected, 1)
            pe.wait_ge(log_ready, 1)
            for i, m in enumerate((core.before, core.after, core.upto)):
                mm = pe.matmul(ps_sums[:, i].rearrange("p t h -> p (t h)"), m[:],
                               log_a[:].rearrange("p t h -> p (t h)"), start=True, stop=True)
            mm.then_inc(summed, 1)

        @block.scalar
        def _(act):
            act.wait_ge(z_ready, 1)
            act.activation(b[:], z[:, :, HEADS2:], ACT.Sigmoid).then_inc(b_ready, 1)
            act.activation(size[:], z[:, :, 0:HEADS2], ACT.Abs).then_inc(act_step, 1)
            act.wait_ge(act_step, 1)
            act.activation(size[:], size[:], ACT.Exp, scale=-1.0).then_inc(act_step, 1)
            act.wait_ge(act_step, 2)
            act.activation(size[:], size[:], ACT.Ln, bias=core.ones[:, 0:1]).then_inc(act_step, 1)
            act.wait_ge(summed, 1)
            act.activation(sums[:], ps_sums[:], ACT.Exp).then_inc(exp_ready, 1)

        @block.vector
        def _(dve):
            steps = [0]

            def link(ins):
                steps[0] += 1
                ins.then_inc(step_done, 1)
                dve.wait_ge(step_done, steps[0])

            def column(k):
                return table[:, :, k, :].rearrange("p h t -> p t h")

            dve.wait_ge(loaded, 32)
            dve.wait_ge(projected, 1)
            dve.tensor_tensor(z[:], ps[:], row[:].unsqueeze(1).broadcast_to([P, TILES, 2 * HEADS2]), ALU.add)\
                .then_inc(z_ready, 1)
            dve.wait_ge(z_ready, 1)
            link(dve.tensor_scalar(log_a[:], z[:, :, 0:HEADS2], 0.0, None, ALU.min))
            dve.wait_ge(act_step, 3)
            dve.tensor_tensor(log_a[:], log_a[:], size[:], ALU.subtract).then_inc(log_ready, 1)
            dve.wait_ge(log_ready, 1)
            dve.tensor_copy(column(LOG_A), log_a[:]).then_inc(table_ready, 1)
            dve.wait_ge(b_ready, 1)
            dve.tensor_copy(column(B), b[:]).then_inc(table_ready, 1)
            dve.tensor_scalar(column(NEG_B), b[:], -1.0 / DH2, None, ALU.mult).then_inc(table_ready, 1)
            dve.wait_ge(exp_ready, 1)
            dve.scalar_tensor_tensor(out=column(NEG_BG), in0=sums[:, 0], scalar=-1.0 / DH2, in1=b[:],
                                     op0=ALU.mult, op1=ALU.mult).then_inc(table_ready, 1)
            dve.tensor_copy(column(TO_END), sums[:, 1]).then_inc(table_ready, 1)
            dve.tensor_scalar(column(FROM_START), sums[:, 2], float(DH2) ** -0.5, None, ALU.mult)\
                .then_inc(table_ready, 1)


def l2_heads_stage(nc, core, w_heads, conv_heads, table, ln_w, ln_b, oT):
    LEVELS = 7
    SY = BATCH
    PAD = TAPS - 1
    Q, K, V, G = range(4)
    FILLS = [[9, 9, 9], [10, 8, 9]]
    with Stage(nc, "l2_heads") as st:
        w = [st.sb(f"w{b}", [P, 4, KC, DH2]) for b in range(2)]
        conv = [st.sb(f"conv{b}", [P, 3, TAPS + 1]) for b in range(2)]
        col = [st.sb(f"col{b}", [P, COLUMNS, TILES]) for b in range(2)]
        gain = st.sb("gain", [P, DH2])
        offset = st.sb("offset", [P, DH2])
        upto_scaled = st.sb("upto_scaled", [P, P])
        padded = [st.sb(f"padded{i}", [P, BATCH, PAD + SEQ]) for i in range(3)]
        taps = [st.sb(f"taps{i}", [P, BATCH, SEQ]) for i in range(3)]
        feat = [[st.sb(f"feat{i}{b}", [P, TOKENS]) for b in range(2)] for i in range(2)]
        feat.append([st.sb("feat2", [P, TOKENS])] * 2)
        gate = [st.sb(f"gate{b}", [P, TILES, DH2]) for b in range(2)]
        e1 = [st.sb(f"e1{c}", [P, SY, P]) for c in range(2)]
        e2 = [st.sb(f"e2{c}", [P, SY, P]) for c in range(2)]
        la_before, la_upto = e1, e2
        M = [[st.sb(f"m{c}{k}", [P, SY, P]) for k in range(2)] for c in range(2)]
        MT = [[st.sb(f"mt{c}{k}", [P, SY, P]) for k in range(2)] for c in range(2)]
        Y = [[st.sb(f"y{c}{k}", [P, SY, P]) for k in range(2)] for c in range(2)]
        qk = [st.sb(f"qk{c}", [P, SY, P]) for c in range(2)]
        bv = [st.sb(f"bv{c}", [P, SY, DH2]) for c in range(2)]
        k_end = st.sb("k_end", [P, SY, DH2])
        o_state = k_end
        r = bv[1]
        u = [st.sb(f"u{c}", [P, SY, DH2]) for c in range(2)]
        state = st.sb("state", [P, SY, DH2])
        o = st.sb("o", [P, TILES, DH2])
        on = st.sb("on", [P, TILES, DH2])
        stats = st.sb("stats", [P, TILES, 6])
        mean_var = st.sb("mean_var", [P, TILES, 2])
        sd = st.sb("sd", [P, TILES])
        rstd = st.sb("rstd", [P, TILES])
        spare = st.sb("spare", [P, 1])
        o_head = st.sb("o_head", [P, TOKENS])
        ps_p = [st.ps(f"ps_p{i}", [P, HALF]) for i in range(2)]
        bank = [[st.ps(f"bank{c}{i}", [P, SY, P]) for i in range(3)] for c in range(2)]

        rows_loaded = st.sem("rows_loaded")
        pool_step = st.sem("pool_step")
        w_loaded = [st.sem(f"w_loaded{b}") for b in range(2)]
        col_loaded = [st.sem(f"col_loaded{b}") for b in range(2)]
        p_filled = [st.sem(f"p_filled{i}") for i in range(2)]
        p_read = [st.sem(f"p_read{i}") for i in range(2)]
        filled = [[st.sem(f"filled{c}{i}") for i in range(3)] for c in range(2)]
        read = [[st.sem(f"read{c}{i}") for i in range(3)] for c in range(2)]
        padded_ready = st.sem("padded_ready")
        conv_step = st.sem("conv_step")
        feat_ready = st.sem("feat_ready")
        la_ready = st.sem("la_ready")
        exp1_ready = [st.sem(f"exp1_ready{c}") for c in range(2)]
        exp2_ready = [st.sem(f"exp2_ready{c}") for c in range(2)]
        e1_ready = [st.sem(f"e1_ready{c}") for c in range(2)]
        e2_ready = [st.sem(f"e2_ready{c}") for c in range(2)]
        y0_ready = [st.sem(f"y0_ready{c}") for c in range(2)]
        stats_ready = st.sem("stats_ready")
        mean_ready = st.sem("mean_ready")
        sd_ready = st.sem("sd_ready")
        rstd_ready = st.sem("rstd_ready")
        on_ready = st.sem("on_ready")
        gained = st.sem("gained")
        o_stored = st.sem("o_stored")
        block = st.block()

        def nth(c, i, h, k):
            return FILLS[c][i] * h + k + 1

        def p_use(h, k, more):
            if isinstance(h, int) and h == -1:
                return {0: 1, 1: 2, 2: 3, 4: 4}[k]
            if isinstance(h, int) and h == 0:
                return 4 + {0: 1, 1: 2, 2: 3, 4: 4}[k]
            return 5 * h + 3 + (k + 1 if more else k - 2)

        def tile_of(c, s):
            return CHUNKS2 * s + c

        def columns(b, k, c):
            return col[b][:, k, :].rearrange("p (s c) -> p c s", c=CHUNKS2)[:, c, :]

        def tiles(ap, c):
            return ap.rearrange("p (s c) d -> p c s d", c=CHUNKS2)[:, c]

        def along(m):
            return m[:].unsqueeze(1).broadcast_to([P, SY, P])

        def flat(ap):
            return ap.rearrange("p s n -> p (s n)")

        def over_heads(eng, prologue, step, epilogue):
            prologue()
            step(0, 0, 0, True, True)
            with eng.Fori(1, HEADS2 // 2) as i:
                step(2 * i - 1, i - 1, 1, False, True)
                step(2 * i, i, 0, False, True)
            step(HEADS2 - 1, HEADS2 // 2 - 1, 1, False, False)
            epilogue()

        @block.sync
        def _(sp):
            sp.dma_start(gain[:], ln_w.partition_broadcast(P)).then_inc(rows_loaded, 16)
            sp.dma_start(offset[:], ln_b.partition_broadcast(P)).then_inc(rows_loaded, 16)

            def load(p, b, waits):
                head = bass.ds(p, 1)
                if waits is not None:
                    sp.wait_ge(conv_step, 9 * (p - 1))
                sp.dma_start(w[b][:, 0:3], w_heads[head, :, 0:3].rearrange("a p w c n -> (a p) w c n"))\
                    .then_inc(w_loaded[b], 16)
                sp.dma_start(conv[b][:], conv_heads[head].rearrange("a p w t -> (a p) w t"))\
                    .then_inc(w_loaded[b], 16)
                if waits is not None:
                    sp.wait_ge(p_read[1], waits)
                sp.dma_start(w[b][:, 3:4], w_heads[head, :, 3:4].rearrange("a p w c n -> (a p) w c n"))\
                    .then_inc(w_loaded[b], 16)

            load(0, 0, None)
            load(1, 1, None)
            load(2, 0, p_use(-1, 4, True))
            load(3, 1, p_use(0, 4, True))
            with sp.Fori(2, HEADS2 // 2) as i:
                load(2 * i, 0, p_use(2 * i - 3, 4, True))
                load(2 * i + 1, 1, p_use(2 * i - 2, 4, True))

        @block.tensor
        def _(pe):
            def fill(c, i, h, k, products):
                if not (isinstance(h, int) and h == 0 and k == 0):
                    pe.wait_ge(read[c][i], nth(c, i, h, k) - 1)
                for out, lhsT, rhs in products:
                    last = (pe.transpose(out, lhsT, core.ident[:]) if rhs is None
                            else pe.matmul(out, lhsT, rhs, start=True, stop=True))
                last.then_inc(filled[c][i], 1)

            def project(p, i, b, h, which, more=True):
                use = p_use(h, which if which < G else 4, more)
                if which == Q:
                    pe.wait_ge(w_loaded[b], 48 * (i + 1))
                for half in range(2):
                    if not (isinstance(use, int) and use == 1):
                        pe.wait_ge(p_read[half], use - 1)
                    if which < G:
                        for c in range(KC):
                            mm = pe.matmul(ps_p[half][:], w[b][:, which, c, :],
                                           core.xnT[:, c, half * HALF:(half + 1) * HALF],
                                           start=(c == 0), stop=(c == KC - 1))
                    else:
                        for j in range(4):
                            t = 4 * half + j
                            for c in range(KC):
                                mm = pe.matmul(ps_p[half][:, j * P:(j + 1) * P],
                                               core.xnT[:, c, t * P:(t + 1) * P], w[b][:, G, c, :],
                                               start=(c == 0), stop=(c == KC - 1))
                    mm.then_inc(p_filled[half], 1)

            def turn_o(h_step, h, more):
                pe.wait_ge(gained, 3 * (h + 1))
                use = p_use(h_step, 3, more)
                for half in range(2):
                    pe.wait_ge(p_read[half], use - 1)
                    for j in range(4):
                        tr = pe.transpose(ps_p[half][:, j * P:(j + 1) * P], on[:, 4 * half + j, :], core.ident[:])
                    tr.then_inc(p_filled[half], 1)

            def cols(ap, c, s):
                t = tile_of(c, s)
                return ap[:, t * P:(t + 1) * P]

            def prologue():
                for which in range(4):
                    project(0, 0, 0, -1, which)

            def step(h, i, b, first, more):
                q, k, v = (feat[x][b] for x in range(3))
                nxt = (h + 1, (i + b), 1 - b, h)
                S = range(SY)
                pe.wait_ge(la_ready, 4 * h + 4)
                pe.wait_ge(feat_ready, 3 * h + 3)
                for c in range(2):
                    fill(c, 1, h, 0, [(bank[c][1][:, s, :], la_before[c][:, s, :], core.after[:]) for s in S])
                    fill(c, 2, h, 0, [(flat(bank[c][2][:]), core.after[:], flat(la_upto[c][:]))])
                    fill(c, 0, h, 0, [(bank[c][0][:, s, :], cols(k, c, s), cols(k, c, s)) for s in S])
                if more:
                    project(*nxt, Q)
                for c in range(2):
                    fill(c, 1, h, 1, [(bank[c][1][:, s, :], cols(k, c, s), cols(q, c, s)) for s in S])
                    fill(c, 2, h, 1, [(bank[c][2][:, s, :], cols(v, c, s), None) for s in S])
                fill(0, 1, h, 2, [(bank[0][1][:, s, :], cols(k, 0, s), None) for s in S])
                for c in range(2):
                    fill(c, 0, h, 1, [(bank[c][0][:, s, :], M[c][0][:, s, :], None) for s in S])
                if more:
                    project(*nxt, K)
                for n in range(1, LEVELS):
                    old, new = (n - 1) % 2, n % 2
                    for c in range(2):
                        if n == 1:
                            pe.wait_ge(read[c][0], nth(c, 0, h, 1))
                        else:
                            pe.wait_ge(read[c][1], nth(c, 1, h, (1 if c else 2) + n - 1))
                        fill(c, 0, h, 1 + n, [(bank[c][0][:, s, :], MT[c][old][:, s, :], M[c][old][:, s, :])
                                              for s in S])
                        if n < LEVELS - 1:
                            fill(c, 1, h, (1 if c else 2) + n,
                                 [(bank[c][1][:, s, :], M[c][old][:, s, :], MT[c][old][:, s, :]) for s in S])
                    for c in range(2):
                        pe.wait_ge(read[c][0], nth(c, 0, h, 1 + n))
                        if n == 1:
                            pe.wait_ge(y0_ready[c], h + 1)
                        fill(c, 2, h, 1 + n, [(bank[c][2][:, s, :], M[c][new][:, s, :], Y[c][old][:, s, :])
                                              for s in S])
                    if n == 1 and more:
                        project(*nxt, V)
                    if n == 2 and not first:
                        turn_o(h, h - 1, more)
                    if n == 3 and more:
                        project(*nxt, G)
                last = (LEVELS - 1) % 2
                pe.wait_ge(read[0][2], nth(0, 2, h, LEVELS))
                fill(0, 1, h, 8, [(bank[0][1][:, s, :], Y[0][last][:, s, :], bv[0][:, s, :]) for s in S])
                pe.wait_ge(read[0][1], nth(0, 1, h, 8))
                fill(0, 2, h, 8, [(bank[0][2][:, s, :], k_end[:, s, :], u[0][:, s, :]) for s in S])
                fill(0, 0, h, 8, [(bank[0][0][:, s, :], qk[0][:, s, :], u[0][:, s, :]) for s in S])
                pe.wait_ge(read[0][2], nth(0, 2, h, 8))
                fill(1, 0, h, 8, [(bank[1][0][:, s, :], cols(k, 1, s), state[:, s, :]) for s in S])
                fill(1, 2, h, 8, [(bank[1][2][:, s, :], cols(q, 1, s), state[:, s, :]) for s in S])
                pe.wait_ge(read[1][0], nth(1, 0, h, 8))
                fill(1, 1, h, 7, [(bank[1][1][:, s, :], Y[1][last][:, s, :], r[:, s, :]) for s in S])
                pe.wait_ge(read[1][1], nth(1, 1, h, 7))
                fill(1, 0, h, 9, [(bank[1][0][:, s, :], qk[1][:, s, :], u[1][:, s, :]) for s in S])

            def epilogue():
                pe.wait_ge(gained, 3 * HEADS2)
                use = p_use(HEADS2 - 1, 3, False) + 1
                for half in range(2):
                    pe.wait_ge(p_read[half], use - 1)
                    for j in range(4):
                        tr = pe.transpose(ps_p[half][:, j * P:(j + 1) * P], on[:, 4 * half + j, :], core.ident[:])
                    tr.then_inc(p_filled[half], 1)

            over_heads(pe, prologue, step, epilogue)

        @block.scalar
        def _(act):
            def load_columns(p, b):
                act.dma_start(col[b][:].rearrange("p k t -> p (k t)"),
                              table[:, bass.ds(p, 1)].rearrange("p a k t -> p (a k t)")).then_inc(col_loaded[b], 16)

            def take(p, b, h, which):
                use = p_use(h, which, True)
                if not (isinstance(h, int) and h == -1):
                    act.wait_ge(conv_step, 9 * (p - 1) + 3 * which + 3)
                for half in range(2):
                    act.wait_ge(p_filled[half], use)
                    src = ps_p[half][:].rearrange("p (s n) -> p s n", n=SEQ)
                    act.copy(padded[which][:, 2 * half:2 * half + 2, PAD:], src).then_inc(padded_ready, 1)
                    act.activation(taps[which][:, 2 * half:2 * half + 2, :], src, ACT.Identity,
                                   bias=conv[b][:, which, TAPS:TAPS + 1],
                                   scale=conv[b][:, which, TAPS - 1:TAPS]).then_inc(p_read[half], 1)

            def silu(p, b, which, first):
                act.wait_ge(conv_step, 9 * p + 3 * which + 3)
                if not first:
                    act.wait_ge(filled[1][0], FILLS[1][0] * (p - 1))
                act.activation(feat[which][b][:], taps[which][:].rearrange("p s n -> p (s n)"), ACT.Silu)\
                    .then_inc(feat_ready, 1)

            def take_gate(p, b, h, first):
                if not first:
                    act.wait_ge(gained, 3 * (p - 1))
                for half in range(2):
                    act.wait_ge(p_filled[half], p_use(h, 4, True))
                    act.activation(gate[b][:, 4 * half:4 * half + 4, :].rearrange("p t n -> p (t n)"),
                                   ps_p[half][:], ACT.Sigmoid).then_inc(p_read[half], 1)

            def take_o(use, stored):
                if stored is not None:
                    act.wait_ge(o_stored, 16 * stored)
                for half in range(2):
                    act.wait_ge(p_filled[half], use)
                    act.copy(o_head[:, half * HALF:(half + 1) * HALF], ps_p[half][:]).then_inc(p_read[half], 1)

            def store_o(use, h):
                for half in range(2):
                    act.wait_ge(p_read[half], use)
                act.dma_start(oT[:, bass.ds(h, 1), :].rearrange("p a n -> p (a n)"), o_head[:])\
                    .then_inc(o_stored, 16)

            def scaled_copies(c, i, h, k, dst, b, column):
                act.wait_ge(filled[c][i], nth(c, i, h, k))
                for s in range(SY):
                    last = act.activation(dst[:, s, :], bank[c][i][:, s, :], ACT.Copy,
                                          scale=columns(b, column, c)[:, s:s + 1])
                last.then_inc(read[c][i], 1)

            def take_copy(c, i, h, k, dst):
                act.wait_ge(filled[c][i], nth(c, i, h, k))
                act.copy(flat(dst[:]), flat(bank[c][i][:])).then_inc(read[c][i], 1)

            def prologue():
                load_columns(0, 0)
                act.wait_ge(w_loaded[0], 48)
                for which in range(3):
                    take(0, 0, -1, which)
                take_gate(0, 0, -1, True)
                for which in range(3):
                    silu(0, 0, which, True)

            def step(h, i, b, first, more):
                for c in range(2):
                    act.wait_ge(filled[c][1], nth(c, 1, h, 0))
                    act.activation(flat(e1[c][:]), flat(bank[c][1][:]), ACT.Exp).then_inc(read[c][1], 1)
                    act.wait_ge(filled[c][2], nth(c, 2, h, 0))
                    act.activation(flat(e2[c][:]), flat(bank[c][2][:]), ACT.Exp).then_inc(read[c][2], 1)
                if more:
                    if not first:
                        act.wait_ge(read[1][0], FILLS[1][0] * h)
                    load_columns(h + 1, 1 - b)
                    act.wait_ge(w_loaded[1 - b], 48 * (i + b + 1))
                    take(h + 1, 1 - b, h, Q)
                act.wait_ge(col_loaded[b], 16 * (i + 1))
                for c in range(2):
                    if not first:
                        act.wait_ge(filled[c][1], FILLS[c][1] * h)
                    scaled_copies(c, 2, h, 1, bv[c], b, B)
                if not first:
                    act.wait_ge(read[1][0], FILLS[1][0] * h)
                scaled_copies(0, 1, h, 2, k_end, b, TO_END)
                for c in range(2):
                    take_copy(c, 0, h, 1, MT[c][0])
                if more:
                    take(h + 1, 1 - b, h, K)
                if not first:
                    act.wait_ge(mean_ready, h)
                    act.activation(sd[:], mean_var[:, :, 1], ACT.Sqrt, bias=core.norm_eps[:]).then_inc(sd_ready, 1)
                for n in range(1, LEVELS - 1):
                    for c in range(2):
                        take_copy(c, 1, h, (1 if c else 2) + n, MT[c][n % 2])
                    if n == 1 and more:
                        take(h + 1, 1 - b, h, V)
                    if n == 2:
                        if not first:
                            use = p_use(h, 3, more)
                            take_o(use, h - 1)
                            store_o(use, h - 1)
                    if n == 3 and more:
                        take_gate(h + 1, 1 - b, h, first)
                if more:
                    for which in range(3):
                        silu(h + 1, 1 - b, which, first)
                take_copy(0, 1, h, 8, u[0])
                take_copy(0, 2, h, 8, state)
                scaled_copies(1, 2, h, 8, o_state, b, FROM_START)
                take_copy(1, 1, h, 7, u[1])

            def epilogue():
                use = p_use(HEADS2 - 1, 3, False) + 1
                act.wait_ge(mean_ready, HEADS2)
                act.activation(sd[:], mean_var[:, :, 1], ACT.Sqrt, bias=core.norm_eps[:]).then_inc(sd_ready, 1)
                take_o(use, HEADS2 - 1)
                store_o(use, HEADS2 - 1)
                act.wait_ge(o_stored, 16 * HEADS2)

            over_heads(act, prologue, step, epilogue)

        @block.vector
        def _(dve):
            def convolve(p, b, which):
                dve.wait_ge(p_read[1], conv_use[0](which))
                for j in range(TAPS - 1):
                    n = 9 * p + 3 * which + j
                    if j > 0:
                        dve.wait_ge(conv_step, n)
                    dve.scalar_tensor_tensor(out=taps[which][:], in0=padded[which][:, :, j:j + SEQ],
                                             scalar=conv[b][:, which, j:j + 1], in1=taps[which][:],
                                             op0=ALU.mult, op1=ALU.add).then_inc(conv_step, 1)

            def moments(h):
                for t in range(TILES):
                    last = dve.bn_stats(stats[:, t, :], o[:, t, :])
                last.then_inc(stats_ready, 1)
                dve.wait_ge(stats_ready, h + 1)
                dve.memset(spare[:], 0.0)
                for t in range(TILES):
                    last = dve.bn_aggr(mean_var[:, t, :], stats[:, t, :])
                last.then_inc(mean_ready, 1)

            def normalise(h, use):
                dve.wait_ge(sd_ready, h + 1)
                dve.reciprocal(rstd[:], sd[:]).then_inc(rstd_ready, 1)
                dve.wait_ge(rstd_ready, h + 1)
                if use is not None:
                    dve.wait_ge(p_filled[1], use)
                for t in range(TILES):
                    last = dve.tensor_scalar(on[:, t, :], o[:, t, :], mean_var[:, t, 0:1], rstd[:, t:t + 1],
                                             ALU.subtract, ALU.mult)
                last.then_inc(on_ready, 1)

            conv_use = [None]

            def prologue():
                dve.wait_ge(pool_step, 4)
                conv_use[0] = lambda which: p_use(-1, which, True)
                for which in range(3):
                    convolve(0, 0, which)

            def step(h, i, b, first, more):
                conv_use[0] = lambda which: p_use(h, which, more)
                dve.wait_ge(col_loaded[b], 16 * (i + 1))
                for c in range(2):
                    dve.wait_ge(e1_ready[c], h + 1)
                    dve.wait_ge(filled[c][0], nth(c, 0, h, 0))
                    for s in range(SY):
                        last = dve.scalar_tensor_tensor(out=M[c][0][:, s, :], in0=bank[c][0][:, s, :],
                                                        scalar=columns(b, NEG_B, c)[:, s:s + 1],
                                                        in1=e1[c][:, s, :], op0=ALU.mult, op1=ALU.mult)
                    last.then_inc(read[c][0], 1)
                for c in range(2):
                    dve.wait_ge(e2_ready[c], h + 1)
                    dve.wait_ge(filled[c][1], nth(c, 1, h, 1))
                    dve.tensor_tensor(flat(qk[c][:]), flat(bank[c][1][:]), flat(e2[c][:]), ALU.mult)\
                        .then_inc(read[c][1], 1)
                if not first:
                    dve.wait_ge(read[1][0], FILLS[1][0] * (h - 1) + 10)
                    moments(h - 1)
                for c in range(2):
                    dve.wait_ge(read[c][0], nth(c, 0, h, 1))
                    dve.tensor_tensor(Y[c][0][:], MT[c][0][:], along(core.ident), ALU.add).then_inc(y0_ready[c], 1)
                if more:
                    convolve(h + 1, 1 - b, Q)
                if not first:
                    normalise(h - 1, on_free[0])
                for n in range(1, LEVELS):
                    old, new = (n - 1) % 2, n % 2
                    for c in range(2):
                        dve.wait_ge(filled[c][0], nth(c, 0, h, 1 + n))
                        dve.tensor_copy(flat(M[c][new][:]), flat(bank[c][0][:])).then_inc(read[c][0], 1)
                    for c in range(2):
                        dve.wait_ge(filled[c][2], nth(c, 2, h, 1 + n))
                        if n > 1:
                            dve.wait_ge(read[c][2], nth(c, 2, h, n))
                        dve.tensor_tensor(flat(Y[c][new][:]), flat(bank[c][2][:]), flat(Y[c][old][:]), ALU.add)\
                            .then_inc(read[c][2], 1)
                    if n == 1 and more:
                        convolve(h + 1, 1 - b, K)
                    if n == 3 and more:
                        convolve(h + 1, 1 - b, V)
                dve.wait_ge(filled[0][0], nth(0, 0, h, 8))
                dve.tensor_copy(tiles(o[:], 0), bank[0][0][:]).then_inc(read[0][0], 1)
                dve.wait_ge(read[1][2], nth(1, 2, h, 1))
                dve.wait_ge(filled[1][0], nth(1, 0, h, 8))
                for s in range(SY):
                    last = dve.scalar_tensor_tensor(out=r[:, s, :], in0=bank[1][0][:, s, :],
                                                    scalar=columns(b, NEG_BG, 1)[:, s:s + 1],
                                                    in1=bv[1][:, s, :], op0=ALU.mult, op1=ALU.add)
                last.then_inc(read[1][0], 1)
                dve.wait_ge(read[1][2], nth(1, 2, h, 8))
                dve.wait_ge(filled[1][0], nth(1, 0, h, 9))
                dve.tensor_tensor(tiles(o[:], 1), bank[1][0][:], o_state[:], ALU.add).then_inc(read[1][0], 1)

            on_free = [None]
            prologue()
            step(0, 0, 0, True, True)
            on_free[0] = None
            step(1, 0, 1, False, True)
            on_free[0] = p_use(1, 3, True)
            step(2, 1, 0, False, True)
            with dve.Fori(2, HEADS2 // 2) as i:
                on_free[0] = p_use(2 * i - 2, 3, True)
                step(2 * i - 1, i - 1, 1, False, True)
                on_free[0] = p_use(2 * i - 1, 3, True)
                step(2 * i, i, 0, False, True)
            on_free[0] = p_use(HEADS2 - 2, 3, True)
            step(HEADS2 - 1, HEADS2 // 2 - 1, 1, False, False)
            dve.wait_ge(read[1][0], FILLS[1][0] * HEADS2)
            moments(HEADS2 - 1)
            normalise(HEADS2 - 1, p_use(HEADS2 - 1, 3, False))

        @block.gpsimd
        def _(pool):
            def prepare(h, i, b, first):
                pool.wait_ge(col_loaded[b], 16 * (i + 1))
                for c in range(2):
                    if not first:
                        pool.wait_ge(read[c][0], nth(c, 0, h - 1, 0))
                        pool.wait_ge(read[c][1], nth(c, 1, h - 1, 1))
                    la = columns(b, LOG_A, c).unsqueeze(2).broadcast_to([P, SY, P])
                    pool.tensor_tensor(la_before[c][:], along(core.before), la, ALU.mult).then_inc(la_ready, 1)
                    pool.tensor_tensor(la_upto[c][:], along(core.upto), la, ALU.mult).then_inc(la_ready, 1)

            def gate_o(h, b):
                every = [P, TILES, DH2]
                pool.wait_ge(on_ready, h + 1)
                pool.tensor_tensor(on[:], on[:], gain[:].unsqueeze(1).broadcast_to(every), ALU.mult)\
                    .then_inc(gained, 1)
                pool.wait_ge(gained, 3 * h + 1)
                pool.tensor_tensor(on[:], on[:], offset[:].unsqueeze(1).broadcast_to(every), ALU.add)\
                    .then_inc(gained, 1)
                pool.wait_ge(gained, 3 * h + 2)
                pool.tensor_tensor(on[:], on[:], gate[b][:], ALU.mult).then_inc(gained, 1)

            def prologue():
                for x in padded:
                    pool.memset(x[:, :, 0:PAD], 0.0).then_inc(pool_step, 1)
                pool.tensor_scalar(upto_scaled[:], core.upto[:], float(DH2) ** -0.5, None, ALU.mult)\
                    .then_inc(pool_step, 1)
                pool.wait_ge(pool_step, 4)
                pool.wait_ge(rows_loaded, 32)
                prepare(0, 0, 0, True)

            def step(h, i, b, first, more):
                for c in range(2):
                    pool.wait_ge(read[c][1], nth(c, 1, h, 0))
                    pool.tensor_tensor(e1[c][:], e1[c][:], along(core.after), ALU.mult).then_inc(e1_ready[c], 1)
                    pool.wait_ge(read[c][2], nth(c, 2, h, 0))
                    pool.tensor_tensor(e2[c][:], e2[c][:], along(upto_scaled), ALU.mult).then_inc(e2_ready[c], 1)
                if not first:
                    gate_o(h - 1, 1 - b)
                if more:
                    prepare(h + 1, i + b, 1 - b, False)

            def epilogue():
                gate_o(HEADS2 - 1, 1)

            over_heads(pool, prologue, step, epilogue)


def l2_attention(nc, core, table, w_gates, b_gates, w_heads, conv_heads, ln_w, ln_b, w_out):
    with ExitStack() as ctx:
        oT = ctx.enter_context(nc.sbuf_tensor("l2a_oT", [P, HEADS2, TOKENS], F32))
        l2_decay_stage(nc, core, w_gates, b_gates, table)
        l2_heads_stage(nc, core, w_heads, conv_heads, table, ln_w, ln_b, oT)
        wide_project_stage(nc, core, "l2_project", oT, w_out, None, HEADS2)


def l2_routed_stage(nc, core, name, xn, slot_of, weight_parts, in_weights, out_weights):
    EG = HALF // CAPACITY2
    GROUPS = EXPERTS2 // EG
    PAIRS = EG // 2
    PARTS = 3
    S = CAPACITY2
    with Stage(nc, name) as st:
        number = st.sb("number", [P, S], I32)
        slot = st.sb("slot", [P, S], BF16)
        ident = st.sb("ident", [P, P], BF16)
        rest = st.sb("rest", [P, TILES, D])
        xp = [st.sb(f"xp{i}", [P, TILES, D], BF16) for i in range(PARTS)]
        w_in = [st.sb(f"w_in{b}", [P, EG, KC * 2 * F2]) for b in range(2)]
        w_out = [st.sb(f"w_out{b}", [F2, EG, D]) for b in range(2)]
        hot = [st.sb(f"hot{b}", [P, TILES, EG, S], BF16) for b in range(2)]
        hotT = st.sb("hotT", [P, PAIRS, TOKENS], BF16)
        xgT = st.sb("xgT", [P, KC, HALF])
        gate = st.sb("gate", [F2, HALF])
        hidden = st.sb("hidden", [F2, HALF])
        pair_weight = st.sb("pair_weight", [P, PAIRS, 2])
        slot_weight = st.sb("slot_weight", [P, PAIRS])
        eo = st.sb("eo", [P, PAIRS, D])
        eo_rest = st.sb("eo_rest", [P, PAIRS, D])
        ep = [st.sb(f"ep{i}", [P, PAIRS, D], BF16) for i in range(PARTS)]
        bank_x = [st.ps(f"bank_x{c}", [P, HALF]) for c in range(KC)]
        bank_g = st.ps("bank_g", [P, HALF])
        bank_u = st.ps("bank_u", [P, HALF])
        bank_t = st.ps("bank_t", [P, TOKENS], BF16)
        bank_e = st.ps("bank_e", [P, 2, D])
        bank_a = [st.ps(f"bank_a{i}", [P, 2, D]) for i in range(2)]

        const_ready = st.sem("const_ready")
        split = st.sem("split")
        w_loaded = [st.sem(f"w_loaded{b}") for b in range(2)]
        hot_ready = st.sem("hot_ready")
        x_filled = st.sem("x_filled")
        x_read = [st.sem(f"x_read{c}") for c in range(KC)]
        up_filled = st.sem("up_filled")
        gate_ready = st.sem("gate_ready")
        hidden_ready = st.sem("hidden_ready")
        t_filled = st.sem("t_filled")
        t_read = st.sem("t_read")
        e_filled = st.sem("e_filled")
        e_read = st.sem("e_read")
        slot_weight_ready = st.sem("slot_weight_ready")
        eo_ready = st.sem("eo_ready")
        part0_ready = st.sem("part0_ready")
        rest_ready = st.sem("rest_ready")
        part1_ready = st.sem("part1_ready")
        part2_ready = st.sem("part2_ready")
        a_filled = [st.sem(f"a_filled{i}") for i in range(2)]
        a_read = [st.sem(f"a_read{i}") for i in range(2)]
        block = st.block()

        def over_groups(eng, prologue, step):
            prologue()
            step(0, 0, 0, True, False)
            with eng.Fori(1, GROUPS // 2) as i:
                step(2 * i - 1, i - 1, 1, False, False)
                step(2 * i, i, 0, False, False)
            step(GROUPS - 1, GROUPS // 2 - 1, 1, False, True)

        @block.sync
        def _(sp):
            def load(g, b, first):
                if not first:
                    sp.wait_ge(e_filled, 3 * (g - 1))
                sp.dma_start(w_in[b][:], in_weights[bass.ds(g * EG, EG)].rearrange("e p c g f -> p e (c g f)"))\
                    .then_inc(w_loaded[b], 16)
                sp.dma_start(w_out[b][:], out_weights[bass.ds(g * EG, EG)].rearrange("e f d -> f e d"))\
                    .then_inc(w_loaded[b], 16)

            load(0, 0, True)
            load(1, 1, True)
            with sp.Fori(1, GROUPS // 2) as i:
                load(2 * i, 0, False)
                load(2 * i + 1, 1, False)

        @block.tensor
        def _(pe):
            def gather(g, b, first, c, tiles):
                if tiles[0] == 0:
                    pe.wait_ge(hot_ready, TILES * (g + 1))
                    if not first:
                        pe.wait_ge(x_read[c], g)
                for t in tiles:
                    for i in range(PARTS):
                        mm = pe.matmul(bank_x[c][:], xp[i][:, t, c * P:(c + 1) * P],
                                       hot[b][:, t].rearrange("p e s -> p (e s)"),
                                       start=(t == 0 and i == 0), stop=(t == TILES - 1 and i == PARTS - 1))
                if tiles[-1] == TILES - 1:
                    mm.then_inc(x_filled, 1)

            def turn_hot(g, b, first, q):
                if not (first and q == 0):
                    pe.wait_ge(t_read, PAIRS * g + q)
                for t in range(TILES):
                    tr = pe.transpose(bank_t[:, t * P:(t + 1) * P],
                                      hot[b][:, t, 2 * q:2 * q + 2, :].rearrange("p e s -> p (e s)"), ident[:])
                tr.then_inc(t_filled, 1)

            def down(g, b, q):
                if q == 0:
                    pe.wait_ge(hidden_ready, g + 1)
                    pe.wait_ge(e_read, g + 1)
                if q == 2:
                    pe.wait_ge(eo_ready, PAIRS * g + 2)
                for j in range(2):
                    e = 2 * q + j
                    mm = pe.matmul(bank_e[j * S:(j + 1) * S, q % 2, :], hidden[:, e * S:(e + 1) * S],
                                   w_out[b][:, e, :], start=True, stop=True)
                if q % 2 == 1:
                    mm.then_inc(e_filled, 1)

            def prologue():
                pe.wait_ge(const_ready, 3)
                pe.wait_ge(split, 5)
                for c in range(KC):
                    gather(0, 0, True, c, range(TILES))

            def step(g, i, b, first, last):
                pe.wait_ge(w_loaded[b], 32 * (i + 1))
                for c in range(KC):
                    pe.wait_ge(x_read[c], g + 1)
                if not first:
                    pe.wait_ge(hidden_ready, g)
                for e in range(EG):
                    for j, bank in enumerate((bank_g, bank_u)):
                        for c in range(KC):
                            at = (2 * c + j) * F2
                            mm = pe.matmul(bank[0:F2, e * S:(e + 1) * S], w_in[b][:, e, at:at + F2],
                                           xgT[:, c, e * S:(e + 1) * S], start=(c == 0), stop=(c == KC - 1))
                mm.then_inc(up_filled, 1)
                if not first:
                    pe.wait_ge(eo_ready, PAIRS * g)
                for q in range(PAIRS):
                    for t in range(TILES):
                        mm = pe.matmul(bank_e[:, 0, 2 * PARTS * q:2 * PARTS * (q + 1)],
                                       hot[b][:, t, 2 * q:2 * q + 2, :].rearrange("p e s -> p (e s)"),
                                       weight_parts[:, t, bass.ds(g * EG + 2 * q, 2), :].rearrange("p e i -> p (e i)"),
                                       start=(t == 0), stop=(t == TILES - 1))
                mm.then_inc(e_filled, 1)
                turn_hot(g, b, first, 0)
                down(g, b, 0)
                down(g, b, 1)
                turn_hot(g, b, first, 1)
                if not last:
                    gather(g + 1, 1 - b, False, 0, range(TILES // 2))
                down(g, b, 2)
                down(g, b, 3)
                turn_hot(g, b, first, 2)
                if not last:
                    gather(g + 1, 1 - b, False, 0, range(TILES // 2, TILES))
                turn_hot(g, b, first, 3)
                if not last:
                    gather(g + 1, 1 - b, False, 1, range(TILES))
                pe.wait_ge(part0_ready, g + 1)
                pe.wait_ge(part1_ready, g + 1)
                pe.wait_ge(part2_ready, g + 1)
                pe.wait_ge(t_read, PAIRS * (g + 1))
                for n in range(TILES // 2):
                    if not (first and n < 2):
                        pe.wait_ge(a_read[n % 2], 2 * g + n // 2)
                    for r in range(2):
                        t = 2 * n + r
                        for q in range(PAIRS):
                            for i in range(PARTS):
                                mm = pe.matmul(bank_a[n % 2][:, r, :], hotT[:, q, t * P:(t + 1) * P],
                                               ep[i][:, q, :], start=(q == 0 and i == 0),
                                               stop=(q == PAIRS - 1 and i == PARTS - 1))
                    mm.then_inc(a_filled[n % 2], 1)

            over_groups(pe, prologue, step)

        @block.scalar
        def _(act):
            def take_x(g):
                act.wait_ge(x_filled, KC * g + 1)
                act.copy(xgT[:, 0, :], bank_x[0][:]).then_inc(x_read[0], 1)

            def prologue():
                act.copy(xp[0][:], xn[:]).then_inc(split, 1)
                act.wait_ge(split, 2)
                act.copy(xp[1][:], rest[:]).then_inc(split, 1)
                take_x(0)

            def step(g, i, b, first, last):
                act.wait_ge(up_filled, g + 1)
                if not first:
                    act.wait_ge(hidden_ready, g)
                act.activation(gate[:], bank_g[0:F2, :], ACT.Silu).then_inc(gate_ready, 1)
                def take_turned(q):
                    act.wait_ge(t_filled, PAIRS * g + q + 1)
                    act.copy(hotT[:, q, :], bank_t[:]).then_inc(t_read, 1)

                def weigh(q):
                    if q % 2 == 0:
                        act.wait_ge(e_filled, 3 * g + 2 + q // 2)
                    act.activation(eo[:, q, :], bank_e[:, q % 2, :], ACT.Copy,
                                   scale=slot_weight[:, q:q + 1]).then_inc(eo_ready, 1)

                take_turned(0)
                act.wait_ge(slot_weight_ready, 2 * (g + 1))
                if not first:
                    act.wait_ge(rest_ready, g)
                weigh(0)
                weigh(1)
                take_turned(1)
                weigh(2)
                weigh(3)
                act.wait_ge(eo_ready, PAIRS * (g + 1))
                if not first:
                    act.wait_ge(a_filled[1], 2 * g)
                act.copy(ep[0][:], eo[:]).then_inc(part0_ready, 1)
                take_turned(2)
                act.wait_ge(rest_ready, g + 1)
                act.copy(ep[1][:], eo_rest[:]).then_inc(part1_ready, 1)
                take_turned(3)
                if not last:
                    take_x(g + 1)

            over_groups(act, prologue, step)

        @block.gpsimd
        def _(pool):
            pool.iota(number[:], pattern=[[1, S]], base=0, channel_multiplier=0).then_inc(const_ready, 1)
            pool.wait_ge(const_ready, 1)
            pool.tensor_copy(slot[:], number[:]).then_inc(const_ready, 1)
            pool.tensor_copy(ident[:], core.ident[:]).then_inc(const_ready, 1)

        @block.vector
        def _(dve):
            def one_hot(g, b, used):
                if used is not None:
                    dve.wait_ge(t_filled, PAIRS * used)
                for t in range(TILES):
                    dve.tensor_tensor(hot[b][:, t], slot[:].unsqueeze(1).broadcast_to([P, EG, S]),
                                      slot_of[:, t, bass.ds(g * EG, EG)].unsqueeze(2).broadcast_to([P, EG, S]),
                                      ALU.is_equal).then_inc(hot_ready, 1)

            def take_x(g):
                dve.wait_ge(x_filled, KC * g + 2)
                dve.tensor_copy(xgT[:, 1, :], bank_x[1][:]).then_inc(x_read[1], 1)

            def prologue():
                dve.wait_ge(const_ready, 3)
                one_hot(0, 0, None)
                dve.wait_ge(split, 1)
                dve.tensor_tensor(rest[:], xn[:], xp[0][:], ALU.subtract).then_inc(split, 1)
                dve.wait_ge(split, 3)
                dve.tensor_tensor(xp[2][:], rest[:], xp[1][:], ALU.subtract).then_inc(split, 2)
                take_x(0)

            def step(g, i, b, first, last):
                dve.wait_ge(gate_ready, g + 1)
                dve.tensor_tensor(hidden[:], gate[:], bank_u[0:F2, :], ALU.mult).then_inc(hidden_ready, 1)
                dve.wait_ge(e_filled, 3 * g + 1)
                dve.tensor_reduce(pair_weight[:], bank_e[:, 0, 0:2 * PARTS * PAIRS].rearrange(
                    "p (q j i) -> p q j i", q=PAIRS, j=2), AX_X, ALU.add).then_inc(e_read, 1)
                dve.wait_ge(e_read, g + 1)
                if not first:
                    dve.wait_ge(eo_ready, PAIRS * g)
                for j in range(2):
                    dve.tensor_copy(slot_weight[j * S:(j + 1) * S, :], pair_weight[j * S:(j + 1) * S, :, j])\
                        .then_inc(slot_weight_ready, 1)
                if not last:
                    one_hot(g + 1, 1 - b, None if first else g)
                dve.wait_ge(part0_ready, g + 1)
                dve.tensor_tensor(eo_rest[:], eo[:], ep[0][:], ALU.subtract).then_inc(rest_ready, 1)
                dve.wait_ge(part1_ready, g + 1)
                dve.tensor_tensor(ep[2][:], eo_rest[:], ep[1][:], ALU.subtract).then_inc(part2_ready, 1)
                if not last:
                    take_x(g + 1)
                for n in range(TILES // 2):
                    dve.wait_ge(a_filled[n % 2], 2 * g + n // 2 + 1)
                    if not first:
                        dve.wait_ge(a_read[n % 2], 2 * g + n // 2)
                    part = core.x[:, 2 * n:2 * n + 2, :]
                    dve.tensor_tensor(part, part, bank_a[n % 2][:], ALU.add).then_inc(a_read[n % 2], 1)

            over_groups(dve, prologue, step)


def l2_ffn(nc, core, name, xn, t):
    with ExitStack() as ctx:
        slot_of = ctx.enter_context(nc.sbuf_tensor(f"{name}_slot_of", [P, TILES, EXPERTS2], BF16))
        parts = ctx.enter_context(nc.sbuf_tensor(f"{name}_parts", [P, TILES, EXPERTS2, 3], BF16))
        route_stage(nc, core, f"{name}_route", t["l2_router"], EXPERTS2, TOP2, slot_of=slot_of, parts=parts)
        l2_routed_stage(nc, core, f"{name}_routed", xn, slot_of, parts, t["l2_in_w"], t["l2_out_w"])
    gated_units_stage(nc, core, f"{name}_shared", F2, SHARED2, t["l2_shared_in_w"], t["l2_shared_out_w"], None)


HIDDEN3 = 1024
CHUNKS3 = HIDDEN3 // P
BLOCK3 = 64
RANK3 = 16
KV3 = 4
REP3 = HEADS // KV3
WIN = 16
BLOCKS3 = SEQ // WIN
PER3 = P // WIN


def l3_decode_stage(nc, core, w_up, w_down, up_q, up_scale, up_a, up_b, down_q, down_scale, down_a, down_b):
    with Stage(nc, "l3_decode") as st:
        q_up = st.sb("q_up", [P, KC, HIDDEN3], I32)
        q_down = st.sb("q_down", [P, CHUNKS3, D], I32)
        s_up = st.sb("s_up", [P, KC, HIDDEN3])
        s_down = st.sb("s_down", [P, CHUNKS3, D])
        a_up = st.sb("a_up", [RANK3, D])
        b_up = st.sb("b_up", [RANK3, HIDDEN3])
        a_down = st.sb("a_down", [RANK3, HIDDEN3])
        b_down = st.sb("b_down", [RANK3, D])
        ps_up = [st.ps(f"ps_up{i}", [P, HALF]) for i in range(4)]
        ps_down = [st.ps(f"ps_down{i}", [P, 2, D]) for i in range(4)]
        up_loaded = st.sem("up_loaded")
        down_loaded = st.sem("down_loaded")
        rank_loaded = st.sem("rank_loaded")
        up_done = st.sem("up_done")
        down_done = st.sem("down_done")
        scaled = st.sem("scaled")
        block = st.block()
        G = P // BLOCK3

        @block.sync
        def _(sp):
            for dst, src in ((a_up, up_a), (b_up, up_b), (a_down, down_a), (b_down, down_b)):
                sp.dma_start(dst[:], src).then_inc(rank_loaded, 16)
            sp.dma_start(q_up[:], up_q.rearrange("(c p) n -> p c n", p=P)).then_inc(up_loaded, 16)
            for c in range(KC):
                for j in range(G):
                    sp.dma_start(s_up[j * BLOCK3:(j + 1) * BLOCK3, c, :],
                                 up_scale[G * c + j].partition_broadcast(BLOCK3)).then_inc(up_loaded, 16)

        @block.scalar
        def _(act):
            act.dma_start(q_down[:], down_q.rearrange("(c p) n -> p c n", p=P)).then_inc(down_loaded, 16)
            for j in range(G):
                act.dma_start(s_down[j * BLOCK3:(j + 1) * BLOCK3, :, :],
                              down_scale.rearrange("(c j) n -> j c n", j=G)[j].partition_broadcast(BLOCK3))\
                    .then_inc(down_loaded, 16)

        @block.tensor
        def _(pe):
            pe.wait_ge(rank_loaded, 64)
            for c in range(KC):
                for h in range(2):
                    mm = pe.matmul(ps_up[2 * c + h][:], a_up[:, c * P:(c + 1) * P],
                                   b_up[:, h * HALF:(h + 1) * HALF], start=True, stop=True)
            mm.then_inc(up_done, 1)
            for c in range(CHUNKS3):
                mm = pe.matmul(ps_down[c // 2][:, c % 2, :], a_down[:, c * P:(c + 1) * P], b_down[:],
                               start=True, stop=True)
            mm.then_inc(down_done, 1)

        @block.vector
        def _(dve):
            dve.wait_ge(up_loaded, 16 * (1 + KC * G))
            dve.scalar_tensor_tensor(out=w_up[:], in0=q_up[:], scalar=-7.5, in1=s_up[:],
                                     op0=ALU.add, op1=ALU.mult).then_inc(scaled, 1)
            dve.wait_ge(down_loaded, 16 * (1 + G))
            dve.scalar_tensor_tensor(out=w_down[:], in0=q_down[:], scalar=-7.5, in1=s_down[:],
                                     op0=ALU.add, op1=ALU.mult).then_inc(scaled, 1)
            dve.wait_ge(scaled, 1)
            dve.wait_ge(up_done, 1)
            for c in range(KC):
                for h in range(2):
                    part = w_up[:, c, h * HALF:(h + 1) * HALF]
                    dve.tensor_tensor(part, part, ps_up[2 * c + h][:], ALU.add)
            dve.wait_ge(scaled, 2)
            dve.wait_ge(down_done, 1)
            for i in range(4):
                part = w_down[:, 2 * i:2 * i + 2, :]
                dve.tensor_tensor(part, part, ps_down[i][:], ALU.add)


def l3_ffn_stage(nc, core, name, w_up, w_down, b_up, b_down):
    with Stage(nc, name) as st:
        bias = st.sb("bias", [P, CHUNKS3])
        row = st.sb("row", [P, D])
        hidden = st.sb("hidden", [P, CHUNKS3, TOKENS])
        NB = 4
        ps_up = [st.ps(f"ps_up{i}", [P, HALF]) for i in range(NB)]
        ps_down = [st.ps(f"ps_down{i}", [P, 2, D]) for i in range(4)]
        loaded = st.sem("loaded")
        up_done = st.sem("up_done")
        first_half = st.sem("first_half")
        second_half = st.sem("second_half")
        row_halved = st.sem("row_halved")
        row_added = st.sem("row_added")
        down_done = st.sem("down_done")
        block = st.block()

        @block.sync
        def _(sp):
            sp.dma_start(bias[:], b_up).then_inc(loaded, 16)
            sp.dma_start(row[:], b_down.partition_broadcast(P)).then_inc(loaded, 16)

        @block.tensor
        def _(pe):
            for f in range(CHUNKS3):
                for h in range(HALVES):
                    n = HALVES * f + h
                    if n >= NB:
                        pe.wait_ge((first_half, second_half)[h], f - 1)
                    for c in range(KC):
                        mm = pe.matmul(ps_up[n % NB][:], w_up[:, c, f * P:(f + 1) * P],
                                       core.xnT[:, c, h * HALF:(h + 1) * HALF], start=(c == 0), stop=(c == KC - 1))
                    mm.then_inc(up_done, 1)
            for t in range(TILES):
                pe.wait_ge(first_half if t < TILES // 2 else second_half, CHUNKS3)
                for f in range(CHUNKS3):
                    mm = pe.matmul(ps_down[t // 2][:, t % 2, :], hidden[:, f, t * P:(t + 1) * P], w_down[:, f, :],
                                   start=(f == 0), stop=(f == CHUNKS3 - 1))
                mm.then_inc(down_done, 1)

        @block.scalar
        def _(act):
            act.wait_ge(loaded, 32)
            for f in range(CHUNKS3):
                act.wait_ge(up_done, HALVES * f + 1)
                act.activation(hidden[:, f, 0:HALF], ps_up[HALVES * f % NB][:], ACT.Relu,
                               bias=bias[:, f:f + 1]).then_inc(first_half, 1)

        @block.vector
        def _(dve):
            dve.wait_ge(loaded, 32)
            dve.tensor_scalar(row[:], row[:], 0.5, None, ALU.mult).then_inc(row_halved, 1)
            dve.wait_ge(row_halved, 1)
            dve.tensor_tensor(core.x[:], core.x[:], row[:].unsqueeze(1).broadcast_to([P, TILES, D]), ALU.add)\
                .then_inc(row_added, 1)
            for f in range(CHUNKS3):
                dve.wait_ge(up_done, HALVES * f + 2)
                dve.tensor_scalar(hidden[:, f, HALF:2 * HALF], ps_up[(HALVES * f + 1) % NB][:], bias[:, f:f + 1],
                                  0.0, ALU.add, ALU.max).then_inc(second_half, 1)
            dve.wait_ge(row_added, 1)
            for q in range(4):
                dve.wait_ge(down_done, 2 * q + 2)
                part = core.x[:, 2 * q:2 * q + 2, :]
                dve.scalar_tensor_tensor(out=part, in0=ps_down[q][:], scalar=0.5, in1=part,
                                         op0=ALU.mult, op1=ALU.add)


def l3_attention(nc, core, weights, angles, head_rows, window, pool_w, w_out):
    SCALE = 1.0 / float(HEAD) ** 0.5
    GROUP = P // HEAD
    with ExitStack() as ctx:
        def sb(name, shape):
            return ctx.enter_context(nc.sbuf_tensor(f"l3a_{name}", shape, F32))

        qk = sb("qk", [P, TILES, (HEADS + KV3) * HEAD])
        v = sb("v", [P, TILES, KV3, HEAD])
        qT = sb("qT", [P, KC, TOKENS])
        oT = sb("oT", [P, KC, TOKENS])
        rope_qkv_stage(nc, core, "l3_qkv", weights, angles, HEADS + KV3, qk, KV3 * HEAD, lambda t: v[:, t, :, :])
        turn_stage(nc, core, "l3_turn", qk, KC, qT)
        with Stage(nc, "l3_heads") as st:
            taste = st.sb("taste", [P, 2, HEAD])
            rows = st.sb("rows", [P, GROUP])
            inside = st.sb("inside", [P, 2, P])
            diagonal = st.sb("diagonal", [P, P])
            term = [st.sb(f"term{b}", [P, 2, KV3, HEAD]) for b in range(2)]
            logit = st.sb("logit", [P, TILES, 2 * KV3])
            R = 2 * KV3
            NW = TOKENS // WIN
            peak = st.sb("peak", [R, NW])
            total = st.sb("total", [R, NW])
            share = st.sb("share", [R, TOKENS])
            both = st.sb("both", [P, TILES, 2, KV3])
            w = st.sb("w", [P, TILES, KV3])
            kw = st.sb("kw", [P, TILES, D])
            vw = st.sb("vw", [P, TILES, D])
            packed = st.sb("packed", [P, BATCH, KC, 2, P])
            z = [st.sb(f"z{b}", [P, D]) for b in range(2)]
            e = [st.sb(f"e{b}", [P, D]) for b in range(2)]
            prob = [st.sb(f"prob{b}", [P, D]) for b in range(2)]
            probT = [st.sb(f"probT{b}", [P, KC, P]) for b in range(2)]
            head_peak = st.sb("head_peak", [P, TILES, HEADS])
            head_total = st.sb("head_total", [P, TILES, HEADS])
            head_inverse = st.sb("head_inverse", [P, TILES, HEADS])
            ps_a = st.ps("ps_a", [P, HALVES, HALF])
            ps_w = st.ps("ps_w", [P, HALF])
            ps_s = [st.ps(f"ps_s{b}", [P, HALF]) for b in range(2)]
            ps_t = st.ps("ps_t", [P, HALF])
            ps_o = [st.ps(f"ps_o{b}", [P, HALF]) for b in range(2)]

            loaded = st.sem("loaded")
            rows_turned = st.sem("rows_turned")
            term_ready = st.sem("term_ready")
            logit_ready = st.sem("logit_ready")
            logit_turned = st.sem("logit_turned")
            step_done = st.sem("step_done")
            shifted = st.sem("shifted")
            exp_ready = st.sem("exp_ready")
            share_ready = st.sem("share_ready")
            share_turned = st.sem("share_turned")
            w_ready = st.sem("w_ready")
            kw_ready = st.sem("kw_ready")
            vw_ready = st.sem("vw_ready")
            block_summed = st.sem("block_summed")
            packed_ready = st.sem("packed_ready")
            scored = st.sem("scored")
            peak_ready = st.sem("peak_ready")
            z_ready = st.sem("z_ready")
            e_ready = st.sem("e_ready")
            total_ready = st.sem("total_ready")
            inverse_ready = st.sem("inverse_ready")
            prob_ready = st.sem("prob_ready")
            prob_turned = st.sem("prob_turned")
            probT_ready = st.sem("probT_ready")
            summed = st.sem("summed")
            o_copied = st.sem("o_copied")
            block = st.block()

            def keys(t):
                return qk[:, t, D:D + KV3 * HEAD].rearrange("p (h d) -> p h d", d=HEAD)

            def windows(ap):
                return ap.rearrange("p (n r) -> p n r", r=WIN)

            def repeated(ap):
                return ap.unsqueeze(2).broadcast_to([P, KV3, REP3, HEAD])

            def spread(t):
                return w[:, t, :].unsqueeze(2).unsqueeze(3).broadcast_to([P, KV3, REP3, HEAD])

            def wide(ap):
                return ap.rearrange("p (j r d) -> p j r d", j=KV3, r=REP3)

            def per_head(ap):
                return ap.rearrange("p (h s) -> p h s", h=HEADS)

            def across(ap, n, m):
                return ap.unsqueeze(2).broadcast_to([ap.shape[0], n, m])

            @block.sync
            def _(sp):
                sp.dma_start(taste[:], pool_w.partition_broadcast(P)).then_inc(loaded, 16)
                sp.dma_start(rows[:], head_rows).then_inc(loaded, 16)
                sp.dma_start(inside[:], window).then_inc(loaded, 16)

            @block.tensor
            def _(pe):
                pe.wait_ge(logit_ready, TILES)
                for t in range(TILES):
                    tr = pe.transpose(ps_a[0:R, t // 4, (t % 4) * P:(t % 4 + 1) * P], logit[:, t, :], core.ident[:])
                tr.then_inc(logit_turned, 1)
                pe.wait_ge(share_ready, 1)
                for t in range(TILES):
                    tr = pe.transpose(ps_w[:, t * R:(t + 1) * R], share[:, t * P:(t + 1) * P],
                                      core.ident[0:R, 0:R])
                tr.then_inc(share_turned, 1)
                for b in range(BATCH):
                    pe.wait_ge(kw_ready, 2 * b + 2)
                    pe.wait_ge(vw_ready, 2 * b + 2)
                    if b >= 2:
                        pe.wait_ge(packed_ready, b - 1)
                    for g in range(KC):
                        for j in range(2):
                            out = ps_a[:, b % 2, (2 * g + j) * P:(2 * g + j + 1) * P]
                            for par in range(2):
                                t = 2 * b + par
                                lhsT = kw[:, t, g * P:(g + 1) * P] if j == 0 else inside[:, par, :]
                                rhs = inside[:, par, :] if j == 0 else vw[:, t, g * P:(g + 1) * P]
                                mm = pe.matmul(out, lhsT, rhs, start=(par == 0), stop=(par == 1))
                    mm.then_inc(block_summed, 1)

                def scores(t):
                    pe.wait_ge(packed_ready, t // 2 + 1)
                    if t >= 2:
                        pe.wait_ge(z_ready, t - 1)
                    for g in range(KC):
                        mm = pe.matmul(ps_s[t % 2][:, g * P:(g + 1) * P], qT[:, g, t * P:(t + 1) * P],
                                       packed[:, t // 2, g, 0, :], start=True, stop=True)
                    mm.then_inc(scored, 1)

                def turn(t):
                    pe.wait_ge(prob_ready, t + 1)
                    if t >= 1:
                        pe.wait_ge(probT_ready, t)
                    for g in range(KC):
                        tr = pe.transpose(ps_t[:, g * P:(g + 1) * P], prob[t % 2][:, g * P:(g + 1) * P],
                                          core.ident[:])
                    tr.then_inc(prob_turned, 1)

                def values(t):
                    pe.wait_ge(probT_ready, t + 1)
                    if t >= 2:
                        pe.wait_ge(o_copied, t - 1)
                    for g in range(KC):
                        mm = pe.matmul(ps_o[t % 2][:, g * P:(g + 1) * P], packed[:, t // 2, g, 1, :],
                                       probT[t % 2][:, g, :], start=True, stop=True)
                    mm.then_inc(summed, 1)

                for t in range(TILES + 2):
                    if t < TILES:
                        scores(t)
                    if 1 <= t <= TILES:
                        turn(t - 1)
                    if t >= 2:
                        values(t - 2)

            @block.scalar
            def _(act):
                act.wait_ge(shifted, 1)
                act.activation(share[:], share[:], ACT.Exp).then_inc(exp_ready, 1)

                def copy_o(t):
                    act.wait_ge(summed, t + 1)
                    act.copy(oT[:, :, t * P:(t + 1) * P], ps_o[t % 2][:, 0:D].rearrange("p (c n) -> p c n", c=KC))\
                        .then_inc(o_copied, 1)

                for t in range(TILES):
                    act.wait_ge(z_ready, t + 1)
                    if t >= 2:
                        act.wait_ge(prob_ready, t - 1)
                    act.activation(e[t % 2][:], z[t % 2][:], ACT.Exp, scale=SCALE).then_inc(e_ready, 1)
                    if t >= 1:
                        act.wait_ge(prob_turned, t)
                        if t >= 3:
                            act.wait_ge(summed, t - 2)
                        act.copy(probT[(t - 1) % 2][:].rearrange("p c n -> p (c n)"), ps_t[:, 0:D])\
                            .then_inc(probT_ready, 1)
                    if t >= 2:
                        copy_o(t - 2)
                act.wait_ge(prob_turned, TILES)
                act.copy(probT[(TILES - 1) % 2][:].rearrange("p c n -> p (c n)"), ps_t[:, 0:D])\
                    .then_inc(probT_ready, 1)
                copy_o(TILES - 2)
                copy_o(TILES - 1)

            @block.gpsimd
            def _(pool):
                pool.wait_ge(loaded, 48)
                pool.tensor_copy(diagonal[:].rearrange("p (h d) -> p h d", d=HEAD), across(rows[:], GROUP, HEAD))\
                    .then_inc(rows_turned, 1)
                for t in range(TILES):
                    pool.wait_ge(w_ready, 1)
                    pool.tensor_tensor(wide(vw[:, t, :]), repeated(v[:, t, :, :]), spread(t), ALU.mult)\
                        .then_inc(vw_ready, 1)

            @block.vector
            def _(dve):
                steps = [0]

                def link(ins):
                    steps[0] += 1
                    ins.then_inc(step_done, 1)
                    dve.wait_ge(step_done, steps[0])

                dve.wait_ge(loaded, 48)
                for t in range(TILES):
                    if t >= 2:
                        dve.wait_ge(logit_ready, t - 1)
                    dve.tensor_tensor(term[t % 2][:], keys(t).unsqueeze(1).broadcast_to([P, 2, KV3, HEAD]),
                                      taste[:].unsqueeze(2).broadcast_to([P, 2, KV3, HEAD]), ALU.mult)\
                        .then_inc(term_ready, 1)
                    dve.wait_ge(term_ready, t + 1)
                    dve.tensor_reduce(logit[:, t, :].rearrange("p (a h) -> p a h", a=2), term[t % 2][:], AX_X,
                                      ALU.add).then_inc(logit_ready, 1)
                dve.wait_ge(logit_turned, 1)
                turned = ps_a[0:R, :, :].rearrange("p h n -> p (h n)")
                link(dve.tensor_reduce(peak[:], windows(turned), AX_X, ALU.max))
                dve.tensor_tensor(windows(share[:]), windows(turned), across(peak[:], NW, WIN), ALU.subtract)\
                    .then_inc(shifted, 1)
                dve.wait_ge(exp_ready, 1)
                link(dve.tensor_reduce(total[:], windows(share[:]), AX_X, ALU.add))
                link(dve.reciprocal(total[:], total[:]))
                dve.tensor_tensor(windows(share[:]), windows(share[:]), across(total[:], NW, WIN), ALU.mult)\
                    .then_inc(share_ready, 1)
                dve.wait_ge(share_turned, 1)
                link(dve.tensor_copy(both[:].rearrange("p t a h -> p (t a h)"), ps_w[:, 0:TILES * R]))
                link(dve.tensor_tensor(w[:], both[:, :, 0, :], both[:, :, 1, :], ALU.add))
                dve.tensor_scalar(w[:], w[:], 0.5, None, ALU.mult).then_inc(w_ready, 1)
                dve.wait_ge(w_ready, 1)
                for t in range(TILES):
                    dve.tensor_tensor(wide(kw[:, t, :]), repeated(keys(t)), spread(t), ALU.mult)\
                        .then_inc(kw_ready, 1)
                dve.wait_ge(rows_turned, 1)
                for b in range(BATCH):
                    dve.wait_ge(block_summed, b + 1)
                    dve.tensor_tensor(packed[:, b].rearrange("p g j n -> p (g j) n"),
                                      ps_a[:, b % 2, :].rearrange("p (g n) -> p g n", n=P),
                                      diagonal[:].unsqueeze(1).broadcast_to([P, 2 * KC, P]), ALU.mult)\
                        .then_inc(packed_ready, 1)

                def shift(t):
                    dve.wait_ge(scored, t + 1)
                    dve.tensor_reduce(head_peak[:, t, :], per_head(ps_s[t % 2][:, 0:D]), AX_X, ALU.max)\
                        .then_inc(peak_ready, 1)
                    dve.wait_ge(peak_ready, t + 1)
                    if t >= 2:
                        dve.wait_ge(e_ready, t - 1)
                    dve.tensor_tensor(per_head(z[t % 2][:]), per_head(ps_s[t % 2][:, 0:D]),
                                      across(head_peak[:, t, :], HEADS, BLOCKS3), ALU.subtract).then_inc(z_ready, 1)

                def normalise(t):
                    dve.wait_ge(e_ready, t + 1)
                    dve.tensor_reduce(head_total[:, t, :], per_head(e[t % 2][:]), AX_X, ALU.add)\
                        .then_inc(total_ready, 1)
                    dve.wait_ge(total_ready, t + 1)
                    dve.reciprocal(head_inverse[:, t, :], head_total[:, t, :]).then_inc(inverse_ready, 1)
                    dve.wait_ge(inverse_ready, t + 1)
                    if t >= 2:
                        dve.wait_ge(prob_turned, t - 1)
                    dve.tensor_tensor(per_head(prob[t % 2][:]), per_head(e[t % 2][:]),
                                      across(head_inverse[:, t, :], HEADS, BLOCKS3), ALU.mult).then_inc(prob_ready, 1)

                shift(0)
                for t in range(TILES):
                    if t + 1 < TILES:
                        shift(t + 1)
                    normalise(t)

        project_stage(nc, core, "l3_project", oT, w_out)


def build(nc, t, out):
    with ExitStack() as ctx:
        core = Core(nc, ctx)
        start_stage(nc, core, t["x"])

        l0_decode_stage(nc, core, t["lut"], t["l0_in_idx"], t["l0_out_idx"], t["l0_in_w"], t["l0_out_w"])
        norm_stage(nc, core)
        gated_units_stage(nc, core, "l0_ffn_a", F0, UNITS0, t["l0_in_w"], t["l0_out_w"], None)
        norm_stage(nc, core)
        l0_attention(nc, core, t["l0_qkv"], t["angles"], t["head_rows"], t["l0_scale"], t["l0_bias"], t["l0_wo"])
        norm_stage(nc, core)
        gated_units_stage(nc, core, "l0_ffn_b", F0, UNITS0, t["l0_in_w"], t["l0_out_w"], None)

        def l1_ffn(name):
            norm_stage(nc, core)
            with nc.sbuf_tensor(f"{name}_weights", [P, TILES, UNITS1], F32) as token_weights:
                route_stage(nc, core, f"{name}_route", t["l1_router"], EXPERTS1, TOP1,
                            UNITS_PER_EXPERT1, token_weights)
                gated_units_stage(nc, core, name, F1, UNITS1, t["l1_in_w"], t["l1_out_w"], token_weights)

        l1_ffn("l1_ffn_a")
        norm_stage(nc, core)
        l1_attention(nc, core, t["l1_wkv_a"], t["l1_norm_w"], t["l1_wq"], t["l1_wkv"], t["l1_columns"],
                     t["l1_sign"], t["l1_wo"], t["l1_bo"])
        l1_ffn("l1_ffn_b")

        def l2_feed_forward(name):
            with nc.sbuf_tensor(f"{name}_xn", [P, TILES, D], F32) as xn:
                norm_stage(nc, core, xn)
                l2_ffn(nc, core, name, xn, t)

        l2_feed_forward("l2_ffn_a")
        norm_stage(nc, core)
        l2_attention(nc, core, t["l2_table"], t["l2_w_gates"], t["l2_b_gates"], t["l2_w_heads"], t["l2_conv"],
                     t["l2_ln_w"], t["l2_ln_b"], t["l2_wo"])
        l2_feed_forward("l2_ffn_b")

        w_up = ctx.enter_context(nc.sbuf_tensor("l3_w_up", [P, KC, HIDDEN3], F32))
        w_down = ctx.enter_context(nc.sbuf_tensor("l3_w_down", [P, CHUNKS3, D], F32))
        l3_decode_stage(nc, core, w_up, w_down, *(t[f"l3_{k}"] for k in (
            "up_q", "up_scale", "up_a", "up_b", "down_q", "down_scale", "down_a", "down_b_rank")))
        norm_stage(nc, core)
        l3_ffn_stage(nc, core, "l3_ffn_a", w_up, w_down, t["l3_bias_up"], t["l3_bias_down"])
        norm_stage(nc, core)
        l3_attention(nc, core, t["l3_qkv"], t["angles"], t["head_rows"], t["l3_window"], t["l3_pool"], t["l3_wo"])
        norm_stage(nc, core)
        l3_ffn_stage(nc, core, "l3_ffn_b", w_up, w_down, t["l3_bias_up"], t["l3_bias_down"])
        end_stage(nc, core, out)


def kernel(**inputs):
    import numpy as np
    import concourse.bacc as bacc
    from concourse.bass_utils import run_bass_kernel_spmd

    def arr(name):
        return np.asarray(inputs[name])

    def in_units(gate, up, units, f):
        g = gate.reshape(KC, P, units, f)
        u = up.reshape(KC, P, units, f)
        return np.stack([g, u], axis=3).transpose(2, 1, 0, 3, 4)

    a = {
        "x": arr("L0_attn_x").reshape(TOKENS, D),
        "lut": arr("L0_ffn_lut"),
        "l0_in_idx": in_units(arr("L0_ffn_gate_idx").T, arr("L0_ffn_up_idx").T, UNITS0, F0)
        .reshape(UNITS0, P, KC * 2 * F0),
        "l0_out_idx": arr("L0_ffn_down_idx").T.reshape(UNITS0, F0, D),
    }
    inv = (1.0 / np.float32(10000.0) ** (np.arange(0, HEAD, 2, dtype=np.float32) / HEAD)).astype(np.float32)
    theta = np.arange(SEQ, dtype=np.float32)[:, None] * inv[None, :]
    a["angles"] = np.stack([np.cos(theta), np.sin(theta)], 1).astype(np.float32).reshape(2, P, 2, HALF_HEAD)\
        .transpose(1, 0, 2, 3)
    a["head_rows"] = np.kron(np.eye(P // HEAD), np.ones((HEAD, 1))).astype(np.float32)
    a["l0_qkv"] = arr("L0_attn_w_qkv")
    a["l0_scale"], a["l0_bias"] = arr("L0_attn_ln_scale"), arr("L0_attn_ln_bias")
    a["l0_wo"] = arr("L0_attn_w_out")
    def expert_units(w):
        return w.reshape(8, KC, P, 2, F1).transpose(0, 3, 2, 1, 4).reshape(16, P, KC, F1)

    def shared_units(w, n, f):
        return w.reshape(KC, P, n, f).transpose(2, 1, 0, 3)

    a["l1_in_w"] = np.stack([
        np.concatenate([expert_units(arr(f"L1_ffn_We_{k}")), shared_units(arr(f"L1_ffn_Ws_{k}"), 4, F1)])
        for k in ("gate", "up")], axis=3)
    a["l1_out_w"] = np.concatenate([arr("L1_ffn_We_down").reshape(16, F1, D),
                                    arr("L1_ffn_Ws_down").reshape(4, F1, D)])
    a["l1_router"] = arr("L1_ffn_W_router")
    order = np.concatenate([np.arange(DH1 - ROPE1), DH1 - ROPE1 + np.arange(0, ROPE1, 2),
                            DH1 - ROPE1 + np.arange(1, ROPE1, 2)])
    wq = arr("L1_attn_wq_w").reshape(HEADS1, DH1, KC, P)[:, order]
    a["l1_wq"] = wq.transpose(0, 3, 2, 1)
    wkv = arr("L1_attn_wkv_b_w").reshape(2, HEADS1, DH1, LATENT)
    a["l1_wkv"] = np.concatenate([wkv[0][:, order], wkv[1]], axis=1).transpose(0, 2, 1)
    freqs = arr("L1_attn_freqs")[:HEADS1]
    one = np.ones((HEADS1, DH1 - ROPE1), np.float32)
    a["l1_columns"] = np.stack([arr("L1_attn_wq_b").reshape(HEADS1, DH1)[:, order]] +
                               [np.concatenate([one, freqs[:, :, k], freqs[:, :, k]], axis=1) for k in (0, 1)],
                               axis=2)
    a["l1_sign"] = np.concatenate([np.ones(P - ROPE1 // 2), -np.ones(ROPE1 // 2)]).astype(np.float32)[:, None]
    a["l1_wkv_a"] = arr("L1_attn_wkv_a_w").T
    a["l1_norm_w"] = arr("L1_attn_norm_w")
    a["l1_wo"] = arr("L1_attn_out_w").T.reshape(HEADS1, P, D)
    a["l1_bo"] = arr("L1_attn_out_b")
    a["l2_in_w"] = arr("L2_ffn_gate_up_proj").reshape(EXPERTS2, KC, P, 2, F2).transpose(0, 2, 1, 3, 4)
    a["l2_out_w"] = arr("L2_ffn_down_proj")
    a["l2_shared_in_w"] = np.stack([shared_units(arr(f"L2_ffn_shared_{k}_w").T, SHARED2, F2)
                                    for k in ("gate", "up")], axis=3)
    a["l2_shared_out_w"] = arr("L2_ffn_shared_down_w").T.reshape(SHARED2, F2, D)
    a["l2_router"] = arr("L2_ffn_gate_w").T
    a["l2_w_gates"] = np.concatenate([arr("L2_attn_Wa"), arr("L2_attn_Wb")], axis=1)
    a["l2_b_gates"] = np.concatenate([arr("L2_attn_ba"), arr("L2_attn_bb")])
    a["l2_w_heads"] = np.stack([arr(f"L2_attn_W{k}").reshape(KC, P, HEADS2, DH2) for k in "qkvg"])\
        .transpose(3, 2, 0, 1, 4)
    a["l2_conv"] = np.stack([
        np.concatenate([arr(f"L2_attn_{k}cw"), arr(f"L2_attn_{k}cb")[:, None]], axis=1)
        .reshape(HEADS2, DH2, TAPS + 1) for k in "qkv"], axis=2)
    a["l2_ln_w"], a["l2_ln_b"] = arr("L2_attn_ln_w"), arr("L2_attn_ln_b")
    a["l2_wo"] = arr("L2_attn_Wo").reshape(HEADS2, P, D)
    a["l3_up_q"] = arr("L3_ffn_w_up_q").T
    a["l3_up_scale"] = arr("L3_ffn_w_up_scale").T
    a["l3_up_a"] = arr("L3_ffn_w_up_lora_a").T
    a["l3_up_b"] = arr("L3_ffn_w_up_lora_b")
    a["l3_down_q"] = arr("L3_ffn_w_down_q").T
    a["l3_down_scale"] = arr("L3_ffn_w_down_scale").T
    a["l3_down_a"] = arr("L3_ffn_w_down_lora_a").T
    a["l3_down_b_rank"] = arr("L3_ffn_w_down_lora_b")
    a["l3_bias_up"] = arr("L3_ffn_b_up").reshape(CHUNKS3, P).T
    a["l3_bias_down"] = arr("L3_ffn_b_down")
    halves = np.concatenate([np.arange(0, HEAD, 2), np.arange(1, HEAD, 2)])
    a["l3_qkv"] = np.concatenate([
        arr("L3_attn_wq").reshape(D, HEADS, HEAD)[:, :, halves].reshape(D, D),
        arr("L3_attn_wk").reshape(D, KV3, HEAD)[:, :, halves].reshape(D, KV3 * HEAD),
        arr("L3_attn_wv")], axis=1)
    a["l3_pool"] = np.stack([arr("L3_attn_cwa")[halves], arr("L3_attn_cwb")[halves]])
    a["l3_wo"] = arr("L3_attn_wo")
    token, blocks = np.arange(P)[:, None, None], np.arange(P)[None, None, :] % BLOCKS3
    a["l3_window"] = (blocks == token // WIN + PER3 * np.arange(2)[None, :, None]).astype(np.float32)
    nc = bacc.Bacc("TRN2", target_bir_lowering=False, num_devices=1)
    arrays, t = {}, {}
    for name, v in a.items():
        v = np.ascontiguousarray(v)
        arrays[f"in_{name}"] = v
        t[name] = nc.dram_tensor(f"in_{name}", v.shape, mybir.dt.from_np(v.dtype), kind="ExternalInput").ap()
    for name, shape in (("l0_in_w", [UNITS0, P, KC, 2, F0]), ("l0_out_w", [UNITS0, F0, D]),
                        ("l2_table", [P, HEADS2, COLUMNS, TILES])):
        t[name] = nc.dram_tensor(name, shape, F32, kind="Internal").ap()
    out = nc.dram_tensor("out", [TOKENS, D], F32, kind="ExternalOutput").ap()
    build(nc, t, out)
    r = run_bass_kernel_spmd(nc, [arrays], core_ids=[0])
    return np.asarray(r.results[0]["out"]).reshape(BATCH, SEQ, D)
```

```python
from contextlib import ExitStack

import concourse.bass as bass
from concourse import mybir

ALU = mybir.AluOpType
ACT = mybir.ActivationFunctionType
F32 = mybir.dt.float32
I32 = mybir.dt.int32
BF16 = mybir.dt.bfloat16
AX_X = mybir.AxisListType.X

P = 128
BATCH, SEQ, D = 4, 256, 256
TOKENS = BATCH * SEQ
TILES = TOKENS // P
KC = D // P
HALF = 512
HALVES = TOKENS // HALF
NORM_EPS = 1e-5


class Stage:

    def __init__(self, nc, name):
        self.nc, self.name, self.ctx, self.sems = nc, name, ExitStack(), []
        self.seen = nc.next_id()

    def __enter__(self):
        return self

    def sb(self, name, shape, dt=F32):
        return self.ctx.enter_context(self.nc.sbuf_tensor(f"{self.name}_{name}_{self.seen}", shape, dt))

    def ps(self, name, shape, dt=F32):
        return self.ctx.enter_context(self.nc.psum_tensor(f"{self.name}_{name}_{self.seen}", shape, dt))

    def sem(self, name):
        s = self.nc.alloc_semaphore(f"{self.name}_{name}_{self.seen}")
        self.sems.append(s)
        return s

    def block(self):
        self.blocks = ExitStack()
        return self.blocks.enter_context(self.nc.Block())

    def __exit__(self, *failed):
        if failed[0] is None:
            self.blocks.close()
            self.nc.clear_and_free_semaphores(self.sems)
            self.nc.all_engine_barrier()
            self.ctx.close()


class Core:

    def __init__(self, nc, ctx):
        def sb(name, shape, dt=F32):
            return ctx.enter_context(nc.sbuf_tensor(name, shape, dt))

        self.x = sb("x", [P, TILES, D])
        self.xnT = sb("xnT", [P, KC, TOKENS])
        self.ident = sb("ident", [P, P])
        self.ident_bf16 = sb("ident_bf16", [P, P], BF16)
        self.ones = sb("ones", [P, P])
        self.before = sb("before", [P, P])
        self.upto = sb("upto", [P, P])
        self.after = sb("after", [P, P])
        self.norm_eps = sb("norm_eps", [P, 1])
        self.half_col = sb("half_col", [P, 1])


def start_stage(nc, core, x_in):
    with Stage(nc, "start") as st:
        loaded = st.sem("loaded")
        filled = st.sem("filled")
        shaped = st.sem("shaped")
        block = st.block()

        @block.sync
        def _(sp):
            sp.dma_start(core.x[:], x_in.rearrange("(t p) d -> p t d", p=P)).then_inc(loaded, 16)
            sp.wait_ge(loaded, 16)

        @block.gpsimd
        def _(pool):
            pool.memset(core.ident[:], 0.0).then_inc(filled, 1)
            for m in (core.ones, core.before, core.upto, core.after):
                pool.memset(m[:], 1.0).then_inc(filled, 1)
            pool.memset(core.norm_eps[:], NORM_EPS).then_inc(filled, 1)
            pool.memset(core.half_col[:], 0.5).then_inc(filled, 1)
            pool.wait_ge(filled, 7)
            pool.affine_select(out=core.ident[:], in_=core.ident[:], compare_op=ALU.not_equal, fill=1.0,
                               base=0, pattern=[[-1, P]], channel_multiplier=1).then_inc(shaped, 1)
            pool.affine_select(out=core.before[:], in_=core.before[:], compare_op=ALU.is_gt, fill=0.0,
                               base=0, pattern=[[1, P]], channel_multiplier=-1).then_inc(shaped, 1)
            pool.affine_select(out=core.upto[:], in_=core.upto[:], compare_op=ALU.is_ge, fill=0.0,
                               base=0, pattern=[[1, P]], channel_multiplier=-1).then_inc(shaped, 1)
            pool.affine_select(out=core.after[:], in_=core.after[:], compare_op=ALU.is_gt, fill=0.0,
                               base=0, pattern=[[-1, P]], channel_multiplier=1).then_inc(shaped, 1)
            pool.wait_ge(shaped, 4)
            pool.tensor_copy(core.ident_bf16[:], core.ident[:])


def end_stage(nc, core, out):
    with Stage(nc, "end") as st:
        stored = st.sem("stored")
        block = st.block()

        @block.sync
        def _(sp):
            sp.dma_start(out.rearrange("(t p) d -> p t d", p=P), core.x[:]).then_inc(stored, 16)
            sp.wait_ge(stored, 16)


def norm_stage(nc, core, kept=None):
    with Stage(nc, "norm") as st:
        stats = st.sb("stats", [P, TILES, 6])
        mean_var = st.sb("mean_var", [P, TILES, 2])
        sd = st.sb("sd", [P, TILES])
        rstd = st.sb("rstd", [P, TILES])
        xn = st.sb("xn", [P, TILES, D]) if kept is None else kept
        turn = st.ps("turn", [P, KC, HALVES, HALF])
        stats_done = st.sem("stats_done")
        mean_var_done = st.sem("mean_var_done")
        sd_done = st.sem("sd_done")
        rstd_done = st.sem("rstd_done")
        xn_ready = st.sem("xn_ready")
        turned = st.sem("turned")
        per_half = TILES // HALVES
        block = st.block()

        @block.vector
        def _(dve):
            for t in range(TILES):
                dve.bn_stats(stats[:, t, :], core.x[:, t, :]).then_inc(stats_done, 1)
            for t in range(TILES):
                dve.wait_ge(stats_done, t + 1)
                dve.bn_aggr(mean_var[:, t, :], stats[:, t, :]).then_inc(mean_var_done, 1)
            dve.wait_ge(sd_done, 1)
            dve.reciprocal(rstd[:], sd[:]).then_inc(rstd_done, 1)
            dve.wait_ge(rstd_done, 1)
            for t in range(TILES):
                dve.tensor_scalar(xn[:, t, :], core.x[:, t, :], mean_var[:, t, 0:1], rstd[:, t:t + 1],
                                  ALU.subtract, ALU.mult).then_inc(xn_ready, 1)
            for h in range(HALVES):
                dve.wait_ge(turned, KC * per_half * (h + 1))
                dve.tensor_copy(core.xnT[:, 1, h * HALF:(h + 1) * HALF], turn[:, 1, h, :])

        @block.scalar
        def _(act):
            act.wait_ge(mean_var_done, TILES)
            act.activation(sd[:], mean_var[:, :, 1], ACT.Sqrt, bias=core.norm_eps[:]).then_inc(sd_done, 1)
            for h in range(HALVES):
                act.wait_ge(turned, KC * per_half * (h + 1))
                act.copy(core.xnT[:, 0, h * HALF:(h + 1) * HALF], turn[:, 0, h, :])

        @block.tensor
        def _(pe):
            for t in range(TILES):
                pe.wait_ge(xn_ready, t + 1)
                for c in range(KC):
                    pe.transpose(turn[:, c, t // per_half, (t % per_half) * P:(t % per_half + 1) * P],
                                 xn[:, t, c * P:(c + 1) * P], core.ident[:]).then_inc(turned, 1)


def gated_units_stage(nc, core, name, F, units, in_weights, out_weights):
    with Stage(nc, name) as st:
        w_in = [st.sb(f"w_in{b}", [P, KC, 2, F]) for b in range(2)]
        w_out = [st.sb(f"w_out{b}", [F, D]) for b in range(2)]
        gate = [st.sb(f"gate{h}", [F, HALF]) for h in range(HALVES)]
        hidden = [st.sb(f"hidden{b}", [F, TOKENS]) for b in range(2)]
        ps_gate = [st.ps(f"ps_gate{h}", [P, HALF]) for h in range(HALVES)]
        ps_up = [st.ps(f"ps_up{h}", [P, HALF]) for h in range(HALVES)]
        BANKS, PER = 4, TILES // 4
        ps_down = [st.ps(f"ps_down{q}", [P, PER, D]) for q in range(BANKS)]
        in_loaded = [st.sem(f"in_loaded{b}") for b in range(2)]
        out_loaded = [st.sem(f"out_loaded{b}") for b in range(2)]
        up_done = st.sem("up_done")
        silu_done = st.sem("silu_done")
        hidden_ready = st.sem("hidden_ready")
        down_bank = st.sem("down_bank")
        added = st.sem("added")
        block = st.block()
        pairs = units // 2

        def over_pairs(eng, unit, lead):
            unit(0, 0, True)
            unit(1, 1, lead == 0)
            if pairs > 1:
                with eng.Fori(1, pairs) as i:
                    unit(2 * i, 0, False)
                    unit(2 * i + 1, 1, False)

        @block.sync
        def _(sp):
            def load(u, b, first):
                if not first:
                    sp.wait_ge(up_done, HALVES * (u - 1))
                sp.dma_start(w_in[b][:], in_weights[bass.ds(u, 1)].rearrange("a p c g f -> (a p) c g f"))\
                    .then_inc(in_loaded[b], 16)
                if not first:
                    sp.wait_ge(down_bank, BANKS * (u - 1))
                sp.dma_start(w_out[b][:], out_weights[bass.ds(u, 1)].rearrange("a f d -> (a f) d"))\
                    .then_inc(out_loaded[b], 16)

            over_pairs(sp, load, 0)

        @block.tensor
        def _(pe):
            def up(u, i, b, first):
                pe.wait_ge(in_loaded[b], 16 * (i + 1))
                for h in range(HALVES):
                    if not first:
                        pe.wait_ge(hidden_ready, 2 * (u - 1) + h + 1)
                    for g, bank in ((0, ps_gate[h]), (1, ps_up[h])):
                        for c in range(KC):
                            mm = pe.matmul(bank[0:F, :], w_in[b][:, c, g, :],
                                           core.xnT[:, c, h * HALF:(h + 1) * HALF],
                                           start=(c == 0), stop=(c == KC - 1))
                    mm.then_inc(up_done, 1)

            def down(u, i, b, first):
                pe.wait_ge(out_loaded[b], 16 * (i + 1))
                pe.wait_ge(hidden_ready, 2 * u + 2)
                for q in range(BANKS):
                    if not first:
                        pe.wait_ge(added, BANKS * (u - 1) + q + 1)
                    for r in range(PER):
                        t = q * PER + r
                        mm = pe.matmul(ps_down[q][:, r, :], hidden[b][:, t * P:(t + 1) * P], w_out[b][:],
                                       start=True, stop=True)
                    mm.then_inc(down_bank, 1)

            up(0, 0, 0, True)
            up(1, 0, 1, False)
            down(0, 0, 0, True)
            if pairs > 1:
                with pe.Fori(1, pairs) as i:
                    up(2 * i, i, 0, False)
                    down(2 * i - 1, i - 1, 1, False)
                    up(2 * i + 1, i, 1, False)
                    down(2 * i, i, 0, False)
            down(units - 1, pairs - 1, 1, False)

        @block.scalar
        def _(act):
            def silu(u, b, first):
                for h in range(HALVES):
                    act.wait_ge(up_done, 2 * u + h + 1)
                    if not first:
                        act.wait_ge(hidden_ready, 2 * (u - 1) + h + 1)
                    act.activation(gate[h][:], ps_gate[h][0:F, :], ACT.Silu).then_inc(silu_done, 1)

            over_pairs(act, silu, 1)

        @block.vector
        def _(dve):
            def mix(u, b, first):
                if not first:
                    dve.wait_ge(down_bank, BANKS * (u - 1))
                for h in range(HALVES):
                    dve.wait_ge(silu_done, 2 * u + h + 1)
                    dve.tensor_tensor(hidden[b][:, h * HALF:(h + 1) * HALF], gate[h][:], ps_up[h][0:F, :],
                                      ALU.mult).then_inc(hidden_ready, 1)

            def add(u, b, first):
                for q in range(BANKS):
                    dve.wait_ge(down_bank, BANKS * u + q + 1)
                    if not first:
                        dve.wait_ge(added, BANKS * (u - 1) + q + 1)
                    dve.scalar_tensor_tensor(
                        out=core.x[:, q * PER:(q + 1) * PER, :], in0=ps_down[q][:], scalar=0.5,
                        in1=core.x[:, q * PER:(q + 1) * PER, :], op0=ALU.mult, op1=ALU.add).then_inc(added, 1)

            mix(0, 0, True)
            mix(1, 1, True)
            add(0, 0, True)
            if pairs > 1:
                with dve.Fori(1, pairs) as i:
                    mix(2 * i, 0, False)
                    add(2 * i - 1, 1, False)
                    mix(2 * i + 1, 1, False)
                    add(2 * i, 0, False)
            add(units - 1, 1, False)


def weighted_units_stage(nc, core, name, F, units, in_weights, out_weights, owners, weight_rows, select):
    ROWS = 3 * owners
    with Stage(nc, name) as st:
        w_in = [st.sb(f"w_in{b}", [P, KC, 2, F]) for b in range(2)]
        w_out = [st.sb(f"w_out{b}", [F, D]) for b in range(2)]
        select_f32 = st.sb("select_f32", [ROWS, units, F])
        chooser = st.sb("chooser", [P, units, F], BF16)
        gate = [st.sb(f"gate{h}", [F, HALF]) for h in range(HALVES)]
        mixed = [st.sb(f"mixed{h}", [F, HALF]) for h in range(HALVES)]
        hidden = [st.sb(f"hidden{b}", [F, TOKENS]) for b in range(2)]
        ps_gate = [st.ps(f"ps_gate{h}", [P, HALF]) for h in range(HALVES)]
        ps_up = [st.ps(f"ps_up{h}", [P, HALF]) for h in range(HALVES)]
        ps_down = [[st.ps(f"ps_down{c}{h}", [P, HALF]) for h in range(HALVES)] for c in range(KC)]
        sums = st.sb("sums", [P, KC, TOKENS])
        select_loaded = st.sem("select_loaded")
        chooser_ready = st.sem("chooser_ready")
        cleared = st.sem("cleared")
        sums_ready = [st.sem(f"sums_ready{c}") for c in range(KC)]
        turned = st.sem("turned")
        in_loaded = [st.sem(f"in_loaded{b}") for b in range(2)]
        out_loaded = [st.sem(f"out_loaded{b}") for b in range(2)]
        up_done = st.sem("up_done")
        silu_done = st.sem("silu_done")
        mixed_ready = st.sem("mixed_ready")
        spread_done = st.sem("spread_done")
        hidden_ready = st.sem("hidden_ready")
        down_done = st.sem("down_done")
        block = st.block()
        pairs = units // 2

        def over_units(eng, unit):
            unit(0, 0, 0, True)
            unit(1, 0, 1, False)
            with eng.Fori(1, pairs) as i:
                unit(2 * i, i, 0, False)
                unit(2 * i + 1, i, 1, False)

        @block.sync
        def _(sp):
            def load(u, b, first):
                if not first:
                    sp.wait_ge(up_done, HALVES * (u - 1))
                sp.dma_start(w_in[b][:], in_weights[bass.ds(u, 1)].rearrange("a p c g f -> (a p) c g f"))\
                    .then_inc(in_loaded[b], 16)
                if not first:
                    sp.wait_ge(down_done, u - 1)
                sp.dma_start(w_out[b][:], out_weights[bass.ds(u, 1)].rearrange("a f d -> (a f) d"))\
                    .then_inc(out_loaded[b], 16)

            load(0, 0, True)
            sp.dma_start(select_f32[:], select).then_inc(select_loaded, 16)
            load(1, 1, True)
            with sp.Fori(1, pairs) as i:
                load(2 * i, 0, False)
                load(2 * i + 1, 1, False)

        @block.gpsimd
        def _(pool):
            pool.memset(chooser[:], 0.0).then_inc(cleared, 1)

        @block.tensor
        def _(pe):
            def up(u, i, b, first):
                pe.wait_ge(in_loaded[b], 16 * (i + 1))
                for h in range(HALVES):
                    if not first:
                        pe.wait_ge(hidden_ready, 2 * (u - 1) + h + 1)
                    for g, bank in ((0, ps_gate[h]), (1, ps_up[h])):
                        for c in range(KC):
                            mm = pe.matmul(bank[0:F, :], w_in[b][:, c, g, :],
                                           core.xnT[:, c, h * HALF:(h + 1) * HALF],
                                           start=(c == 0), stop=(c == KC - 1))
                    mm.then_inc(up_done, 1)

            def spread(u, h):
                pe.wait_ge(silu_done, 2 * u + h + 1)
                pe.matmul(ps_gate[h][0:F, :], chooser[:, bass.ds(u, 1), :].rearrange("k a f -> k (a f)"),
                          weight_rows[:, h * HALF:(h + 1) * HALF], start=True, stop=True).then_inc(spread_done, 1)

            def down(u, i, b, h, last):
                pe.wait_ge(out_loaded[b], 16 * (i + 1))
                pe.wait_ge(hidden_ready, 2 * u + h + 1)
                for c in range(KC):
                    mm = pe.matmul(ps_down[c][h][:], w_out[b][:, c * P:(c + 1) * P],
                                   hidden[b][:, h * HALF:(h + 1) * HALF],
                                   start=(isinstance(u, int) and u == 0), stop=last)
                if last or h == 1:
                    mm.then_inc(down_done, 1)

            def step(u, i, b, first):
                up(u, i, b, first)
                if first:
                    pe.wait_ge(chooser_ready, 1)
                spread(u, 0)
                if not first:
                    down(u - 1, i - 1 + b, 1 - b, 0, False)
                spread(u, 1)
                if not first:
                    down(u - 1, i - 1 + b, 1 - b, 1, False)

            over_units(pe, step)
            for h in range(HALVES):
                down(units - 1, pairs - 1, 1, h, True)
            pe.wait_ge(hidden_ready, 2 * units)
            banks = (ps_gate[0], ps_up[0], ps_gate[1], ps_up[1])
            for q, bank in enumerate(banks):
                for c in range(KC):
                    pe.wait_ge(sums_ready[c], q // 2 + 1)
                for r in range(2):
                    t = 2 * q + r
                    for c in range(KC):
                        tr = pe.transpose(bank[:, (r * KC + c) * P:(r * KC + c + 1) * P],
                                          sums[:, c, t * P:(t + 1) * P], core.ident[:])
                tr.then_inc(turned, 1)

        @block.scalar
        def _(act):
            act.wait_ge(select_loaded, 16)
            act.wait_ge(cleared, 1)
            act.copy(chooser[0:ROWS], select_f32[:]).then_inc(chooser_ready, 1)

            def silu(u, i, b, first):
                for h in range(HALVES):
                    act.wait_ge(up_done, 2 * u + h + 1)
                    if not first:
                        act.wait_ge(mixed_ready, 2 * (u - 1) + h + 1)
                    act.activation(gate[h][:], ps_gate[h][0:F, :], ACT.Silu).then_inc(silu_done, 1)

            over_units(act, silu)
            for h in range(HALVES):
                act.wait_ge(down_done, units + h)
                act.copy(sums[:, 0, h * HALF:(h + 1) * HALF], ps_down[0][h][:]).then_inc(sums_ready[0], 1)

        @block.vector
        def _(dve):
            def mix(u, i, b, first):
                for h in range(HALVES):
                    dve.wait_ge(silu_done, 2 * u + h + 1)
                    if not first:
                        dve.wait_ge(hidden_ready, 2 * (u - 1) + h + 1)
                    dve.tensor_tensor(mixed[h][:], gate[h][:], ps_up[h][0:F, :], ALU.mult).then_inc(mixed_ready, 1)
                for h in range(HALVES):
                    dve.wait_ge(mixed_ready, 2 * u + h + 1)
                    dve.wait_ge(spread_done, 2 * u + h + 1)
                    if not (isinstance(u, int) and u < 2):
                        dve.wait_ge(down_done, u - 1)
                    dve.tensor_tensor(hidden[b][:, h * HALF:(h + 1) * HALF], mixed[h][:], ps_gate[h][0:F, :],
                                      ALU.mult).then_inc(hidden_ready, 1)

            over_units(dve, mix)
            for h in range(HALVES):
                dve.wait_ge(down_done, units + h)
                dve.tensor_copy(sums[:, 1, h * HALF:(h + 1) * HALF], ps_down[1][h][:]).then_inc(sums_ready[1], 1)
            for q, bank in enumerate((ps_gate[0], ps_up[0], ps_gate[1], ps_up[1])):
                dve.wait_ge(turned, q + 1)
                part = core.x[:, 2 * q:2 * q + 2, :].rearrange("p t d -> p (t d)")
                dve.tensor_tensor(part, part, bank[:], ALU.add)


LUT = 16
INTER0 = 688
F0, UNITS0 = 115, 6
NO_ENTRY = LUT


IN0 = KC * 2 * F0


def l0_ffn_stage(nc, core, name, w, source=None):
    N = IN0 + D
    OWN = 7
    OTHER = LUT - OWN
    SLOTS = 4
    with Stage(nc, name) as st:
        gate = [st.sb(f"gate{h}", [F0, HALF]) for h in range(HALVES)]
        hidden = [st.sb(f"hidden{b}", [F0, TOKENS]) for b in range(2)]
        sums = st.sb("sums", [P, KC, TOKENS])
        ps_gate = [st.ps(f"ps_gate{h}", [P, HALF]) for h in range(HALVES)]
        ps_up = [st.ps(f"ps_up{h}", [P, HALF]) for h in range(HALVES)]
        ps_down = [[st.ps(f"ps_down{c}{h}", [P, HALF]) for h in range(HALVES)] for c in range(KC)]
        turn_banks = (ps_gate[0], ps_up[0], ps_gate[1], ps_up[1])
        up_done = st.sem("up_done")
        silu_done = st.sem("silu_done")
        hidden_ready = st.sem("hidden_ready")
        down_done = st.sem("down_done")
        sums_ready = [st.sem(f"sums_ready{c}") for c in range(KC)]
        turned = st.sem("turned")
        if source is not None:
            lut, in_idx, out_idx = source
            table = st.sb("table", [P, LUT])
            idx = st.sb("idx", [P, UNITS0, N], I32)
            term = [st.sb(f"term{b}", [P, N]) for b in range(2)]
            other_term = [st.sb(f"other_term{b}", [P, N]) for b in range(SLOTS)]
            other_sum = [st.sb(f"other_sum{b}", [P, N]) for b in range(2)]
            zeroed = st.sem("zeroed")
            table_loaded = st.sem("table_loaded")
            idx_loaded = [st.sem(f"idx_loaded{u}") for u in range(UNITS0)]
            term_done = st.sem("term_done")
            other_term_done = st.sem("other_term_done")
            other_added = st.sem("other_added")
            w_done = st.sem("w_done")
        block = st.block()

        if source is not None:
            @block.sync
            def _(sp):
                sp.dma_start(table[:], lut.partition_broadcast(P)).then_inc(table_loaded, 16)
                sp.wait_ge(zeroed, 1)
                for u in range(UNITS0):
                    sp.dma_start(idx[:, u, 0:IN0], in_idx[u]).then_inc(idx_loaded[u], 16)
                    sp.dma_start(idx[0:F0, u, IN0:N], out_idx[u]).then_inc(idx_loaded[u], 16)

            @block.gpsimd
            def _(pool):
                pool.memset(idx[64:P, :, IN0:N], 0).then_inc(zeroed, 1)
                for u in range(UNITS0):
                    total = other_sum[u % 2]
                    for k in range(1, OTHER):
                        n = u * OTHER + k
                        pool.wait_ge(other_term_done, n + 1)
                        if k == 1 and u >= 2:
                            pool.wait_ge(w_done, (OWN + 1) * (u - 1))
                        if k > 1:
                            pool.wait_ge(other_added, u * (OTHER - 1) + k - 1)
                        before = other_term[(n - 1) % SLOTS] if k == 1 else total
                        pool.tensor_tensor(total[:], before[:], other_term[n % SLOTS][:], ALU.add)\
                            .then_inc(other_added, 1)

        @block.tensor
        def _(pe):
            def up(u):
                if source is not None:
                    pe.wait_ge(w_done, (OWN + 1) * (u + 1))
                for h in range(HALVES):
                    if u > 0:
                        pe.wait_ge(hidden_ready, 2 * (u - 1) + h + 1)
                    for g, bank in ((0, ps_gate[h]), (1, ps_up[h])):
                        for c in range(KC):
                            at = (2 * c + g) * F0
                            mm = pe.matmul(bank[0:F0, :], w[:, u, at:at + F0],
                                           core.xnT[:, c, h * HALF:(h + 1) * HALF],
                                           start=(c == 0), stop=(c == KC - 1))
                    mm.then_inc(up_done, 1)

            def down(u):
                for h in range(HALVES):
                    pe.wait_ge(hidden_ready, 2 * u + h + 1)
                    for c in range(KC):
                        mm = pe.matmul(ps_down[c][h][:], w[0:F0, u, IN0 + c * P:IN0 + (c + 1) * P],
                                       hidden[u % 2][:, h * HALF:(h + 1) * HALF],
                                       start=(u == 0), stop=(u == UNITS0 - 1))
                    if h == 1 or u == UNITS0 - 1:
                        mm.then_inc(down_done, 1)

            up(0)
            for u in range(1, UNITS0):
                up(u)
                down(u - 1)
            down(UNITS0 - 1)
            pe.wait_ge(hidden_ready, 2 * UNITS0)
            for q, bank in enumerate(turn_banks):
                for c in range(KC):
                    pe.wait_ge(sums_ready[c], q // 2 + 1)
                for r in range(2):
                    t = 2 * q + r
                    for c in range(KC):
                        tr = pe.transpose(bank[:, (r * KC + c) * P:(r * KC + c + 1) * P],
                                          sums[:, c, t * P:(t + 1) * P], core.ident[:])
                tr.then_inc(turned, 1)

        @block.scalar
        def _(act):
            for u in range(UNITS0):
                for h in range(HALVES):
                    act.wait_ge(up_done, 2 * u + h + 1)
                    if u > 0:
                        act.wait_ge(hidden_ready, 2 * (u - 1) + h + 1)
                    act.activation(gate[h][:], ps_gate[h][0:F0, :], ACT.Silu).then_inc(silu_done, 1)
            for h in range(HALVES):
                act.wait_ge(down_done, UNITS0 + h)
                act.copy(sums[:, 0, h * HALF:(h + 1) * HALF], ps_down[0][h][:]).then_inc(sums_ready[0], 1)

        @block.vector
        def _(dve):
            def make_term(u, j, out):
                return dve.tensor_scalar(out, idx[:, u, :], float(j), table[:, j:j + 1], ALU.is_equal, ALU.mult)

            def other(u, k):
                n = u * OTHER + k
                if n >= SLOTS:
                    before = n - SLOTS
                    dve.wait_ge(other_added, before // OTHER * (OTHER - 1) + max(before % OTHER, 1))
                make_term(u, OWN + k, other_term[n % SLOTS][:]).then_inc(other_term_done, 1)

            def finish(u):
                dve.wait_ge(other_added, (OTHER - 1) * (u + 1))
                dve.wait_ge(w_done, (OWN + 1) * u + OWN)
                dve.tensor_tensor(w[:, u, :], w[:, u, :], other_sum[u % 2][:], ALU.add).then_inc(w_done, 1)

            def make_terms(u):
                dve.wait_ge(idx_loaded[u], 32)
                other(u, 0)
                other(u, 1)
                if u > 0:
                    finish(u - 1)
                make_term(u, 0, w[:, u, :]).then_inc(w_done, 1)
                for j in range(1, OWN):
                    n = u * (OWN - 1) + j - 1
                    if j > 2:
                        dve.wait_ge(w_done, u * (OWN + 1) + j - 1)
                    make_term(u, j, term[n % 2][:]).then_inc(term_done, 1)
                    other(u, 1 + j)
                    dve.wait_ge(term_done, n + 1)
                    dve.wait_ge(w_done, u * (OWN + 1) + j)
                    dve.tensor_tensor(w[:, u, :], w[:, u, :], term[n % 2][:], ALU.add).then_inc(w_done, 1)
                for k in range(1 + OWN, OTHER):
                    other(u, k)

            def mix(u):
                for h in range(HALVES):
                    dve.wait_ge(silu_done, 2 * u + h + 1)
                    if u >= 2:
                        dve.wait_ge(down_done, u - 1)
                    dve.tensor_tensor(hidden[u % 2][:, h * HALF:(h + 1) * HALF], gate[h][:], ps_up[h][0:F0, :],
                                      ALU.mult).then_inc(hidden_ready, 1)

            if source is not None:
                dve.wait_ge(table_loaded, 16)
                make_terms(0)
                make_terms(1)
            for u in range(UNITS0):
                if source is not None and u + 2 < UNITS0:
                    make_terms(u + 2)
                if source is not None and u + 2 == UNITS0:
                    finish(UNITS0 - 1)
                mix(u)
            for h in range(HALVES):
                dve.wait_ge(down_done, UNITS0 + h)
                dve.tensor_copy(sums[:, 1, h * HALF:(h + 1) * HALF], ps_down[1][h][:]).then_inc(sums_ready[1], 1)
            for q, bank in enumerate(turn_banks):
                dve.wait_ge(turned, q + 1)
                part = core.x[:, 2 * q:2 * q + 2, :].rearrange("p t d -> p (t d)")
                dve.scalar_tensor_tensor(out=part, in0=bank[:], scalar=0.5, in1=part, op0=ALU.mult, op1=ALU.add)


HEAD = 16
HALF_HEAD = HEAD // 2
HEADS = D // HEAD


def rope_qkv_stage(nc, core, name, weights, angles, heads, qk, v_cols, v_view):
    N = heads * HEAD
    with Stage(nc, name) as st:
        w = st.sb("w", [P, KC, N + v_cols])
        angle = st.sb("angle", [P, 2, 2, HALF_HEAD])
        raw = [st.sb(f"raw{b}", [P, N]) for b in range(2)]
        by_cos = [st.sb(f"by_cos{b}", [P, N]) for b in range(2)]
        by_sin = [st.sb(f"by_sin{b}", [P, N]) for b in range(2)]
        ps_qk = [st.ps(f"ps_qk{b}", [P, HALF]) for b in range(2)]
        ps_v = [st.ps(f"ps_v{b}", [P, HALF]) for b in range(2)]
        loaded = st.sem("loaded")
        projected = st.sem("projected")
        raw_ready = st.sem("raw_ready")
        v_ready = st.sem("v_ready")
        cos_ready = st.sem("cos_ready")
        sin_ready = st.sem("sin_ready")
        turned = st.sem("turned")
        block = st.block()

        def pairs(ap):
            return ap.rearrange("p (h e j) -> p h e j", e=2, j=HALF_HEAD)

        def factor(t, which):
            return angle[:, t % 2, which, :].unsqueeze(1).broadcast_to([P, heads * 2, HALF_HEAD])

        @block.sync
        def _(sp):
            sp.dma_start(w[:], weights.rearrange("(c p) n -> p c n", p=P)).then_inc(loaded, 16)
            sp.dma_start(angle[:], angles).then_inc(loaded, 16)

        @block.tensor
        def _(pe):
            pe.wait_ge(loaded, 32)
            for t in range(TILES):
                if t >= 2:
                    pe.wait_ge(raw_ready, t - 1)
                    pe.wait_ge(v_ready, t - 1)
                for bank, lo, hi in ((ps_qk[t % 2], 0, N), (ps_v[t % 2], N, N + v_cols)):
                    for c in range(KC):
                        mm = pe.matmul(bank[:, 0:hi - lo], core.xnT[:, c, t * P:(t + 1) * P], w[:, c, lo:hi],
                                       start=(c == 0), stop=(c == KC - 1))
                mm.then_inc(projected, 1)

        @block.scalar
        def _(act):
            for t in range(TILES):
                act.wait_ge(projected, t + 1)
                if t >= 2:
                    act.wait_ge(cos_ready, t - 1)
                    act.wait_ge(sin_ready, t - 1)
                act.copy(raw[t % 2][:], ps_qk[t % 2][:, 0:N]).then_inc(raw_ready, 1)
                width = v_view(t).shape[-1]
                act.copy(v_view(t), ps_v[t % 2][:, 0:v_cols].rearrange("p (h d) -> p h d", d=width))\
                    .then_inc(v_ready, 1)

        @block.gpsimd
        def _(pool):
            pool.wait_ge(loaded, 32)
            for t in range(TILES):
                pool.wait_ge(raw_ready, t + 1)
                if t >= 2:
                    pool.wait_ge(turned, 2 * (t - 1))
                pool.tensor_tensor(by_sin[t % 2][:].rearrange("p (n j) -> p n j", j=HALF_HEAD),
                                   raw[t % 2][:].rearrange("p (n j) -> p n j", j=HALF_HEAD),
                                   factor(t, 1), ALU.mult).then_inc(sin_ready, 1)

        @block.vector
        def _(dve):
            dve.wait_ge(loaded, 32)

            def cosines(t):
                dve.wait_ge(raw_ready, t + 1)
                if t >= 2:
                    dve.wait_ge(turned, 2 * (t - 1))
                dve.tensor_tensor(by_cos[t % 2][:].rearrange("p (n j) -> p n j", j=HALF_HEAD),
                                  raw[t % 2][:].rearrange("p (n j) -> p n j", j=HALF_HEAD),
                                  factor(t, 0), ALU.mult).then_inc(cos_ready, 1)

            def turn(t):
                dve.wait_ge(cos_ready, t + 1)
                dve.wait_ge(sin_ready, t + 1)
                c, s, o = pairs(by_cos[t % 2][:]), pairs(by_sin[t % 2][:]), pairs(qk[:, t, :])
                dve.tensor_tensor(o[:, :, 0, :], c[:, :, 0, :], s[:, :, 1, :], ALU.subtract).then_inc(turned, 1)
                dve.tensor_tensor(o[:, :, 1, :], s[:, :, 0, :], c[:, :, 1, :], ALU.add).then_inc(turned, 1)

            cosines(0)
            for t in range(1, TILES):
                cosines(t)
                turn(t - 1)
            turn(TILES - 1)


def turn_stage(nc, core, name, src, chunks, dst, affine=None):
    with Stage(nc, name) as st:
        columns = st.sb("columns", [P, 2])
        loaded = st.sem("loaded")
        banks = [st.ps(f"bank{b}", [P, 4, P]) for b in range(4)]
        turned = st.sem("turned")
        copied = [st.sem(f"copied{e}") for e in range(2)]
        block = st.block()

        if affine is not None:
            @block.sync
            def _(sp):
                sp.dma_start(columns[:], affine).then_inc(loaded, 16)

        @block.tensor
        def _(pe):
            for t in range(TILES):
                if t >= 4:
                    pe.wait_ge(copied[t % 2], (t - 4) // 2 + 1)
                for c in range(chunks):
                    tr = pe.transpose(banks[t % 4][:, c, :], src[:, t, c * P:(c + 1) * P], core.ident[:])
                tr.then_inc(turned, 1)

        @block.scalar
        def _(act):
            if affine is not None:
                act.wait_ge(loaded, 16)
            for t in range(0, TILES, 2):
                act.wait_ge(turned, t + 1)
                out, bank = dst[:, :, t * P:(t + 1) * P], banks[t % 4][:, 0:chunks, :]
                if affine is None:
                    act.copy(out, bank).then_inc(copied[0], 1)
                else:
                    act.activation(out, bank, ACT.Identity, bias=columns[:, 1:2], scale=columns[:, 0:1])\
                        .then_inc(copied[0], 1)

        @block.vector
        def _(dve):
            if affine is not None:
                dve.wait_ge(loaded, 16)
            for t in range(1, TILES, 2):
                dve.wait_ge(turned, t + 1)
                out, bank = dst[:, :, t * P:(t + 1) * P], banks[t % 4][:, 0:chunks, :]
                if affine is None:
                    dve.tensor_copy(out, bank).then_inc(copied[1], 1)
                else:
                    dve.tensor_scalar(out, bank, columns[:, 0:1], columns[:, 1:2], ALU.mult, ALU.add)\
                        .then_inc(copied[1], 1)


def project_stage(nc, core, name, oT, weights):
    with Stage(nc, name) as st:
        w = st.sb("w", [P, KC, D])
        banks = [st.ps(f"bank{q}", [P, 2, D]) for q in range(4)]
        loaded = st.sem("loaded")
        projected = st.sem("projected")
        block = st.block()

        @block.sync
        def _(sp):
            sp.dma_start(w[:], weights.rearrange("(c p) n -> p c n", p=P)).then_inc(loaded, 16)

        @block.tensor
        def _(pe):
            pe.wait_ge(loaded, 16)
            for t in range(TILES):
                for c in range(KC):
                    mm = pe.matmul(banks[t // 2][:, t % 2, :], oT[:, c, t * P:(t + 1) * P], w[:, c, :],
                                   start=(c == 0), stop=(c == KC - 1))
                mm.then_inc(projected, 1)

        @block.vector
        def _(dve):
            for q in range(4):
                dve.wait_ge(projected, 2 * q + 2)
                dve.tensor_tensor(core.x[:, 2 * q:2 * q + 2, :], core.x[:, 2 * q:2 * q + 2, :],
                                  banks[q][:], ALU.add)


def l0_head_norm_stage(nc, core, qk):
    PER = 2
    STEPS = TILES // PER
    ROWS = PER * 2 * HEADS
    with Stage(nc, "head_norm") as st:
        total = [st.sb(f"total{b}", [P, ROWS]) for b in range(STEPS)]
        squares = [st.sb(f"squares{b}", [P, ROWS, HEAD]) for b in range(2)]
        spread = [st.sb(f"spread{b}", [P, ROWS]) for b in range(STEPS)]
        sd = [st.sb(f"sd{b}", [P, ROWS]) for b in range(STEPS)]
        rstd = [st.sb(f"rstd{b}", [P, ROWS]) for b in range(STEPS)]
        total_ready = st.sem("total_ready")
        mean_ready = st.sem("mean_ready")
        centred = st.sem("centred")
        squared = st.sem("squared")
        spread_ready = st.sem("spread_ready")
        sd_ready = st.sem("sd_ready")
        rstd_ready = st.sem("rstd_ready")
        scaled = st.sem("scaled")
        block = st.block()

        def heads(s):
            return qk[:, s * PER:(s + 1) * PER, :].rearrange("p t (h d) -> p (t h) d", d=HEAD)

        def across(ap):
            return ap.unsqueeze(2).broadcast_to([P, ROWS, HEAD])

        @block.vector
        def _(dve):
            def centre(s):
                dve.tensor_reduce(total[s][:], heads(s), AX_X, ALU.add).then_inc(total_ready, 1)
                dve.wait_ge(total_ready, s + 1)
                dve.tensor_scalar(total[s][:], total[s][:], 1.0 / HEAD, None, ALU.mult).then_inc(mean_ready, 1)
                dve.wait_ge(mean_ready, s + 1)
                dve.tensor_tensor(heads(s), heads(s), across(total[s][:]), ALU.subtract).then_inc(centred, 1)

            def finish(s):
                dve.wait_ge(squared, s + 1)
                dve.tensor_reduce(spread[s][:], squares[s % 2][:], AX_X, ALU.add).then_inc(spread_ready, 1)
                dve.wait_ge(sd_ready, s + 1)
                dve.reciprocal(rstd[s][:], sd[s][:]).then_inc(rstd_ready, 1)
                dve.wait_ge(rstd_ready, s + 1)
                dve.tensor_tensor(heads(s), heads(s), across(rstd[s][:]), ALU.mult).then_inc(scaled, 1)

            centre(0)
            for s in range(STEPS):
                if s + 1 < STEPS:
                    centre(s + 1)
                finish(s)

        @block.scalar
        def _(act):
            for s in range(STEPS):
                act.wait_ge(centred, s + 1)
                if s >= 2:
                    act.wait_ge(spread_ready, s - 1)
                act.activation(squares[s % 2][:], heads(s), ACT.Square).then_inc(squared, 1)
                act.wait_ge(spread_ready, s + 1)
                act.activation(sd[s][:], spread[s][:], ACT.Sqrt, bias=core.norm_eps[:],
                               scale=1.0 / HEAD).then_inc(sd_ready, 1)


def l0_attention(nc, core, weights, angles, head_rows, affine, w_out):
    VA = HEAD + 1
    GROUP = P // HEAD
    with ExitStack() as ctx:
        def sb(name, shape):
            return ctx.enter_context(nc.sbuf_tensor(f"l0a_{name}", shape, F32))

        v1 = sb("v1", [P, TILES, HEADS, VA])
        qkT = sb("qkT", [P, 2 * KC, TOKENS])
        with nc.sbuf_tensor("l0a_qk", [P, TILES, 2 * D], F32) as qk:
            rope_qkv_stage(nc, core, "l0_qkv", weights, angles, 2 * HEADS, qk, D,
                           lambda t: v1[:, t, :, 0:HEAD])
            l0_head_norm_stage(nc, core, qk)
            turn_stage(nc, core, "l0_turn", qk, 2 * KC, qkT, affine)
        o = sb("o", [P, TILES, D])
        with Stage(nc, "l0_heads") as st:
            rows = st.sb("rows", [P, GROUP])
            causal = st.sb("causal", [P, 3 * P])
            own_k = [st.sb(f"own_k{b}", [P, GROUP, SEQ]) for b in range(2)]
            NB = 4
            squares = [st.sb(f"squares{b}", [P, 3 * P]) for b in range(NB)]
            masked = [st.sb(f"masked{b}", [P, 3 * P]) for b in range(NB)]
            fourth = [st.sb(f"fourth{b}", [P, 3 * P]) for b in range(NB)]
            inverse = st.sb("inverse", [P, TILES, HEADS])
            ps_s = [st.ps(f"ps_s{b}", [P, HALF]) for b in range(NB)]
            ps_o = [st.ps(f"ps_o{b}", [P, HALF]) for b in range(4)]
            rows_loaded = st.sem("rows_loaded")
            causal_ready = st.sem("causal_ready")
            ones_ready = st.sem("ones_ready")
            own_ready = st.sem("own_ready")
            scored = st.sem("scored")
            squared = st.sem("squared")
            mask_done = st.sem("mask_done")
            fourth_ready = st.sem("fourth_ready")
            summed = st.sem("summed")
            inverse_ready = st.sem("inverse_ready")
            o_ready = st.sem("o_ready")
            ALL = BATCH * HEADS
            LAG = 3
            block = st.block()

            @block.sync
            def _(sp):
                sp.dma_start(rows[:], head_rows).then_inc(rows_loaded, 16)

            @block.gpsimd
            def _(pool):
                pool.tensor_copy(causal[:, 0:P], core.upto[:]).then_inc(causal_ready, 1)
                pool.memset(causal[:, P:2 * P], 1.0).then_inc(causal_ready, 1)
                pool.tensor_copy(causal[:, 2 * P:3 * P], core.upto[:]).then_inc(causal_ready, 1)
                pool.memset(v1[:, :, :, HEAD:VA], 1.0).then_inc(ones_ready, 1)
                pool.wait_ge(rows_loaded, 16)
                for n in range(BATCH * KC):
                    b, g = n // KC, n % KC
                    if n >= 2:
                        pool.wait_ge(scored, GROUP * (n - 1))
                    pool.tensor_tensor(
                        own_k[n % 2][:],
                        qkT[:, KC + g, b * SEQ:(b + 1) * SEQ].unsqueeze(1).broadcast_to([P, GROUP, SEQ]),
                        rows[:].unsqueeze(2).broadcast_to([P, GROUP, SEQ]), ALU.mult).then_inc(own_ready, 1)

            @block.tensor
            def _(pe):
                def scores(n):
                    b, h = n // HEADS, n % HEADS
                    g, e = h // GROUP, h % GROUP
                    pe.wait_ge(own_ready, n // GROUP + 1)
                    if n >= NB:
                        pe.wait_ge(squared, n - NB + 1)
                    k = own_k[(n // GROUP) % 2]
                    q = qkT[:, g, b * SEQ:(b + 1) * SEQ]
                    pe.matmul(ps_s[n % NB][:, 0:2 * P], k[:, e, 0:P], q, start=True, stop=True)
                    pe.matmul(ps_s[n % NB][:, 2 * P:3 * P], k[:, e, P:2 * P], q[:, P:2 * P],
                              start=True, stop=True).then_inc(scored, 1)

                def values(n):
                    b, h = n // HEADS, n % HEADS
                    pe.wait_ge(fourth_ready, n + 1)
                    if h == 0 and b >= 2:
                        pe.wait_ge(o_ready, 2 * (b - 1))
                    a = fourth[n % NB]
                    out0, out1 = (ps_o[2 * (b % 2) + j][:, h * VA:(h + 1) * VA] for j in range(2))
                    pe.matmul(out0, a[:, 0:P], v1[:, 2 * b, h, :], start=True, stop=True)
                    pe.matmul(out1, a[:, P:2 * P], v1[:, 2 * b, h, :], start=True, stop=False)
                    pe.matmul(out1, a[:, 2 * P:3 * P], v1[:, 2 * b + 1, h, :], start=False, stop=True)\
                        .then_inc(summed, 1)

                pe.wait_ge(ones_ready, 1)
                for n in range(ALL + LAG):
                    if n < ALL:
                        scores(n)
                    if n >= LAG:
                        values(n - LAG)

            @block.scalar
            def _(act):
                for n in range(ALL + 1):
                    if n < ALL:
                        act.wait_ge(scored, n + 1)
                        if n >= NB:
                            act.wait_ge(mask_done, n - NB + 1)
                        act.activation(squares[n % NB][:], ps_s[n % NB][:, 0:3 * P], ACT.Square)\
                            .then_inc(squared, 1)
                    if n >= 1:
                        m = n - 1
                        act.wait_ge(mask_done, m + 1)
                        if m >= NB:
                            act.wait_ge(summed, m - NB + 1)
                        act.activation(fourth[m % NB][:], masked[m % NB][:], ACT.Square)\
                            .then_inc(fourth_ready, 1)

            @block.vector
            def _(dve):
                def norm(b):
                    dve.wait_ge(summed, HEADS * (b + 1))
                    for j in range(2):
                        t = 2 * b + j
                        bank = ps_o[2 * (b % 2) + j][:, 0:HEADS * VA].rearrange("p (h d) -> p h d", d=VA)
                        dve.reciprocal(inverse[:, t, :], bank[:, :, HEAD]).then_inc(inverse_ready, 1)
                        dve.wait_ge(inverse_ready, t + 1)
                        dve.tensor_tensor(o[:, t, :].rearrange("p (h d) -> p h d", d=HEAD), bank[:, :, 0:HEAD],
                                          inverse[:, t, :].unsqueeze(2).broadcast_to([P, HEADS, HEAD]),
                                          ALU.mult).then_inc(o_ready, 1)

                dve.wait_ge(causal_ready, 3)
                for n in range(ALL):
                    dve.wait_ge(squared, n + 1)
                    if n >= NB:
                        dve.wait_ge(fourth_ready, n - NB + 1)
                    dve.tensor_tensor(masked[n % NB][:], squares[n % NB][:], causal[:], ALU.mult)\
                        .then_inc(mask_done, 1)
                    if n % HEADS == LAG + 2 and n >= HEADS:
                        norm(n // HEADS - 1)
                norm(BATCH - 1)

        oT = sb("oT", [P, KC, TOKENS])
        turn_stage(nc, core, "l0_turn_o", o, KC, oT)
        project_stage(nc, core, "l0_project", oT, w_out)


EXPERTS1, TOP1 = 8, 2
OWNERS1 = EXPERTS1 + 1
EXPERT1, SHARED1 = 176, 352
INTER1 = EXPERTS1 * EXPERT1 + SHARED1
F1, UNITS1 = 126, 14


def route_stage(nc, core, name, router, experts, top, weight_rows=None, slot_of=None, parts=None,
                xn=None, xn_parts=None):
    E = experts
    with Stage(nc, name) as st:
        w = st.sb("w", [P, KC, E])
        score = st.sb("score", [P, TILES, E])
        peak = st.sb("peak", [P, TILES])
        total = st.sb("total", [P, TILES])
        best = st.sb("best", [P, TILES, 8])
        above = st.sb("above", [P, TILES, E])
        equal = st.sb("equal", [P, TILES, E])
        count = [st.sb(f"count{b}", [P, TILES, E]) for b in range(2)]
        n_above = st.sb("n_above", [P, TILES])
        chosen = st.sb("chosen", [P, TILES, E])
        earlier = st.sb("earlier", [P, TILES, E])
        ps = st.ps("ps", [P, TILES, E])
        ps_rank = st.ps("ps_rank", [P, TILES, E])
        if weight_rows is not None:
            every = st.sb("every", [P, TILES, E + 1])
            every_rest = st.sb("every_rest", [P, TILES, E + 1])
            row_parts = st.sb("row_parts", [P, TILES, 3, E + 1], BF16)
            spare = st.sb("spare", [P, 1])
            turn = st.ps("turn", [P, TOKENS], BF16)
            row_parts_ready = st.sem("row_parts_ready")
            rows_turned = st.sem("rows_turned")
            rows_cleared = st.sem("rows_cleared")
        loaded = st.sem("loaded")
        logits_ready = st.sem("logits_ready")
        shifted = st.sem("shifted")
        exp_ready = st.sem("exp_ready")
        step_done = st.sem("step_done")
        chosen_ready = st.sem("chosen_ready")
        earlier_ready = st.sem("earlier_ready")
        rank_ready = st.sem("rank_ready")
        block = st.block()

        def across(ap):
            return ap.unsqueeze(2).broadcast_to([P, TILES, E])

        @block.sync
        def _(sp):
            sp.dma_start(w[:], router.rearrange("(c p) n -> p c n", p=P)).then_inc(loaded, 16)

        @block.tensor
        def _(pe):
            pe.wait_ge(loaded, 16)
            for t in range(TILES):
                for c in range(KC):
                    mm = pe.matmul(ps[:, t, :], core.xnT[:, c, t * P:(t + 1) * P], w[:, c, :],
                                   start=(c == 0), stop=(c == KC - 1))
            mm.then_inc(logits_ready, 1)
            if slot_of is not None:
                pe.wait_ge(chosen_ready, 1)
                pe.matmul(ps_rank[:].rearrange("p t e -> p (t e)"), core.before[:],
                          chosen[:].rearrange("p t e -> p (t e)"), start=True, stop=False)
                pe.wait_ge(earlier_ready, 1)
                pe.matmul(ps_rank[:].rearrange("p t e -> p (t e)"), core.ones[:],
                          earlier[:].rearrange("p t e -> p (t e)"), start=False, stop=True).then_inc(rank_ready, 1)

            if weight_rows is not None:
                pe.wait_ge(row_parts_ready, 1)
                for t in range(TILES):
                    tr = pe.transpose(turn[0:3 * (E + 1), t * P:(t + 1) * P],
                                      row_parts[:, t].rearrange("p k e -> p (k e)"), core.ident_bf16[:])
                tr.then_inc(rows_turned, 1)

        if weight_rows is not None:
            @block.gpsimd
            def _(pool):
                pool.memset(weight_rows[:], 0.0).then_inc(rows_cleared, 1)

        if xn_parts is not None:
            rest_of_xn = st.sb("rest_of_xn", [P, TILES, D])
            cut = st.sem("cut")

            @block.gpsimd
            def _(pool):
                pool.wait_ge(cut, 1)
                pool.tensor_tensor(rest_of_xn[:], xn[:], xn_parts[0][:], ALU.subtract).then_inc(cut, 1)
                pool.wait_ge(cut, 3)
                pool.tensor_tensor(xn_parts[2][:], rest_of_xn[:], xn_parts[1][:], ALU.subtract)

        @block.scalar
        def _(act):
            if xn_parts is not None:
                act.copy(xn_parts[0][:], xn[:]).then_inc(cut, 1)
            act.wait_ge(shifted, 1)
            act.activation(score[:], score[:], ACT.Exp).then_inc(exp_ready, 1)
            if xn_parts is not None:
                act.wait_ge(cut, 2)
                act.copy(xn_parts[1][:], rest_of_xn[:]).then_inc(cut, 1)

        @block.vector
        def _(dve):
            steps = [0]

            def link(ins):
                steps[0] += 1
                ins.then_inc(step_done, 1)
                dve.wait_ge(step_done, steps[0])

            dve.wait_ge(logits_ready, 1)
            link(dve.tensor_reduce(peak[:], ps[:], AX_X, ALU.max))
            dve.tensor_tensor(score[:], ps[:], across(peak[:]), ALU.subtract).then_inc(shifted, 1)
            dve.wait_ge(exp_ready, 1)
            link(dve.tensor_reduce(total[:], score[:], AX_X, ALU.add))
            link(dve.reciprocal(total[:], total[:]))
            link(dve.tensor_tensor(score[:], score[:], across(total[:]), ALU.mult))
            for t in range(TILES):
                last = dve.max(best[:, t, :], score[:, t, :])
                if t < TILES - 1:
                    last.then_inc(step_done, 1)
                    steps[0] += 1
            link(last)
            least = best[:, :, top - 1].unsqueeze(2).broadcast_to([P, TILES, E])
            link(dve.tensor_tensor(above[:], score[:], least, ALU.is_gt))
            link(dve.tensor_tensor(equal[:], score[:], least, ALU.is_equal))
            link(dve.tensor_reduce(n_above[:], above[:], AX_X, ALU.add))
            src, n, b = equal, 1, 0
            while n < E:
                dst = count[b]
                link(dve.tensor_copy(dst[:, :, 0:n], src[:, :, 0:n]))
                link(dve.tensor_tensor(dst[:, :, n:E], src[:, :, n:E], src[:, :, 0:E - n], ALU.add))
                src, n, b = dst, 2 * n, 1 - b
            link(dve.tensor_tensor(src[:], src[:], across(n_above[:]), ALU.add))
            link(dve.scalar_tensor_tensor(out=chosen[:], in0=src[:], scalar=float(top), in1=equal[:],
                                          op0=ALU.is_le, op1=ALU.mult))
            dve.tensor_tensor(chosen[:], chosen[:], above[:], ALU.add).then_inc(chosen_ready, 1)
            dve.wait_ge(chosen_ready, 1)
            link(dve.scalar_tensor_tensor(out=score[:], in0=score[:], scalar=0.5, in1=chosen[:],
                                          op0=ALU.mult, op1=ALU.mult))
            def cut_weights(part, src, rest):
                for k in range(3):
                    link(dve.tensor_copy(part(k), src if k == 0 else rest))
                    if k < 2:
                        link(dve.tensor_tensor(rest, src if k == 0 else rest, part(k), ALU.subtract))

            if slot_of is not None:
                link(dve.memset(earlier[:, 0, :], 0.0))
                for t in range(1, TILES):
                    add = dve.tensor_tensor(earlier[:, t, :], earlier[:, t - 1, :], chosen[:, t - 1, :], ALU.add)
                    if t < TILES - 1:
                        link(add)
                add.then_inc(earlier_ready, 1)
                cut_weights(lambda k: parts[:, :, :, k], score[:], above[:])
                dve.wait_ge(rank_ready, 1)
                link(dve.scalar_tensor_tensor(out=equal[:], in0=ps_rank[:], scalar=1.0, in1=chosen[:],
                                              op0=ALU.add, op1=ALU.mult))
                dve.tensor_scalar(slot_of[:], equal[:], 1.0, None, ALU.subtract)
            else:
                link(dve.memset(every[:, :, E:], 0.5))
                link(dve.tensor_copy(every[:, :, 0:E], score[:]))
                cut_weights(lambda k: row_parts[:, :, k, :], every[:], every_rest[:])
                dve.memset(spare[:], 0.0).then_inc(row_parts_ready, 1)
                dve.wait_ge(rows_turned, 1)
                dve.wait_ge(rows_cleared, 1)
                dve.tensor_copy(weight_rows[0:3 * (E + 1), :], turn[0:3 * (E + 1), :])


HEADS1 = 16
DH1 = 128
LATENT = 64
ROPE1 = 64
RMS_EPS = 1e-6
MASKED = -1e30


def l1_latent_stage(nc, core, weights, norm_w, latT):
    with Stage(nc, "latent") as st:
        w = st.sb("w", [P, KC, LATENT])
        gain = st.sb("gain", [P, LATENT])
        eps = st.sb("eps", [P, 1])
        squares = st.sb("squares", [P, TILES, LATENT])
        lat = st.sb("lat", [P, TILES, LATENT])
        total = st.sb("total", [P, TILES])
        rms = st.sb("rms", [P, TILES])
        inverse = st.sb("inverse", [P, TILES])
        ps = st.ps("ps", [P, TILES, LATENT])
        turn = st.ps("turn", [P, HALVES, HALF])
        loaded = st.sem("loaded")
        eps_ready = st.sem("eps_ready")
        projected = st.sem("projected")
        squared = st.sem("squared")
        total_ready = st.sem("total_ready")
        rms_ready = st.sem("rms_ready")
        step_done = st.sem("step_done")
        lat_ready = st.sem("lat_ready")
        turned = st.sem("turned")
        block = st.block()

        @block.sync
        def _(sp):
            sp.dma_start(w[:], weights.rearrange("(c p) n -> p c n", p=P)).then_inc(loaded, 16)
            sp.dma_start(gain[:], norm_w.partition_broadcast(P)).then_inc(loaded, 16)

        @block.gpsimd
        def _(pool):
            pool.memset(eps[:], RMS_EPS).then_inc(eps_ready, 1)

        @block.tensor
        def _(pe):
            pe.wait_ge(loaded, 32)
            for t in range(TILES):
                for c in range(KC):
                    mm = pe.matmul(ps[:, t, :], core.xnT[:, c, t * P:(t + 1) * P], w[:, c, :],
                                   start=(c == 0), stop=(c == KC - 1))
            mm.then_inc(projected, 1)
            pe.wait_ge(lat_ready, 1)
            for t in range(TILES):
                tr = pe.transpose(turn[0:LATENT, t // 4, (t % 4) * P:(t % 4 + 1) * P], lat[:, t, :], core.ident[:])
            tr.then_inc(turned, 1)

        @block.scalar
        def _(act):
            act.wait_ge(projected, 1)
            act.activation(squares[:], ps[:], ACT.Square).then_inc(squared, 1)
            act.wait_ge(total_ready, 1)
            act.wait_ge(eps_ready, 1)
            act.activation(rms[:], total[:], ACT.Sqrt, bias=eps[:], scale=1.0 / LATENT).then_inc(rms_ready, 1)

        @block.vector
        def _(dve):
            dve.wait_ge(squared, 1)
            dve.tensor_reduce(total[:], squares[:], AX_X, ALU.add).then_inc(total_ready, 1)
            dve.wait_ge(rms_ready, 1)
            dve.reciprocal(inverse[:], rms[:]).then_inc(step_done, 1)
            dve.wait_ge(step_done, 1)
            dve.tensor_tensor(lat[:], ps[:], inverse[:].unsqueeze(2).broadcast_to([P, TILES, LATENT]),
                              ALU.mult).then_inc(step_done, 1)
            dve.wait_ge(step_done, 2)
            dve.wait_ge(loaded, 32)
            dve.tensor_tensor(lat[:], lat[:], gain[:].unsqueeze(1).broadcast_to([P, TILES, LATENT]),
                              ALU.mult).then_inc(lat_ready, 1)
            dve.wait_ge(turned, 1)
            dve.tensor_copy(latT[:], turn[0:LATENT, :, :].rearrange("p h n -> p (h n)"))


def wide_project_stage(nc, core, name, oT, weights, bias, heads):
    with Stage(nc, name) as st:
        w = st.sb("w", [P, heads, D])
        row = st.sb("row", [P, D])
        banks = [st.ps(f"bank{q}", [P, 2, D]) for q in range(4)]
        PARTS = 4
        loaded = [st.sem(f"loaded{i}") for i in range(PARTS)]
        bias_loaded = st.sem("bias_loaded")
        projected = st.sem("projected")
        bias_added = st.sem("bias_added")
        block = st.block()
        per = heads // PARTS

        @block.sync
        def _(sp):
            for i in range(PARTS):
                sp.dma_start(w[:, i * per:(i + 1) * per, :],
                             weights[i * per:(i + 1) * per].rearrange("h p d -> p h d")).then_inc(loaded[i], 16)
            if bias is not None:
                sp.dma_start(row[:], bias.partition_broadcast(P)).then_inc(bias_loaded, 16)

        @block.tensor
        def _(pe):
            for t in range(TILES):
                for h in range(heads):
                    if t == 0 and h % per == 0:
                        pe.wait_ge(loaded[h // per], 16)
                    mm = pe.matmul(banks[t // 2][:, t % 2, :], oT[:, h, t * P:(t + 1) * P], w[:, h, :],
                                   start=(h == 0), stop=(h == heads - 1))
                mm.then_inc(projected, 1)

        @block.vector
        def _(dve):
            if bias is not None:
                dve.wait_ge(bias_loaded, 16)
                dve.tensor_tensor(core.x[:], core.x[:], row[:].unsqueeze(1).broadcast_to([P, TILES, D]),
                                  ALU.add).then_inc(bias_added, 1)
                dve.wait_ge(bias_added, 1)
            for q in range(4):
                dve.wait_ge(projected, 2 * q + 2)
                dve.tensor_tensor(core.x[:, 2 * q:2 * q + 2, :], core.x[:, 2 * q:2 * q + 2, :],
                                  banks[q][:], ALU.add)


def l1_attention(nc, core, wkv_a, norm_w, wq, wkv, columns, signs, w_out, b_out):
    SCALE = 1.0 / float(DH1) ** 0.5
    X0, X1 = P - ROPE1, P - ROPE1 // 2
    with ExitStack() as ctx:
        latT = ctx.enter_context(nc.sbuf_tensor("l1a_latT", [LATENT, TOKENS], F32))
        oT = ctx.enter_context(nc.sbuf_tensor("l1a_oT", [P, HEADS1, TOKENS], F32))
        l1_latent_stage(nc, core, wkv_a, norm_w, latT)
        with Stage(nc, "l1_heads") as st:
            w_q = [st.sb(f"w_q{b}", [P, KC, DH1]) for b in range(2)]
            w_kv = [st.sb(f"w_kv{b}", [LATENT, 2 * DH1]) for b in range(2)]
            sign = st.sb("sign", [P, 1])
            column = [st.sb(f"column{b}", [P, 3]) for b in range(2)]
            derived = [st.sb(f"derived{b}", [P, 3]) for b in range(2)]
            mask = st.sb("mask", [P, 3 * P])
            o_head = [st.sb(f"o_head{b}", [P, TOKENS]) for b in range(2)]
            qT = [st.sb(f"qT{b}", [P, TOKENS]) for b in range(2)]
            kT = [st.sb(f"kT{b}", [P, TOKENS]) for b in range(2)]
            cross = [st.sb(f"cross{i}", [P, TOKENS]) for i in range(2)]
            v = [st.sb(f"v{b}", [P, TILES, DH1]) for b in range(2)]
            logit = [st.sb(f"logit{b}", [P, 3 * P]) for b in range(2)]
            peak = st.sb("peak", [P, BATCH, 2])
            shift = st.sb("shift", [P, BATCH, 2])
            total = st.sb("total", [P, BATCH, 2])
            inverse = st.sb("inverse", [P, BATCH, 2])
            e = [st.sb(f"e{b}", [P, 3 * P]) for b in range(2)]
            prob = [st.sb(f"prob{b}", [P, 3 * P]) for b in range(2)]
            probT = [st.sb(f"probT{b}", [P, 3 * P]) for b in range(2)]
            ps_p = [st.ps(f"ps_p{b}", [P, HALF]) for b in range(2)]
            ps_s = [st.ps(f"ps_s{b}", [P, HALF]) for b in range(2)]
            ps_t = [st.ps(f"ps_t{b}", [P, HALF]) for b in range(2)]
            ps_o = [st.ps(f"ps_o{b}", [P, HALF]) for b in range(2)]

            small_loaded = st.sem("small_loaded")
            sine_ready = st.sem("sine_ready")
            derived_ready = st.sem("derived_ready")
            o_stored = [st.sem(f"o_stored{b}") for b in range(2)]
            mask_step = st.sem("mask_step")
            w_loaded = [st.sem(f"w_loaded{b}") for b in range(2)]
            projected = st.sem("projected")
            plain_done = st.sem("plain_done")
            cross_done = st.sem("cross_done")
            qk_ready = st.sem("qk_ready")
            scored = st.sem("scored")
            masked = st.sem("masked")
            peak_ready = st.sem("peak_ready")
            shift_ready = st.sem("shift_ready")
            exp_done = st.sem("exp_done")
            inverse_ready = st.sem("inverse_ready")
            prob_ready = st.sem("prob_ready")
            turned = st.sem("turned")
            probT_ready = st.sem("probT_ready")
            summed = st.sem("summed")
            o_copied = st.sem("o_copied")
            block = st.block()

            def over_heads(eng, prologue, step):
                prologue()
                step(0, 0, True, True)
                with eng.Fori(1, HEADS1 // 2) as i:
                    step(2 * i - 1, 1, False, True)
                    step(2 * i, 0, False, True)
                step(HEADS1 - 1, 1, False, False)

            @block.sync
            def _(sp):
                sp.dma_start(sign[:], signs).then_inc(small_loaded, 16)

                def load(h, b, first):
                    if not first:
                        sp.wait_ge(projected, 6 * (h - 1))
                    sp.dma_start(column[b][:], columns[bass.ds(h, 1)].rearrange("a p n -> (a p) n"))\
                        .then_inc(w_loaded[b], 16)
                    sp.dma_start(w_q[b][:], wq[bass.ds(h, 1)].rearrange("a p c n -> (a p) c n"))\
                        .then_inc(w_loaded[b], 16)
                    sp.dma_start(w_kv[b][:], wkv[bass.ds(h, 1)].rearrange("a p n -> (a p) n"))\
                        .then_inc(w_loaded[b], 16)

                def store(h, b):
                    sp.wait_ge(o_copied, 2 * h + 2)
                    sp.dma_start(oT[:, bass.ds(h, 1), :].rearrange("p a n -> p (a n)"), o_head[b][:])\
                        .then_inc(o_stored[b], 16)

                load(0, 0, True)
                load(1, 1, True)
                load(2, 0, False)
                store(0, 0)
                with sp.Fori(1, HEADS1 // 2 - 1) as i:
                    load(2 * i + 1, 1, False)
                    store(2 * i - 1, 1)
                    load(2 * i + 2, 0, False)
                    store(2 * i, 0)
                load(HEADS1 - 1, 1, False)
                for h in (HEADS1 - 3, HEADS1 - 2, HEADS1 - 1):
                    store(h, h % 2)
                for b in range(2):
                    sp.wait_ge(o_stored[b], 16 * (HEADS1 // 2))

            @block.tensor
            def _(pe):
                def project_q(p, i, b, first):
                    pe.wait_ge(w_loaded[b], 48 * (i + 1))
                    for h in range(HALVES):
                        if not first:
                            pe.wait_ge(plain_done, 6 * (p - 1) + 5 + h)
                        for c in range(KC):
                            mm = pe.matmul(ps_p[h][:], w_q[b][:, c, :], core.xnT[:, c, h * HALF:(h + 1) * HALF],
                                           start=(c == 0), stop=(c == KC - 1))
                        mm.then_inc(projected, 1)

                def project_k(p, b):
                    for h in range(HALVES):
                        pe.wait_ge(plain_done, 6 * p + h + 1)
                        pe.wait_ge(cross_done, 4 * p + h + 1)
                        pe.matmul(ps_p[h][:], w_kv[b][:, 0:DH1], latT[:, h * HALF:(h + 1) * HALF],
                                  start=True, stop=True).then_inc(projected, 1)

                def project_v(p, b):
                    for h in range(HALVES):
                        pe.wait_ge(plain_done, 6 * p + h + 3)
                        pe.wait_ge(cross_done, 4 * p + h + 3)
                        for j in range(4):
                            t = 4 * h + j
                            mm = pe.matmul(ps_p[h][:, j * DH1:(j + 1) * DH1], latT[:, t * P:(t + 1) * P],
                                           w_kv[b][:, DH1:2 * DH1], start=True, stop=True)
                        mm.then_inc(projected, 1)

                def scores(h, b, n, first):
                    if n == 0:
                        pe.wait_ge(qk_ready, 2 * h + 2)
                    if not (first and n < 2):
                        pe.wait_ge(masked, BATCH * h + n - 1)
                    q, k = qT[b][:, n * SEQ:(n + 1) * SEQ], kT[b][:, n * SEQ:(n + 1) * SEQ]
                    pe.matmul(ps_s[n % 2][:, 0:P], q[:, 0:P], k[:, 0:P], start=True, stop=True)
                    pe.matmul(ps_s[n % 2][:, P:3 * P], q[:, P:2 * P], k, start=True, stop=True)\
                        .then_inc(scored, 1)

                def turn(h, n, first):
                    pe.wait_ge(prob_ready, BATCH * h + n + 1)
                    if not (first and n < 2):
                        pe.wait_ge(probT_ready, BATCH * h + n - 1)
                    for j in range(3):
                        tr = pe.transpose(ps_t[n % 2][:, j * P:(j + 1) * P], prob[n % 2][:, j * P:(j + 1) * P],
                                          core.ident[:])
                    tr.then_inc(turned, 1)

                def values(h, b, n, first):
                    pe.wait_ge(probT_ready, BATCH * h + n + 1)
                    if not first and n % 2 == 0:
                        pe.wait_ge(o_copied, 2 * (h - 1) + n // 2 + 1)
                    out = ps_o[n // 2][:, (n % 2) * SEQ:(n % 2 + 1) * SEQ]
                    pe.matmul(out, v[b][:, 2 * n, :], probT[n % 2][:, 0:2 * P], start=True, stop=False)
                    pe.matmul(out[:, P:2 * P], v[b][:, 2 * n + 1, :], probT[n % 2][:, 2 * P:3 * P],
                              start=False, stop=True).then_inc(summed, 1)

                def prologue():
                    project_q(0, 0, 0, True)
                    project_k(0, 0)
                    project_v(0, 0)
                    scores(0, 0, 0, True)
                    scores(0, 0, 1, True)

                def step(h, b, first, more):
                    nb = 1 - b
                    i = (h + 1) // 2 if isinstance(h, int) else h_half[0]
                    if more:
                        project_q(h + 1, i, nb, False)
                    turn(h, 0, first)
                    scores(h, b, 2, first)
                    if more:
                        project_k(h + 1, nb)
                    turn(h, 1, first)
                    values(h, b, 0, first)
                    scores(h, b, 3, first)
                    if more:
                        project_v(h + 1, nb)
                    turn(h, 2, first)
                    values(h, b, 1, first)
                    if more:
                        scores(h + 1, nb, 0, False)
                    turn(h, 3, first)
                    values(h, b, 2, first)
                    if more:
                        scores(h + 1, nb, 1, False)
                    values(h, b, 3, first)

                h_half = [0]
                prologue()
                step(0, 0, True, True)
                with pe.Fori(1, HEADS1 // 2) as i:
                    h_half[0] = i
                    step(2 * i - 1, 1, False, True)
                    step(2 * i, 0, False, True)
                step(HEADS1 - 1, 1, False, False)

            @block.scalar
            def _(act):
                def plain(p, b, which, first):
                    dst = (qT, kT)[which][b]
                    if not first:
                        act.wait_ge(summed, BATCH * (p - 1))
                    if which == 0:
                        act.wait_ge(derived_ready, 2 * p + 2)
                    for h in range(HALVES):
                        act.wait_ge(projected, 6 * p + 2 * which + h + 1)
                        out = dst[:, h * HALF:(h + 1) * HALF]
                        if which == 0:
                            act.activation(out, ps_p[h][:], ACT.Identity, bias=derived[b][:, 2:3],
                                           scale=column[b][:, 1:2]).then_inc(plain_done, 1)
                        else:
                            act.activation(out, ps_p[h][:], ACT.Copy, scale=column[b][:, 1:2])\
                                .then_inc(plain_done, 1)

                def copy_v(p, b, first):
                    if not first:
                        act.wait_ge(summed, BATCH * (p - 1))
                    for h in range(HALVES):
                        act.wait_ge(projected, 6 * p + 4 + h + 1)
                        act.copy(v[b][:, 4 * h:4 * h + 4, :].rearrange("p t n -> p (t n)"), ps_p[h][:])\
                            .then_inc(plain_done, 1)

                def exps(h, n, first):
                    act.wait_ge(shift_ready, BATCH * h + n + 1)
                    if not (first and n < 2):
                        act.wait_ge(prob_ready, BATCH * h + n - 1)
                    for j, (lo, hi) in enumerate(((0, P), (P, 3 * P))):
                        last = act.activation(e[n % 2][:, lo:hi], logit[n % 2][:, lo:hi], ACT.Exp,
                                              bias=shift[:, n, j:j + 1], scale=SCALE,
                                              accum_out=total[:, n, j:j + 1])
                        last.then_inc(exp_done, 1)

                def copy_o(h, b, i, j):
                    if i is not None:
                        act.wait_ge(o_stored[b], 16 * i)
                    act.wait_ge(summed, BATCH * h + 2 * j + 2)
                    act.copy(o_head[b][:, 2 * j * SEQ:2 * (j + 1) * SEQ], ps_o[j][:]).then_inc(o_copied, 1)

                def prologue():
                    plain(0, 0, 0, True)
                    plain(0, 0, 1, True)
                    copy_v(0, 0, True)
                    exps(0, 0, True)
                    exps(0, 1, True)

                def step(h, b, first, more):
                    if more:
                        plain(h + 1, 1 - b, 0, first)
                    if more:
                        plain(h + 1, 1 - b, 1, first)
                    exps(h, 2, first)
                    exps(h, 3, first)
                    if more:
                        copy_v(h + 1, 1 - b, first)
                        exps(h + 1, 0, False)
                        exps(h + 1, 1, False)
                    for j in range(2):
                        copy_o(h, b, stored_before[0], j)

                stored_before = [None]
                prologue()
                step(0, 0, True, True)
                with act.Fori(1, HEADS1 // 2) as i:
                    stored_before[0] = i - 1
                    step(2 * i - 1, 1, False, True)
                    stored_before[0] = i
                    step(2 * i, 0, False, True)
                stored_before[0] = HEADS1 // 2 - 1
                step(HEADS1 - 1, 1, False, False)

            @block.vector
            def _(dve):
                def sines_of(p, b, which, first, halves=range(HALVES)):
                    if not first:
                        dve.wait_ge(qk_ready, 2 * (p - 1) + which + 1)
                    for h in halves:
                        dve.wait_ge(plain_done, 6 * p + 2 * which + h + 1)
                        for src, dst in ((X1, X0), (X0, X1)):
                            rows, to = slice(src, src + ROPE1 // 2), slice(dst, dst + ROPE1 // 2)
                            out = cross[which][to, h * HALF:(h + 1) * HALF]
                            if which == 0:
                                last = dve.tensor_scalar(out, ps_p[h][rows, :], derived[b][rows, 0:1],
                                                         derived[b][rows, 1:2], ALU.mult, ALU.add)
                            else:
                                last = dve.tensor_scalar(out, ps_p[h][rows, :], derived[b][rows, 0:1],
                                                         None, ALU.mult)
                        last.then_inc(cross_done, 1)

                def mask_max(h, n, first):
                    dve.wait_ge(scored, BATCH * h + n + 1)
                    if not (first and n < 2):
                        dve.wait_ge(exp_done, 2 * (BATCH * h + n - 1))
                    dve.tensor_tensor(logit[n % 2][:], ps_s[n % 2][:, 0:3 * P], mask[:], ALU.add)\
                        .then_inc(masked, 1)
                    dve.wait_ge(masked, BATCH * h + n + 1)
                    for j, (lo, hi) in enumerate(((0, P), (P, 3 * P))):
                        last = dve.tensor_reduce(peak[:, n, j:j + 1], logit[n % 2][:, lo:hi], AX_X, ALU.max)
                        last.then_inc(peak_ready, 1)
                    dve.wait_ge(peak_ready, 2 * (BATCH * h + n + 1))
                    dve.tensor_scalar(shift[:, n, :], peak[:, n, :], -SCALE, None, ALU.mult)\
                        .then_inc(shift_ready, 1)

                def invert(h, n):
                    dve.wait_ge(exp_done, 2 * (BATCH * h + n + 1))
                    dve.reciprocal(inverse[:, n, :], total[:, n, :]).then_inc(inverse_ready, 1)

                def copy_probT(h, n, first):
                    dve.wait_ge(turned, BATCH * h + n + 1)
                    if not (first and n < 2):
                        dve.wait_ge(summed, BATCH * h + n - 1)
                    dve.tensor_copy(probT[n % 2][:], ps_t[n % 2][:, 0:3 * P]).then_inc(probT_ready, 1)

                def prologue():
                    dve.wait_ge(mask_step, 3)
                    sines_of(0, 0, 0, True)
                    sines_of(0, 0, 1, True)
                    mask_max(0, 0, True)
                    mask_max(0, 1, True)

                def step(h, b, first, more):
                    invert(h, 0)
                    invert(h, 1)
                    if more:
                        sines_of(h + 1, 1 - b, 0, False)
                    copy_probT(h, 0, first)
                    mask_max(h, 2, first)
                    copy_probT(h, 1, first)
                    if more:
                        sines_of(h + 1, 1 - b, 1, False, (0,))
                    invert(h, 2)
                    if more:
                        sines_of(h + 1, 1 - b, 1, False, (1,))
                    mask_max(h, 3, first)
                    invert(h, 3)
                    copy_probT(h, 2, first)
                    if more:
                        mask_max(h + 1, 0, False)
                    copy_probT(h, 3, first)
                    if more:
                        mask_max(h + 1, 1, False)

                over_heads(dve, prologue, step)

            @block.gpsimd
            def _(pool):
                def derive(p, b, i, first):
                    pool.wait_ge(w_loaded[b], 48 * (i + 1))
                    if not first:
                        pool.wait_ge(cross_done, 4 * (p - 1))
                        pool.wait_ge(plain_done, 6 * (p - 1))
                    pool.tensor_tensor(derived[b][:, 0:1], column[b][:, 2:3], sign[:], ALU.mult)\
                        .then_inc(sine_ready, 1)
                    pool.wait_ge(sine_ready, p + 1)
                    pool.tensor_tensor(derived[b][:, 1:2], column[b][:, 0:1], derived[b][:, 0:1], ALU.mult)\
                        .then_inc(derived_ready, 1)
                    pool.tensor_tensor(derived[b][:, 2:3], column[b][:, 0:1], column[b][:, 1:2], ALU.mult)\
                        .then_inc(derived_ready, 1)

                def add_sines(p, b, which):
                    pool.wait_ge(plain_done, 6 * p + 2 * which + 2)
                    pool.wait_ge(cross_done, 4 * p + 2 * which + 2)
                    dst = (qT, kT)[which][b]
                    pool.tensor_tensor(dst[:], dst[:], cross[which][:], ALU.add)\
                        .then_inc(qk_ready, 1)

                def normalise(h, n, first):
                    pool.wait_ge(inverse_ready, BATCH * h + n + 1)
                    if not (first and n < 2):
                        pool.wait_ge(turned, BATCH * h + n - 1)
                    for j, (lo, hi) in enumerate(((0, P), (P, 3 * P))):
                        last = pool.tensor_tensor(prob[n % 2][:, lo:hi], e[n % 2][:, lo:hi],
                                                  inverse[:, n, j:j + 1].broadcast_to([P, hi - lo]), ALU.mult)
                    last.then_inc(prob_ready, 1)

                def prologue():
                    pool.memset(mask[:], 0.0).then_inc(mask_step, 1)
                    pool.wait_ge(mask_step, 1)
                    for lo in (0, 2 * P):
                        pool.affine_select(out=mask[:, lo:lo + P], in_=mask[:, lo:lo + P], compare_op=ALU.is_ge,
                                           fill=MASKED, base=0, pattern=[[-1, P]], channel_multiplier=1)\
                            .then_inc(mask_step, 1)
                    for c in cross:
                        pool.memset(c[0:X0, :], 0.0).then_inc(mask_step, 1)
                        pool.wait_ge(mask_step, 4 + cross.index(c))
                    pool.wait_ge(small_loaded, 16)
                    derive(0, 0, 0, True)
                    derive(1, 1, 0, True)
                    add_sines(0, 0, 0)
                    add_sines(0, 0, 1)

                def step(h, b, first, more):
                    normalise(h, 0, first)
                    normalise(h, 1, first)
                    if more:
                        add_sines(h + 1, 1 - b, 0)
                    normalise(h, 2, first)
                    if more:
                        add_sines(h + 1, 1 - b, 1)
                    normalise(h, 3, first)

                prologue()
                step(0, 0, True, True)
                with pool.Fori(1, HEADS1 // 2) as i:
                    derive(2 * i, 0, i, False)
                    step(2 * i - 1, 1, False, True)
                    derive(2 * i + 1, 1, i, False)
                    step(2 * i, 0, False, True)
                step(HEADS1 - 1, 1, False, False)
        wide_project_stage(nc, core, "l1_project", oT, w_out, b_out, HEADS1)


F2, SHARED2 = 96, 2
EXPERTS2, TOP2, CAPACITY2 = 64, 6, 64
HEADS2 = 16
DH2 = 128
TAPS = 4
CHUNKS2 = SEQ // P
LOG_A, NEG_B, B, NEG_BG, TO_END, FROM_START = range(6)
COLUMNS = 6


def l2_decay_stage(nc, core, weights, bias, table_out):
    with Stage(nc, "decay") as st:
        w = st.sb("w", [P, KC, 2 * HEADS2])
        row = st.sb("row", [P, 2 * HEADS2])
        z = st.sb("z", [P, TILES, 2 * HEADS2])
        size = st.sb("size", [P, TILES, HEADS2])
        log_a = st.sb("log_a", [P, TILES, HEADS2])
        b = st.sb("b", [P, TILES, HEADS2])
        sums = st.sb("sums", [P, 3, TILES, HEADS2])
        ps = st.ps("ps", [P, TILES, 2 * HEADS2])
        ps_sums = st.ps("ps_sums", [P, 3, TILES, HEADS2])
        table = st.sb("table", [P, HEADS2, COLUMNS, TILES])
        table_ready = st.sem("table_ready")
        stored = st.sem("stored")
        loaded = st.sem("loaded")
        projected = st.sem("projected")
        z_ready = st.sem("z_ready")
        b_ready = st.sem("b_ready")
        act_step = st.sem("act_step")
        log_ready = st.sem("log_ready")
        summed = st.sem("summed")
        exp_ready = st.sem("exp_ready")
        step_done = st.sem("step_done")
        block = st.block()

        @block.sync
        def _(sp):
            sp.dma_start(w[:], weights.rearrange("(c p) n -> p c n", p=P)).then_inc(loaded, 16)
            sp.dma_start(row[:], bias.partition_broadcast(P)).then_inc(loaded, 16)
            sp.wait_ge(table_ready, COLUMNS)
            sp.dma_start(table_out, table[:]).then_inc(stored, 16)
            sp.wait_ge(stored, 16)

        @block.tensor
        def _(pe):
            pe.wait_ge(loaded, 32)
            for t in range(TILES):
                for c in range(KC):
                    mm = pe.matmul(ps[:, t, :], core.xnT[:, c, t * P:(t + 1) * P], w[:, c, :],
                                   start=(c == 0), stop=(c == KC - 1))
            mm.then_inc(projected, 1)
            pe.wait_ge(log_ready, 1)
            for i, m in enumerate((core.before, core.after, core.upto)):
                mm = pe.matmul(ps_sums[:, i].rearrange("p t h -> p (t h)"), m[:],
                               log_a[:].rearrange("p t h -> p (t h)"), start=True, stop=True)
            mm.then_inc(summed, 1)

        @block.scalar
        def _(act):
            act.wait_ge(z_ready, 1)
            act.activation(b[:], z[:, :, HEADS2:], ACT.Sigmoid).then_inc(b_ready, 1)
            act.activation(size[:], z[:, :, 0:HEADS2], ACT.Abs).then_inc(act_step, 1)
            act.wait_ge(act_step, 1)
            act.activation(size[:], size[:], ACT.Exp, scale=-1.0).then_inc(act_step, 1)
            act.wait_ge(act_step, 2)
            act.activation(size[:], size[:], ACT.Ln, bias=core.ones[:, 0:1]).then_inc(act_step, 1)
            act.wait_ge(summed, 1)
            act.activation(sums[:], ps_sums[:], ACT.Exp).then_inc(exp_ready, 1)

        @block.vector
        def _(dve):
            steps = [0]

            def link(ins):
                steps[0] += 1
                ins.then_inc(step_done, 1)
                dve.wait_ge(step_done, steps[0])

            def column(k):
                return table[:, :, k, :].rearrange("p h t -> p t h")

            dve.wait_ge(loaded, 32)
            dve.wait_ge(projected, 1)
            dve.tensor_tensor(z[:], ps[:], row[:].unsqueeze(1).broadcast_to([P, TILES, 2 * HEADS2]), ALU.add)\
                .then_inc(z_ready, 1)
            dve.wait_ge(z_ready, 1)
            link(dve.tensor_scalar(log_a[:], z[:, :, 0:HEADS2], 0.0, None, ALU.min))
            dve.wait_ge(act_step, 3)
            dve.tensor_tensor(log_a[:], log_a[:], size[:], ALU.subtract).then_inc(log_ready, 1)
            dve.wait_ge(log_ready, 1)
            dve.tensor_copy(column(LOG_A), log_a[:]).then_inc(table_ready, 1)
            dve.wait_ge(b_ready, 1)
            dve.tensor_copy(column(B), b[:]).then_inc(table_ready, 1)
            dve.tensor_scalar(column(NEG_B), b[:], -1.0 / DH2, None, ALU.mult).then_inc(table_ready, 1)
            dve.wait_ge(exp_ready, 1)
            dve.scalar_tensor_tensor(out=column(NEG_BG), in0=sums[:, 0], scalar=-1.0 / DH2, in1=b[:],
                                     op0=ALU.mult, op1=ALU.mult).then_inc(table_ready, 1)
            dve.tensor_copy(column(TO_END), sums[:, 1]).then_inc(table_ready, 1)
            dve.tensor_scalar(column(FROM_START), sums[:, 2], float(DH2) ** -0.5, None, ALU.mult)\
                .then_inc(table_ready, 1)


def l2_heads_stage(nc, core, w_heads, conv_heads, table, ln_w, ln_b, oT):
    LEVELS = 6
    BK = P // 2
    TOP, LOW = slice(0, BK), slice(BK, P)
    SY = BATCH
    PAD = TAPS - 1
    Q, K, V, G = range(4)
    FILLS = [[9, 9, 9], [10, 8, 9]]
    with Stage(nc, "l2_heads") as st:
        w = [st.sb(f"w{b}", [P, 4, KC, DH2]) for b in range(2)]
        conv = [st.sb(f"conv{b}", [P, 3, TAPS + 1]) for b in range(2)]
        col = [st.sb(f"col{b}", [P, COLUMNS, TILES]) for b in range(2)]
        gain = st.sb("gain", [P, DH2])
        offset = st.sb("offset", [P, DH2])
        upto_scaled = st.sb("upto_scaled", [P, P])
        padded = [st.sb(f"padded{i}", [P, BATCH, PAD + SEQ]) for i in range(3)]
        taps = [st.sb(f"taps{i}", [P, BATCH, SEQ]) for i in range(3)]
        feat = [[st.sb(f"feat{i}{b}", [P, TOKENS]) for b in range(2)] for i in range(2)]
        feat.append([st.sb("feat2", [P, TOKENS])] * 2)
        gate = [st.sb(f"gate{b}", [P, TILES, DH2]) for b in range(2)]
        e1 = [st.sb(f"e1{c}", [P, SY, P]) for c in range(2)]
        e2 = [st.sb(f"e2{c}", [P, SY, P]) for c in range(2)]
        la_before, la_upto = e1, e2
        m_first = [st.sb(f"m_first{c}", [P, SY, P]) for c in range(2)]
        m_stacked = [st.sb(f"m_stacked{c}", [P, SY, BK]) for c in range(2)]
        m_whole = [st.sb(f"m_whole{c}", [P, SY, P]) for c in range(2)]
        mt_whole = [st.sb(f"mt_whole{c}", [P, SY, P]) for c in range(2)]
        y_stacked = [st.sb(f"y_stacked{c}", [P, SY, BK]) for c in range(2)]
        Y = [st.sb(f"y{c}", [P, SY, P]) for c in range(2)]
        yt_a = [st.sb(f"yt_a{c}", [BK, SY, BK]) for c in range(2)]
        cy_b = [st.sb(f"cy_b{c}", [BK, SY, BK]) for c in range(2)]
        qk = [st.sb(f"qk{c}", [P, SY, P]) for c in range(2)]
        bv = [st.sb(f"bv{c}", [P, SY, DH2]) for c in range(2)]
        k_end = st.sb("k_end", [P, SY, DH2])
        o_state = k_end
        r = bv[1]
        u = [st.sb(f"u{c}", [P, SY, DH2]) for c in range(2)]
        state = st.sb("state", [P, SY, DH2])
        o = st.sb("o", [P, TILES, DH2])
        on = st.sb("on", [P, TILES, DH2])
        stats = st.sb("stats", [P, TILES, 6])
        mean_var = st.sb("mean_var", [P, TILES, 2])
        sd = st.sb("sd", [P, TILES])
        rstd = st.sb("rstd", [P, TILES])
        spare = st.sb("spare", [P, 1])
        o_head = st.sb("o_head", [P, TOKENS])
        ps_p = [st.ps(f"ps_p{i}", [P, HALF]) for i in range(2)]
        bank = [[st.ps(f"bank{c}{i}", [P, SY, P]) for i in range(3)] for c in range(2)]

        rows_loaded = st.sem("rows_loaded")
        pool_step = st.sem("pool_step")
        w_loaded = [st.sem(f"w_loaded{b}") for b in range(2)]
        col_loaded = [st.sem(f"col_loaded{b}") for b in range(2)]
        p_filled = [st.sem(f"p_filled{i}") for i in range(2)]
        p_read = [st.sem(f"p_read{i}") for i in range(2)]
        filled = [[st.sem(f"filled{c}{i}") for i in range(3)] for c in range(2)]
        read = [[st.sem(f"read{c}{i}") for i in range(3)] for c in range(2)]
        padded_ready = st.sem("padded_ready")
        conv_step = st.sem("conv_step")
        feat_ready = st.sem("feat_ready")
        la_ready = st.sem("la_ready")
        exp1_ready = [st.sem(f"exp1_ready{c}") for c in range(2)]
        exp2_ready = [st.sem(f"exp2_ready{c}") for c in range(2)]
        e1_ready = [st.sem(f"e1_ready{c}") for c in range(2)]
        e2_ready = [st.sem(f"e2_ready{c}") for c in range(2)]
        m0_ready = [st.sem(f"m0_ready{c}") for c in range(2)]
        y0_ready = [st.sem(f"y0_ready{c}") for c in range(2)]
        whole_ready = [st.sem(f"whole_ready{c}") for c in range(2)]
        stats_ready = st.sem("stats_ready")
        mean_ready = st.sem("mean_ready")
        sd_ready = st.sem("sd_ready")
        rstd_ready = st.sem("rstd_ready")
        on_ready = st.sem("on_ready")
        gained = st.sem("gained")
        o_stored = st.sem("o_stored")
        block = st.block()

        def nth(c, i, h, k):
            return FILLS[c][i] * h + k + 1

        def p_use(h, k, more):
            if isinstance(h, int) and h == -1:
                return {0: 1, 1: 2, 2: 3, 4: 4}[k]
            if isinstance(h, int) and h == 0:
                return 4 + {0: 1, 1: 2, 2: 3, 4: 4}[k]
            return 5 * h + 3 + (k + 1 if more else k - 2)

        def tile_of(c, s):
            return CHUNKS2 * s + c

        def columns(b, k, c):
            return col[b][:, k, :].rearrange("p (s c) -> p c s", c=CHUNKS2)[:, c, :]

        def tiles(ap, c):
            return ap.rearrange("p (s c) d -> p c s d", c=CHUNKS2)[:, c]

        def along(m):
            return m[:].unsqueeze(1).broadcast_to([P, SY, P])

        def blocks(half):
            return core.ident[half, half].unsqueeze(1).broadcast_to([BK, SY, BK])

        def flat(ap):
            return ap.rearrange("p s n -> p (s n)")

        POOL_STEPS = 4 + 6

        def over_heads(eng, prologue, step, epilogue):
            prologue()
            step(0, 0, 0, True, True)
            with eng.Fori(1, HEADS2 // 2) as i:
                step(2 * i - 1, i - 1, 1, False, True)
                step(2 * i, i, 0, False, True)
            step(HEADS2 - 1, HEADS2 // 2 - 1, 1, False, False)
            epilogue()

        @block.sync
        def _(sp):
            sp.dma_start(gain[:], ln_w.partition_broadcast(P)).then_inc(rows_loaded, 16)
            sp.dma_start(offset[:], ln_b.partition_broadcast(P)).then_inc(rows_loaded, 16)

            def load(p, b, waits):
                head = bass.ds(p, 1)
                if waits is not None:
                    sp.wait_ge(conv_step, 9 * (p - 1))
                sp.dma_start(w[b][:, 0:3], w_heads[head, :, 0:3].rearrange("a p w c n -> (a p) w c n"))\
                    .then_inc(w_loaded[b], 16)
                sp.dma_start(conv[b][:], conv_heads[head].rearrange("a p w t -> (a p) w t"))\
                    .then_inc(w_loaded[b], 16)
                if waits is not None:
                    sp.wait_ge(p_read[1], waits)
                sp.dma_start(w[b][:, 3:4], w_heads[head, :, 3:4].rearrange("a p w c n -> (a p) w c n"))\
                    .then_inc(w_loaded[b], 16)

            def load_columns(p, b, first):
                if not first:
                    sp.wait_ge(read[1][0], FILLS[1][0] * (p - 1))
                sp.dma_start(col[b][:].rearrange("p k t -> p (k t)"),
                             table[:, bass.ds(p, 1)].rearrange("p a k t -> p (a k t)")).then_inc(col_loaded[b], 16)

            def store_o(use, h):
                sp.wait_ge(p_read[1], use)
                sp.dma_start(oT[:, bass.ds(h, 1), :].rearrange("p a n -> p (a n)"), o_head[:])\
                    .then_inc(o_stored, 16)

            def during(h, b, more=True):
                if more:
                    load_columns(h + 1, 1 - b, False)
                store_o(p_use(h, 3, more), h - 1)

            load_columns(0, 0, True)
            load(0, 0, None)
            load(1, 1, None)
            load_columns(1, 1, True)
            load(2, 0, p_use(-1, 4, True))
            load(3, 1, p_use(0, 4, True))
            with sp.Fori(1, HEADS2 // 2 - 1) as i:
                during(2 * i - 1, 1)
                load(2 * i + 2, 0, p_use(2 * i - 1, 4, True))
                during(2 * i, 0)
                load(2 * i + 3, 1, p_use(2 * i, 4, True))
            during(HEADS2 - 3, 1)
            during(HEADS2 - 2, 0)
            during(HEADS2 - 1, 1, False)
            store_o(p_use(HEADS2 - 1, 3, False) + 1, HEADS2 - 1)
            sp.wait_ge(o_stored, 16 * HEADS2)

        @block.tensor
        def _(pe):
            def fill(c, i, h, k, products):
                if not (isinstance(h, int) and h == 0 and k == 0):
                    pe.wait_ge(read[c][i], nth(c, i, h, k) - 1)
                for out, lhsT, rhs in products:
                    last = (pe.transpose(out, lhsT, core.ident[:]) if rhs is None
                            else pe.matmul(out, lhsT, rhs, start=True, stop=True))
                last.then_inc(filled[c][i], 1)

            def project(p, i, b, h, which, halves=(0, 1)):
                use = p_use(h, which if which < G else 4, True)
                if which == Q:
                    pe.wait_ge(w_loaded[b], 48 * (i + 1))
                for half in halves:
                    if not (isinstance(use, int) and use == 1):
                        pe.wait_ge(p_read[half], use - 1)
                    if which < G:
                        for c in range(KC):
                            mm = pe.matmul(ps_p[half][:], w[b][:, which, c, :],
                                           core.xnT[:, c, half * HALF:(half + 1) * HALF],
                                           start=(c == 0), stop=(c == KC - 1))
                    else:
                        for j in range(4):
                            t = 4 * half + j
                            for c in range(KC):
                                mm = pe.matmul(ps_p[half][:, j * P:(j + 1) * P],
                                               core.xnT[:, c, t * P:(t + 1) * P], w[b][:, G, c, :],
                                               start=(c == 0), stop=(c == KC - 1))
                    mm.then_inc(p_filled[half], 1)

            def turn_o(h_step, h, more):
                pe.wait_ge(gained, 3 * (h + 1))
                use = p_use(h_step, 3, more)
                for half in range(2):
                    pe.wait_ge(p_read[half], use - 1)
                    for j in range(4):
                        tr = pe.transpose(ps_p[half][:, j * P:(j + 1) * P], on[:, 4 * half + j, :], core.ident[:])
                    tr.then_inc(p_filled[half], 1)

            def cols(ap, c, s):
                t = tile_of(c, s)
                return ap[:, t * P:(t + 1) * P]

            def prologue():
                for which in range(4):
                    project(0, 0, 0, -1, which)

            def step(h, i, b, first, more):
                q, k, v = (feat[x][b] for x in range(3))
                nxt = (h + 1, (i + b), 1 - b, h)
                S = range(SY)
                pe.wait_ge(la_ready, 4 * h + 4)
                for c in range(2):
                    fill(c, 1, h, 0, [(bank[c][1][:, s, :], la_before[c][:, s, :], core.after[:]) for s in S])
                    fill(c, 2, h, 0, [(flat(bank[c][2][:]), core.after[:], flat(la_upto[c][:]))])
                    if c == 0:
                        pe.wait_ge(feat_ready, 3 * h + 3)
                    fill(c, 0, h, 0, [(bank[c][0][:, s, :], cols(k, c, s), cols(k, c, s)) for s in S])
                if more:
                    project(*nxt, Q)
                for c in range(2):
                    fill(c, 1, h, 1, [(bank[c][1][:, s, :], cols(k, c, s), cols(q, c, s)) for s in S])
                for c in range(2):
                    fill(c, 0, h, 1, [(bank[c][0][:, s, :], m_first[c][:, s, :], None) for s in S])
                    fill(c, 2, h, 1, [(bank[c][2][:, s, :], cols(v, c, s), None) for s in S])
                fill(0, 1, h, 2, [(bank[0][1][:, s, :], cols(k, 0, s), None) for s in S])
                before_turns = {1: (K, 0), 2: (V, 0), 3: (V, 1)}
                for n in range(1, LEVELS):
                    for c in range(2):
                        if n == 1:
                            pe.wait_ge(m0_ready[c], h + 1)
                            pe.wait_ge(read[c][0], nth(c, 0, h, 1))
                        else:
                            pe.wait_ge(read[c][1], nth(c, 1, h, (1 if c else 2) + n - 1))
                        fill(c, 0, h, 1 + n, [(bank[c][0][:, s, 0:BK], mt_whole[c][:, s, :], m_stacked[c][:, s, :])
                                              for s in S])
                    if n in before_turns and more:
                        project(*nxt, before_turns[n][0], (before_turns[n][1],))
                    if n == 4 and not first:
                        turn_o(h, h - 1, more)
                    for c in range(2):
                        if n < LEVELS - 1:
                            pe.wait_ge(whole_ready[c], (LEVELS - 2) * h + n)
                            fill(c, 1, h, (1 if c else 2) + n,
                                 [(bank[c][1][:, s, :], m_whole[c][:, s, :], None) for s in S])
                        else:
                            pe.wait_ge(read[c][0], nth(c, 0, h, 1 + n))
                        if n == 1:
                            pe.wait_ge(y0_ready[c], h + 1)
                        fill(c, 2, h, 1 + n, [(bank[c][2][:, s, 0:BK], m_whole[c][:, s, :], y_stacked[c][:, s, :])
                                              for s in S])
                    if n == 1 and more:
                        project(*nxt, K, (1,))
                for c in range(2):
                    pe.wait_ge(read[c][2], nth(c, 2, h, LEVELS))
                    pe.wait_ge(read[c][1], nth(c, 1, h, 6 if c else 7) - 1)
                    pe.wait_ge(read[c][0], nth(c, 0, h, 7) - 1)
                    for s in S:
                        tr = pe.transpose(bank[c][1][:, s, :], Y[c][:, s, :], core.ident[:])
                    tr.then_inc(filled[c][1], 1)
                    for s in S:
                        mm = pe.matmul(bank[c][0][TOP, s, 0:BK], m_first[c][LOW, s, TOP], Y[c][LOW, s, LOW],
                                       start=True, stop=True)
                    mm.then_inc(filled[c][0], 1)
                if more:
                    project(*nxt, G, (0,))
                for c in range(2):
                    pe.wait_ge(read[c][1], nth(c, 1, h, 6 if c else 7))
                    pe.wait_ge(read[c][0], nth(c, 0, h, 7))
                    pe.matmul(bank[c][2][:, 0, 0:1], core.ident[:], core.ident[:, 0:1], start=True, stop=True)
                    for s in S:
                        mm = pe.matmul(bank[c][2][TOP, s, 0:BK], yt_a[c][:, s, :], cy_b[c][:, s, :],
                                       start=True, stop=True)
                    mm.then_inc(filled[c][2], 1)
                if more:
                    project(*nxt, G, (1,))
                pe.wait_ge(read[0][2], nth(0, 2, h, 7))
                fill(0, 1, h, 8, [(bank[0][1][:, s, :], Y[0][:, s, :], bv[0][:, s, :]) for s in S])
                pe.wait_ge(read[0][1], nth(0, 1, h, 8))
                fill(0, 2, h, 8, [(bank[0][2][:, s, :], k_end[:, s, :], u[0][:, s, :]) for s in S])
                fill(0, 0, h, 8, [(bank[0][0][:, s, :], qk[0][:, s, :], u[0][:, s, :]) for s in S])
                pe.wait_ge(read[0][2], nth(0, 2, h, 8))
                fill(1, 0, h, 8, [(bank[1][0][:, s, :], cols(k, 1, s), state[:, s, :]) for s in S])
                fill(1, 2, h, 8, [(bank[1][2][:, s, :], cols(q, 1, s), state[:, s, :]) for s in S])
                pe.wait_ge(read[1][0], nth(1, 0, h, 8))
                fill(1, 1, h, 7, [(bank[1][1][:, s, :], Y[1][:, s, :], r[:, s, :]) for s in S])
                pe.wait_ge(read[1][1], nth(1, 1, h, 7))
                fill(1, 0, h, 9, [(bank[1][0][:, s, :], qk[1][:, s, :], u[1][:, s, :]) for s in S])

            def epilogue():
                pe.wait_ge(gained, 3 * HEADS2)
                use = p_use(HEADS2 - 1, 3, False) + 1
                for half in range(2):
                    pe.wait_ge(p_read[half], use - 1)
                    for j in range(4):
                        tr = pe.transpose(ps_p[half][:, j * P:(j + 1) * P], on[:, 4 * half + j, :], core.ident[:])
                    tr.then_inc(p_filled[half], 1)

            over_heads(pe, prologue, step, epilogue)

        @block.scalar
        def _(act):
            def take(p, b, h, which, halves=(0, 1)):
                use = p_use(h, which, True)
                if not (isinstance(h, int) and h == -1):
                    act.wait_ge(conv_step, 9 * (p - 1) + 3 * which + 3)
                for half in halves:
                    act.wait_ge(p_filled[half], use)
                    src = ps_p[half][:].rearrange("p (s n) -> p s n", n=SEQ)
                    act.copy(padded[which][:, 2 * half:2 * half + 2, PAD:], src).then_inc(padded_ready, 1)
                    act.activation(taps[which][:, 2 * half:2 * half + 2, :], src, ACT.Identity,
                                   bias=conv[b][:, which, TAPS:TAPS + 1],
                                   scale=conv[b][:, which, TAPS - 1:TAPS]).then_inc(p_read[half], 1)

            def silu(p, b, which, first):
                act.wait_ge(conv_step, 9 * p + 3 * which + 3)
                if not first:
                    act.wait_ge(filled[1][0], FILLS[1][0] * (p - 1))
                act.activation(feat[which][b][:], taps[which][:].rearrange("p s n -> p (s n)"), ACT.Silu)\
                    .then_inc(feat_ready, 1)

            def take_gate(p, b, h, first, halves=(0, 1)):
                if not first:
                    act.wait_ge(gained, 3 * (p - 1))
                for half in halves:
                    act.wait_ge(p_filled[half], p_use(h, 4, True))
                    act.activation(gate[b][:, 4 * half:4 * half + 4, :].rearrange("p t n -> p (t n)"),
                                   ps_p[half][:], ACT.Sigmoid).then_inc(p_read[half], 1)

            def take_o(use, stored):
                if stored is not None:
                    act.wait_ge(o_stored, 16 * stored)
                for half in range(2):
                    act.wait_ge(p_filled[half], use)
                    act.copy(o_head[:, half * HALF:(half + 1) * HALF], ps_p[half][:]).then_inc(p_read[half], 1)

            def scaled_copies(c, i, h, k, dst, b, column):
                act.wait_ge(filled[c][i], nth(c, i, h, k))
                for s in range(SY):
                    last = act.activation(dst[:, s, :], bank[c][i][:, s, :], ACT.Copy,
                                          scale=columns(b, column, c)[:, s:s + 1])
                last.then_inc(read[c][i], 1)

            def take_copy(c, i, h, k, dst):
                act.wait_ge(filled[c][i], nth(c, i, h, k))
                act.copy(flat(dst[:]), flat(bank[c][i][:])).then_inc(read[c][i], 1)

            def prologue():
                act.wait_ge(pool_step, POOL_STEPS)
                act.wait_ge(w_loaded[0], 48)
                for which in range(3):
                    take(0, 0, -1, which)
                take_gate(0, 0, -1, True)
                for which in range(3):
                    silu(0, 0, which, True)

            def step(h, i, b, first, more):
                for c in range(2):
                    act.wait_ge(filled[c][1], nth(c, 1, h, 0))
                    act.activation(flat(e1[c][:]), flat(bank[c][1][:]), ACT.Exp).then_inc(read[c][1], 1)
                    act.wait_ge(filled[c][2], nth(c, 2, h, 0))
                    act.activation(flat(e2[c][:]), flat(bank[c][2][:]), ACT.Exp).then_inc(read[c][2], 1)
                if more:
                    act.wait_ge(w_loaded[1 - b], 48 * (i + b + 1))
                    take(h + 1, 1 - b, h, Q)
                for c in range(2):
                    act.wait_ge(filled[c][0], nth(c, 0, h, 1))
                    act.copy(mt_whole[c][TOP, :, TOP], bank[c][0][TOP, :, TOP])
                    act.copy(mt_whole[c][LOW, :, LOW], bank[c][0][LOW, :, LOW]).then_inc(read[c][0], 1)
                act.wait_ge(col_loaded[b], 16 * (i + 1))
                for c in range(2):
                    if not first:
                        act.wait_ge(filled[c][1], FILLS[c][1] * h)
                    scaled_copies(c, 2, h, 1, bv[c], b, B)
                if not first:
                    act.wait_ge(read[1][0], FILLS[1][0] * h)
                scaled_copies(0, 1, h, 2, k_end, b, TO_END)
                if not first:
                    act.wait_ge(mean_ready, h)
                    act.activation(sd[:], mean_var[:, :, 1], ACT.Sqrt, bias=core.norm_eps[:]).then_inc(sd_ready, 1)
                takes = {1: (K, 0), 2: (V, 0), 3: (V, 1)}
                for n in range(1, LEVELS - 1):
                    if n in takes and more:
                        take(h + 1, 1 - b, h, takes[n][0], (takes[n][1],))
                    if n == 4 and not first:
                        use = p_use(h, 3, more)
                        take_o(use, h - 1)
                    for c in range(2):
                        take_copy(c, 1, h, (1 if c else 2) + n, mt_whole[c])
                    if n == 1 and more:
                        take(h + 1, 1 - b, h, K, (1,))
                if more:
                    silu(h + 1, 1 - b, Q, first)
                    silu(h + 1, 1 - b, K, first)
                for c in range(2):
                    act.wait_ge(filled[c][1], nth(c, 1, h, 6 if c else 7))
                    act.copy(yt_a[c][:], bank[c][1][TOP, :, 0:BK]).then_inc(read[c][1], 1)
                if more:
                    silu(h + 1, 1 - b, V, first)
                for c in range(2):
                    act.wait_ge(filled[c][2], nth(c, 2, h, 7))
                    act.copy(Y[c][TOP, :, LOW], bank[c][2][TOP, :, 0:BK]).then_inc(read[c][2], 1)
                if more:
                    take_gate(h + 1, 1 - b, h, first, (0,))
                take_copy(0, 1, h, 8, u[0])
                take_copy(0, 2, h, 8, state)
                if more:
                    take_gate(h + 1, 1 - b, h, first, (1,))
                scaled_copies(1, 2, h, 8, o_state, b, FROM_START)
                take_copy(1, 1, h, 7, u[1])

            def epilogue():
                use = p_use(HEADS2 - 1, 3, False) + 1
                act.wait_ge(mean_ready, HEADS2)
                act.activation(sd[:], mean_var[:, :, 1], ACT.Sqrt, bias=core.norm_eps[:]).then_inc(sd_ready, 1)
                take_o(use, HEADS2 - 1)

            over_heads(act, prologue, step, epilogue)

        @block.vector
        def _(dve):
            def convolve(p, b, which, earlier=range(TAPS - 1)):
                if earlier[0] == 0:
                    dve.wait_ge(p_read[1], conv_use[0](which))
                for j in earlier:
                    n = 9 * p + 3 * which + j
                    if j > 0:
                        dve.wait_ge(conv_step, n)
                    dve.scalar_tensor_tensor(out=taps[which][:], in0=padded[which][:, :, j:j + SEQ],
                                             scalar=conv[b][:, which, j:j + 1], in1=taps[which][:],
                                             op0=ALU.mult, op1=ALU.add).then_inc(conv_step, 1)

            def moments(h):
                for t in range(TILES):
                    last = dve.bn_stats(stats[:, t, :], o[:, t, :])
                last.then_inc(stats_ready, 1)
                dve.wait_ge(stats_ready, h + 1)
                dve.memset(spare[:], 0.0)
                for t in range(TILES):
                    last = dve.bn_aggr(mean_var[:, t, :], stats[:, t, :])
                last.then_inc(mean_ready, 1)

            def normalise(h, use):
                dve.wait_ge(sd_ready, h + 1)
                dve.reciprocal(rstd[:], sd[:]).then_inc(rstd_ready, 1)
                dve.wait_ge(rstd_ready, h + 1)
                if use is not None:
                    dve.wait_ge(p_filled[1], use)
                for t in range(TILES):
                    last = dve.tensor_scalar(on[:, t, :], o[:, t, :], mean_var[:, t, 0:1], rstd[:, t:t + 1],
                                             ALU.subtract, ALU.mult)
                last.then_inc(on_ready, 1)

            conv_use = [None]

            def prologue():
                dve.wait_ge(pool_step, POOL_STEPS)
                conv_use[0] = lambda which: p_use(-1, which, True)
                for which in range(3):
                    convolve(0, 0, which)

            def step(h, i, b, first, more):
                conv_use[0] = lambda which: p_use(h, which, more)
                dve.wait_ge(col_loaded[b], 16 * (i + 1))
                for c in range(2):
                    dve.wait_ge(e1_ready[c], h + 1)
                    dve.wait_ge(filled[c][0], nth(c, 0, h, 0))
                    for s in range(SY):
                        last = dve.scalar_tensor_tensor(out=m_first[c][:, s, :], in0=bank[c][0][:, s, :],
                                                        scalar=columns(b, NEG_B, c)[:, s:s + 1],
                                                        in1=e1[c][:, s, :], op0=ALU.mult, op1=ALU.mult)
                    last.then_inc(read[c][0], 1)
                for c in range(2):
                    dve.wait_ge(read[c][0], nth(c, 0, h, 0))
                    dve.tensor_copy(m_stacked[c][TOP], m_first[c][TOP, :, TOP])
                    dve.tensor_copy(m_stacked[c][LOW], m_first[c][LOW, :, LOW]).then_inc(m0_ready[c], 1)
                if not first:
                    dve.wait_ge(read[1][0], FILLS[1][0] * (h - 1) + 10)
                    moments(h - 1)
                for c in range(2):
                    dve.wait_ge(e2_ready[c], h + 1)
                    dve.wait_ge(filled[c][1], nth(c, 1, h, 1))
                    dve.tensor_tensor(flat(qk[c][:]), flat(bank[c][1][:]), flat(e2[c][:]), ALU.mult)\
                        .then_inc(read[c][1], 1)
                for c in range(2):
                    dve.wait_ge(read[c][0], nth(c, 0, h, 1))
                    dve.tensor_tensor(y_stacked[c][TOP], mt_whole[c][TOP, :, TOP], blocks(TOP), ALU.add)
                    dve.tensor_tensor(y_stacked[c][LOW], mt_whole[c][LOW, :, LOW], blocks(LOW), ALU.add)\
                        .then_inc(y0_ready[c], 1)
                before_y = {2: (Q, 1), 3: (K, 0), 4: (K, 2), 5: (V, 1)}
                after_y = {1: (Q, 0), 2: (Q, 2), 3: (K, 1), 4: (V, 0), 5: (V, 2)}
                for n in range(1, LEVELS):
                    for c in range(2):
                        dve.wait_ge(filled[c][0], nth(c, 0, h, 1 + n))
                        dve.tensor_copy(m_whole[c][TOP, :, TOP], bank[c][0][TOP, :, 0:BK])
                        whole = dve.tensor_copy(m_whole[c][LOW, :, LOW], bank[c][0][LOW, :, 0:BK])
                        if n < LEVELS - 1:
                            whole.then_inc(whole_ready[c], 1)
                            dve.tensor_copy(m_stacked[c][:], bank[c][0][:, :, 0:BK]).then_inc(read[c][0], 1)
                        else:
                            whole.then_inc(read[c][0], 1)
                    if n == 1 and not first:
                        normalise(h - 1, on_free[0])
                    if n in before_y and more:
                        which, tap = before_y[n]
                        convolve(h + 1, 1 - b, which, (tap,))
                    for c in range(2):
                        dve.wait_ge(filled[c][2], nth(c, 2, h, 1 + n))
                        if n > 1:
                            dve.wait_ge(read[c][2], nth(c, 2, h, n))
                        else:
                            dve.wait_ge(y0_ready[c], h + 1)
                        if n < LEVELS - 1:
                            dve.tensor_tensor(y_stacked[c][:], bank[c][2][:, :, 0:BK], y_stacked[c][:], ALU.add)\
                                .then_inc(read[c][2], 1)
                        else:
                            dve.tensor_tensor(Y[c][TOP, :, TOP], bank[c][2][TOP, :, 0:BK], y_stacked[c][TOP], ALU.add)
                            dve.tensor_tensor(Y[c][LOW, :, LOW], bank[c][2][LOW, :, 0:BK], y_stacked[c][LOW],
                                              ALU.add).then_inc(read[c][2], 1)
                    if more:
                        which, tap = after_y[n]
                        convolve(h + 1, 1 - b, which, (tap,))
                for c in range(2):
                    dve.wait_ge(filled[c][0], nth(c, 0, h, 7))
                    dve.tensor_copy(cy_b[c][:], bank[c][0][TOP, :, 0:BK]).then_inc(read[c][0], 1)
                dve.wait_ge(filled[0][0], nth(0, 0, h, 8))
                dve.tensor_copy(tiles(o[:], 0), bank[0][0][:]).then_inc(read[0][0], 1)
                dve.wait_ge(read[1][2], nth(1, 2, h, 1))
                dve.wait_ge(filled[1][0], nth(1, 0, h, 8))
                for s in range(SY):
                    last = dve.scalar_tensor_tensor(out=r[:, s, :], in0=bank[1][0][:, s, :],
                                                    scalar=columns(b, NEG_BG, 1)[:, s:s + 1],
                                                    in1=bv[1][:, s, :], op0=ALU.mult, op1=ALU.add)
                last.then_inc(read[1][0], 1)
                dve.wait_ge(read[1][2], nth(1, 2, h, 8))
                dve.wait_ge(filled[1][0], nth(1, 0, h, 9))
                dve.tensor_tensor(tiles(o[:], 1), bank[1][0][:], o_state[:], ALU.add).then_inc(read[1][0], 1)

            on_free = [None]
            prologue()
            step(0, 0, 0, True, True)
            on_free[0] = None
            step(1, 0, 1, False, True)
            on_free[0] = p_use(1, 3, True)
            step(2, 1, 0, False, True)
            with dve.Fori(2, HEADS2 // 2) as i:
                on_free[0] = p_use(2 * i - 2, 3, True)
                step(2 * i - 1, i - 1, 1, False, True)
                on_free[0] = p_use(2 * i - 1, 3, True)
                step(2 * i, i, 0, False, True)
            on_free[0] = p_use(HEADS2 - 2, 3, True)
            step(HEADS2 - 1, HEADS2 // 2 - 1, 1, False, False)
            dve.wait_ge(read[1][0], FILLS[1][0] * HEADS2)
            moments(HEADS2 - 1)
            normalise(HEADS2 - 1, p_use(HEADS2 - 1, 3, False))

        @block.gpsimd
        def _(pool):
            def prepare(h, i, b, first):
                pool.wait_ge(col_loaded[b], 16 * (i + 1))
                for c in range(2):
                    if not first:
                        pool.wait_ge(read[c][0], nth(c, 0, h - 1, 0))
                        pool.wait_ge(read[c][1], nth(c, 1, h - 1, 1))
                    la = columns(b, LOG_A, c).unsqueeze(2).broadcast_to([P, SY, P])
                    pool.tensor_tensor(la_before[c][:], along(core.before), la, ALU.mult).then_inc(la_ready, 1)
                    pool.tensor_tensor(la_upto[c][:], along(core.upto), la, ALU.mult).then_inc(la_ready, 1)

            def gate_o(h, b):
                every = [P, TILES, DH2]
                pool.wait_ge(on_ready, h + 1)
                pool.tensor_tensor(on[:], on[:], gain[:].unsqueeze(1).broadcast_to(every), ALU.mult)\
                    .then_inc(gained, 1)
                pool.wait_ge(gained, 3 * h + 1)
                pool.tensor_tensor(on[:], on[:], offset[:].unsqueeze(1).broadcast_to(every), ALU.add)\
                    .then_inc(gained, 1)
                pool.wait_ge(gained, 3 * h + 2)
                pool.tensor_tensor(on[:], on[:], gate[b][:], ALU.mult).then_inc(gained, 1)

            def prologue():
                for x in padded:
                    pool.memset(x[:, :, 0:PAD], 0.0).then_inc(pool_step, 1)
                pool.tensor_scalar(upto_scaled[:], core.upto[:], float(DH2) ** -0.5, None, ALU.mult)\
                    .then_inc(pool_step, 1)
                for c in range(2):
                    for m in (m_whole[c], mt_whole[c], Y[c]):
                        pool.memset(m[:], 0.0).then_inc(pool_step, 1)
                pool.wait_ge(pool_step, POOL_STEPS)
                pool.wait_ge(rows_loaded, 32)
                prepare(0, 0, 0, True)

            def step(h, i, b, first, more):
                for c in range(2):
                    pool.wait_ge(read[c][1], nth(c, 1, h, 0))
                    pool.tensor_tensor(e1[c][:], e1[c][:], along(core.after), ALU.mult).then_inc(e1_ready[c], 1)
                    pool.wait_ge(read[c][2], nth(c, 2, h, 0))
                    pool.tensor_tensor(e2[c][:], e2[c][:], along(upto_scaled), ALU.mult).then_inc(e2_ready[c], 1)
                if not first:
                    gate_o(h - 1, 1 - b)
                if more:
                    prepare(h + 1, i + b, 1 - b, False)

            def epilogue():
                gate_o(HEADS2 - 1, 1)

            over_heads(pool, prologue, step, epilogue)


def l2_attention(nc, core, table, w_gates, b_gates, w_heads, conv_heads, ln_w, ln_b, w_out):
    with ExitStack() as ctx:
        oT = ctx.enter_context(nc.sbuf_tensor("l2a_oT", [P, HEADS2, TOKENS], F32))
        l2_decay_stage(nc, core, w_gates, b_gates, table)
        l2_heads_stage(nc, core, w_heads, conv_heads, table, ln_w, ln_b, oT)
        wide_project_stage(nc, core, "l2_project", oT, w_out, None, HEADS2)


def l2_routed_stage(nc, core, name, xp, slot_of, weight_parts, in_weights, out_weights):
    EG = HALF // CAPACITY2
    GROUPS = EXPERTS2 // EG
    PAIRS = EG // 2
    PARTS = 3
    S = CAPACITY2
    with Stage(nc, name) as st:
        number = st.sb("number", [P, S], I32)
        slot = st.sb("slot", [P, S], BF16)
        w_in = [st.sb(f"w_in{b}", [P, EG, KC * 2 * F2]) for b in range(2)]
        w_out = [st.sb(f"w_out{b}", [F2, EG, D]) for b in range(2)]
        hot = [st.sb(f"hot{b}", [P, TILES, EG, S], BF16) for b in range(2)]
        hotT = st.sb("hotT", [P, PAIRS, TOKENS], BF16)
        xgT = st.sb("xgT", [P, KC, HALF])
        gate = st.sb("gate", [F2, HALF])
        hidden = st.sb("hidden", [F2, HALF])
        pair_weight = st.sb("pair_weight", [P, PAIRS, 2])
        slot_weight = st.sb("slot_weight", [P, PAIRS])
        eo = st.sb("eo", [P, PAIRS, D])
        eo_rest = st.sb("eo_rest", [P, PAIRS, D])
        ep = [st.sb(f"ep{i}", [P, PAIRS, D], BF16) for i in range(PARTS)]
        bank_x = [st.ps(f"bank_x{c}", [P, HALF]) for c in range(KC)]
        bank_g = st.ps("bank_g", [P, HALF])
        bank_u = st.ps("bank_u", [P, HALF])
        bank_t = st.ps("bank_t", [P, TOKENS], BF16)
        bank_e = st.ps("bank_e", [P, 2, D])
        bank_a = [st.ps(f"bank_a{i}", [P, 2, D]) for i in range(2)]

        const_ready = st.sem("const_ready")
        w_loaded = [st.sem(f"w_loaded{b}") for b in range(2)]
        hot_ready = st.sem("hot_ready")
        x_filled = st.sem("x_filled")
        x_read = [st.sem(f"x_read{c}") for c in range(KC)]
        up_filled = st.sem("up_filled")
        gate_ready = st.sem("gate_ready")
        hidden_ready = st.sem("hidden_ready")
        t_filled = st.sem("t_filled")
        t_read = st.sem("t_read")
        e_filled = st.sem("e_filled")
        e_read = st.sem("e_read")
        slot_weight_ready = st.sem("slot_weight_ready")
        eo_ready = st.sem("eo_ready")
        part0_ready = st.sem("part0_ready")
        rest_ready = st.sem("rest_ready")
        part1_ready = st.sem("part1_ready")
        part2_ready = st.sem("part2_ready")
        a_filled = [st.sem(f"a_filled{i}") for i in range(2)]
        a_read = [st.sem(f"a_read{i}") for i in range(2)]
        block = st.block()

        def over_groups(eng, prologue, step):
            prologue()
            step(0, 0, 0, True, False)
            with eng.Fori(1, GROUPS // 2) as i:
                step(2 * i - 1, i - 1, 1, False, False)
                step(2 * i, i, 0, False, False)
            step(GROUPS - 1, GROUPS // 2 - 1, 1, False, True)

        @block.sync
        def _(sp):
            def load(g, b, first):
                if not first:
                    sp.wait_ge(e_filled, 3 * (g - 1))
                sp.dma_start(w_in[b][:], in_weights[bass.ds(g * EG, EG)].rearrange("e p c g f -> p e (c g f)"))\
                    .then_inc(w_loaded[b], 16)
                sp.dma_start(w_out[b][:], out_weights[bass.ds(g * EG, EG)].rearrange("e f d -> f e d"))\
                    .then_inc(w_loaded[b], 16)

            load(0, 0, True)
            load(1, 1, True)
            with sp.Fori(1, GROUPS // 2) as i:
                load(2 * i, 0, False)
                load(2 * i + 1, 1, False)

        @block.tensor
        def _(pe):
            def gather(g, b, first, c, tiles):
                if tiles[0] == 0 and not first:
                    pe.wait_ge(hot_ready, TILES * (g + 1))
                    pe.wait_ge(x_read[c], g)
                for t in tiles:
                    if first and c == 0:
                        pe.wait_ge(hot_ready, t + 1)
                    for i in range(PARTS):
                        mm = pe.matmul(bank_x[c][:], xp[i][:, t, c * P:(c + 1) * P],
                                       hot[b][:, t].rearrange("p e s -> p (e s)"),
                                       start=(t == 0 and i == 0), stop=(t == TILES - 1 and i == PARTS - 1))
                if tiles[-1] == TILES - 1:
                    mm.then_inc(x_filled, 1)

            def turn_hot(g, b, first, q):
                if not (first and q == 0):
                    pe.wait_ge(t_read, PAIRS * g + q)
                for t in range(TILES):
                    tr = pe.transpose(bank_t[:, t * P:(t + 1) * P],
                                      hot[b][:, t, 2 * q:2 * q + 2, :].rearrange("p e s -> p (e s)"),
                                      core.ident_bf16[:])
                tr.then_inc(t_filled, 1)

            def down(g, b, q):
                if q == 0:
                    pe.wait_ge(hidden_ready, g + 1)
                    pe.wait_ge(e_read, g + 1)
                if q == 2:
                    pe.wait_ge(eo_ready, PAIRS * g + 2)
                for j in range(2):
                    e = 2 * q + j
                    mm = pe.matmul(bank_e[j * S:(j + 1) * S, q % 2, :], hidden[:, e * S:(e + 1) * S],
                                   w_out[b][:, e, :], start=True, stop=True)
                if q % 2 == 1:
                    mm.then_inc(e_filled, 1)

            def prologue():
                pe.wait_ge(const_ready, 2)
                for c in range(KC):
                    gather(0, 0, True, c, range(TILES))

            def step(g, i, b, first, last):
                pe.wait_ge(w_loaded[b], 32 * (i + 1))
                for c in range(KC):
                    pe.wait_ge(x_read[c], g + 1)
                if not first:
                    pe.wait_ge(hidden_ready, g)
                for e in range(EG):
                    for j, bank in enumerate((bank_g, bank_u)):
                        for c in range(KC):
                            at = (2 * c + j) * F2
                            mm = pe.matmul(bank[0:F2, e * S:(e + 1) * S], w_in[b][:, e, at:at + F2],
                                           xgT[:, c, e * S:(e + 1) * S], start=(c == 0), stop=(c == KC - 1))
                mm.then_inc(up_filled, 1)
                if not first:
                    pe.wait_ge(eo_ready, PAIRS * g)
                for q in range(PAIRS):
                    for t in range(TILES):
                        mm = pe.matmul(bank_e[:, 0, 2 * PARTS * q:2 * PARTS * (q + 1)],
                                       hot[b][:, t, 2 * q:2 * q + 2, :].rearrange("p e s -> p (e s)"),
                                       weight_parts[:, t, bass.ds(g * EG + 2 * q, 2), :].rearrange("p e i -> p (e i)"),
                                       start=(t == 0), stop=(t == TILES - 1))
                mm.then_inc(e_filled, 1)
                turn_hot(g, b, first, 0)
                down(g, b, 0)
                down(g, b, 1)
                turn_hot(g, b, first, 1)
                if not last:
                    gather(g + 1, 1 - b, False, 0, range(TILES // 2))
                down(g, b, 2)
                down(g, b, 3)
                turn_hot(g, b, first, 2)
                if not last:
                    gather(g + 1, 1 - b, False, 0, range(TILES // 2, TILES))
                turn_hot(g, b, first, 3)
                if not last:
                    gather(g + 1, 1 - b, False, 1, range(TILES))
                pe.wait_ge(part0_ready, g + 1)
                pe.wait_ge(part1_ready, g + 1)
                pe.wait_ge(part2_ready, g + 1)
                pe.wait_ge(t_read, PAIRS * (g + 1))
                for n in range(TILES // 2):
                    if not (first and n < 2):
                        pe.wait_ge(a_read[n % 2], 2 * g + n // 2)
                    for r in range(2):
                        t = 2 * n + r
                        for q in range(PAIRS):
                            for i in range(PARTS):
                                mm = pe.matmul(bank_a[n % 2][:, r, :], hotT[:, q, t * P:(t + 1) * P],
                                               ep[i][:, q, :], start=(q == 0 and i == 0),
                                               stop=(q == PAIRS - 1 and i == PARTS - 1))
                    mm.then_inc(a_filled[n % 2], 1)

            over_groups(pe, prologue, step)

        @block.scalar
        def _(act):
            def take_x(g):
                act.wait_ge(x_filled, KC * g + 1)
                act.copy(xgT[:, 0, :], bank_x[0][:]).then_inc(x_read[0], 1)

            def prologue():
                take_x(0)

            def step(g, i, b, first, last):
                act.wait_ge(up_filled, g + 1)
                if not first:
                    act.wait_ge(hidden_ready, g)
                act.activation(gate[:], bank_g[0:F2, :], ACT.Silu).then_inc(gate_ready, 1)
                def take_turned(q):
                    act.wait_ge(t_filled, PAIRS * g + q + 1)
                    act.copy(hotT[:, q, :], bank_t[:]).then_inc(t_read, 1)

                def weigh(q):
                    if q % 2 == 0:
                        act.wait_ge(e_filled, 3 * g + 2 + q // 2)
                    act.activation(eo[:, q, :], bank_e[:, q % 2, :], ACT.Copy,
                                   scale=slot_weight[:, q:q + 1]).then_inc(eo_ready, 1)

                take_turned(0)
                act.wait_ge(slot_weight_ready, 2 * (g + 1))
                if not first:
                    act.wait_ge(rest_ready, g)
                weigh(0)
                weigh(1)
                take_turned(1)
                weigh(2)
                weigh(3)
                act.wait_ge(eo_ready, PAIRS * (g + 1))
                if not first:
                    act.wait_ge(a_filled[1], 2 * g)
                act.copy(ep[0][:], eo[:]).then_inc(part0_ready, 1)
                take_turned(2)
                act.wait_ge(rest_ready, g + 1)
                act.copy(ep[1][:], eo_rest[:]).then_inc(part1_ready, 1)
                take_turned(3)
                if not last:
                    take_x(g + 1)

            over_groups(act, prologue, step)

        @block.gpsimd
        def _(pool):
            pool.iota(number[:], pattern=[[1, S]], base=0, channel_multiplier=0).then_inc(const_ready, 1)
            pool.wait_ge(const_ready, 1)
            pool.tensor_copy(slot[:], number[:]).then_inc(const_ready, 1)

        @block.vector
        def _(dve):
            def one_hot(g, b, used):
                if used is not None:
                    dve.wait_ge(t_filled, PAIRS * used)
                for t in range(TILES):
                    dve.tensor_tensor(hot[b][:, t], slot[:].unsqueeze(1).broadcast_to([P, EG, S]),
                                      slot_of[:, t, bass.ds(g * EG, EG)].unsqueeze(2).broadcast_to([P, EG, S]),
                                      ALU.is_equal).then_inc(hot_ready, 1)

            def take_x(g):
                dve.wait_ge(x_filled, KC * g + 2)
                dve.tensor_copy(xgT[:, 1, :], bank_x[1][:]).then_inc(x_read[1], 1)

            def prologue():
                dve.wait_ge(const_ready, 2)
                one_hot(0, 0, None)
                take_x(0)

            def step(g, i, b, first, last):
                if not last:
                    one_hot(g + 1, 1 - b, None if first else g)
                dve.wait_ge(gate_ready, g + 1)
                dve.tensor_tensor(hidden[:], gate[:], bank_u[0:F2, :], ALU.mult).then_inc(hidden_ready, 1)
                dve.wait_ge(e_filled, 3 * g + 1)
                dve.tensor_reduce(pair_weight[:], bank_e[:, 0, 0:2 * PARTS * PAIRS].rearrange(
                    "p (q j i) -> p q j i", q=PAIRS, j=2), AX_X, ALU.add).then_inc(e_read, 1)
                dve.wait_ge(e_read, g + 1)
                if not first:
                    dve.wait_ge(eo_ready, PAIRS * g)
                for j in range(2):
                    dve.tensor_copy(slot_weight[j * S:(j + 1) * S, :], pair_weight[j * S:(j + 1) * S, :, j])\
                        .then_inc(slot_weight_ready, 1)
                dve.wait_ge(part0_ready, g + 1)
                dve.tensor_tensor(eo_rest[:], eo[:], ep[0][:], ALU.subtract).then_inc(rest_ready, 1)
                dve.wait_ge(part1_ready, g + 1)
                dve.tensor_tensor(ep[2][:], eo_rest[:], ep[1][:], ALU.subtract).then_inc(part2_ready, 1)
                if not last:
                    take_x(g + 1)
                for n in range(TILES // 2):
                    dve.wait_ge(a_filled[n % 2], 2 * g + n // 2 + 1)
                    if not first:
                        dve.wait_ge(a_read[n % 2], 2 * g + n // 2)
                    part = core.x[:, 2 * n:2 * n + 2, :]
                    dve.tensor_tensor(part, part, bank_a[n % 2][:], ALU.add).then_inc(a_read[n % 2], 1)

            over_groups(dve, prologue, step)


def l2_ffn(nc, core, name, xn, t):
    with ExitStack() as ctx:
        def bf16(tensor, shape):
            return ctx.enter_context(nc.sbuf_tensor(f"{name}_{tensor}", shape, BF16))

        slot_of = bf16("slot_of", [P, TILES, EXPERTS2])
        parts = bf16("parts", [P, TILES, EXPERTS2, 3])
        xn_parts = [bf16(f"xn_part{i}", [P, TILES, D]) for i in range(3)]
        route_stage(nc, core, f"{name}_route", t["l2_router"], EXPERTS2, TOP2, slot_of=slot_of, parts=parts,
                    xn=xn, xn_parts=xn_parts)
        l2_routed_stage(nc, core, f"{name}_routed", xn_parts, slot_of, parts, t["l2_in_w"], t["l2_out_w"])
    gated_units_stage(nc, core, f"{name}_shared", F2, SHARED2, t["l2_shared_in_w"], t["l2_shared_out_w"])


def l1_ffn(nc, core, name, t):
    with nc.sbuf_tensor(f"{name}_weight_rows", [P, TOKENS], BF16) as weight_rows:
        route_stage(nc, core, f"{name}_route", t["l1_router"], EXPERTS1, TOP1, weight_rows=weight_rows)
        weighted_units_stage(nc, core, name, F1, UNITS1, t["l1_in_w"], t["l1_out_w"], OWNERS1, weight_rows,
                             t["l1_select"])


HIDDEN3 = 1024
CHUNKS3 = HIDDEN3 // P
BLOCK3 = 64
RANK3 = 16
KV3 = 4
REP3 = HEADS // KV3
WIN = 16
BLOCKS3 = SEQ // WIN
PER3 = P // WIN


def l3_decode_stage(nc, core, w_up, w_down, up_q, up_scale, up_a, up_b, down_q, down_scale, down_a, down_b):
    with Stage(nc, "l3_decode") as st:
        q_up = st.sb("q_up", [P, KC, HIDDEN3], I32)
        q_down = st.sb("q_down", [P, CHUNKS3, D], I32)
        s_up = st.sb("s_up", [P, KC, HIDDEN3])
        s_down = st.sb("s_down", [P, CHUNKS3, D])
        a_up = st.sb("a_up", [RANK3, D])
        b_up = st.sb("b_up", [RANK3, HIDDEN3])
        a_down = st.sb("a_down", [RANK3, HIDDEN3])
        b_down = st.sb("b_down", [RANK3, D])
        ps_up = [st.ps(f"ps_up{i}", [P, HALF]) for i in range(4)]
        ps_down = [st.ps(f"ps_down{i}", [P, 2, D]) for i in range(4)]
        up_loaded = st.sem("up_loaded")
        down_loaded = st.sem("down_loaded")
        rank_loaded = st.sem("rank_loaded")
        up_done = st.sem("up_done")
        down_done = st.sem("down_done")
        scaled = st.sem("scaled")
        block = st.block()
        G = P // BLOCK3

        @block.sync
        def _(sp):
            for dst, src in ((a_up, up_a), (b_up, up_b), (a_down, down_a), (b_down, down_b)):
                sp.dma_start(dst[:], src).then_inc(rank_loaded, 16)
            sp.dma_start(q_up[:], up_q.rearrange("(c p) n -> p c n", p=P)).then_inc(up_loaded, 16)
            for c in range(KC):
                for j in range(G):
                    sp.dma_start(s_up[j * BLOCK3:(j + 1) * BLOCK3, c, :],
                                 up_scale[G * c + j].partition_broadcast(BLOCK3)).then_inc(up_loaded, 16)

        @block.scalar
        def _(act):
            act.dma_start(q_down[:], down_q.rearrange("(c p) n -> p c n", p=P)).then_inc(down_loaded, 16)
            for j in range(G):
                act.dma_start(s_down[j * BLOCK3:(j + 1) * BLOCK3, :, :],
                              down_scale.rearrange("(c j) n -> j c n", j=G)[j].partition_broadcast(BLOCK3))\
                    .then_inc(down_loaded, 16)

        @block.tensor
        def _(pe):
            pe.wait_ge(rank_loaded, 64)
            for c in range(KC):
                for h in range(2):
                    mm = pe.matmul(ps_up[2 * c + h][:], a_up[:, c * P:(c + 1) * P],
                                   b_up[:, h * HALF:(h + 1) * HALF], start=True, stop=True)
            mm.then_inc(up_done, 1)
            for c in range(CHUNKS3):
                mm = pe.matmul(ps_down[c // 2][:, c % 2, :], a_down[:, c * P:(c + 1) * P], b_down[:],
                               start=True, stop=True)
            mm.then_inc(down_done, 1)

        @block.vector
        def _(dve):
            dve.wait_ge(up_loaded, 16 * (1 + KC * G))
            dve.scalar_tensor_tensor(out=w_up[:], in0=q_up[:], scalar=-7.5, in1=s_up[:],
                                     op0=ALU.add, op1=ALU.mult).then_inc(scaled, 1)
            dve.wait_ge(down_loaded, 16 * (1 + G))
            dve.scalar_tensor_tensor(out=w_down[:], in0=q_down[:], scalar=-7.5, in1=s_down[:],
                                     op0=ALU.add, op1=ALU.mult).then_inc(scaled, 1)
            dve.wait_ge(scaled, 1)
            dve.wait_ge(up_done, 1)
            for c in range(KC):
                for h in range(2):
                    part = w_up[:, c, h * HALF:(h + 1) * HALF]
                    dve.tensor_tensor(part, part, ps_up[2 * c + h][:], ALU.add)
            dve.wait_ge(scaled, 2)
            dve.wait_ge(down_done, 1)
            for i in range(4):
                part = w_down[:, 2 * i:2 * i + 2, :]
                dve.tensor_tensor(part, part, ps_down[i][:], ALU.add)


def l3_ffn_stage(nc, core, name, w_up, w_down, b_up, b_down):
    with Stage(nc, name) as st:
        bias = st.sb("bias", [P, CHUNKS3])
        row = st.sb("row", [P, D])
        hidden = st.sb("hidden", [P, CHUNKS3, TOKENS])
        NB = 4
        ps_up = [st.ps(f"ps_up{i}", [P, HALF]) for i in range(NB)]
        ps_down = [st.ps(f"ps_down{i}", [P, 2, D]) for i in range(4)]
        loaded = st.sem("loaded")
        up_done = st.sem("up_done")
        first_half = st.sem("first_half")
        second_half = st.sem("second_half")
        row_halved = st.sem("row_halved")
        row_added = st.sem("row_added")
        down_done = st.sem("down_done")
        block = st.block()

        @block.sync
        def _(sp):
            sp.dma_start(bias[:], b_up).then_inc(loaded, 16)
            sp.dma_start(row[:], b_down.partition_broadcast(P)).then_inc(loaded, 16)

        @block.tensor
        def _(pe):
            for f in range(CHUNKS3):
                for h in range(HALVES):
                    n = HALVES * f + h
                    if n >= NB:
                        pe.wait_ge((first_half, second_half)[h], f - 1)
                    for c in range(KC):
                        mm = pe.matmul(ps_up[n % NB][:], w_up[:, c, f * P:(f + 1) * P],
                                       core.xnT[:, c, h * HALF:(h + 1) * HALF], start=(c == 0), stop=(c == KC - 1))
                    mm.then_inc(up_done, 1)
            for t in range(TILES):
                pe.wait_ge(first_half if t < TILES // 2 else second_half, CHUNKS3)
                for f in range(CHUNKS3):
                    mm = pe.matmul(ps_down[t // 2][:, t % 2, :], hidden[:, f, t * P:(t + 1) * P], w_down[:, f, :],
                                   start=(f == 0), stop=(f == CHUNKS3 - 1))
                mm.then_inc(down_done, 1)

        @block.scalar
        def _(act):
            act.wait_ge(loaded, 32)
            for f in range(CHUNKS3):
                act.wait_ge(up_done, HALVES * f + 1)
                act.activation(hidden[:, f, 0:HALF], ps_up[HALVES * f % NB][:], ACT.Relu,
                               bias=bias[:, f:f + 1]).then_inc(first_half, 1)

        @block.vector
        def _(dve):
            dve.wait_ge(loaded, 32)
            dve.tensor_scalar(row[:], row[:], 0.5, None, ALU.mult).then_inc(row_halved, 1)
            dve.wait_ge(row_halved, 1)
            dve.tensor_tensor(core.x[:], core.x[:], row[:].unsqueeze(1).broadcast_to([P, TILES, D]), ALU.add)\
                .then_inc(row_added, 1)
            for f in range(CHUNKS3):
                dve.wait_ge(up_done, HALVES * f + 2)
                dve.tensor_scalar(hidden[:, f, HALF:2 * HALF], ps_up[(HALVES * f + 1) % NB][:], bias[:, f:f + 1],
                                  0.0, ALU.add, ALU.max).then_inc(second_half, 1)
            dve.wait_ge(row_added, 1)
            for q in range(4):
                dve.wait_ge(down_done, 2 * q + 2)
                part = core.x[:, 2 * q:2 * q + 2, :]
                dve.scalar_tensor_tensor(out=part, in0=ps_down[q][:], scalar=0.5, in1=part,
                                         op0=ALU.mult, op1=ALU.add)


def l3_attention(nc, core, weights, angles, head_rows, window, pool_w, w_out):
    SCALE = 1.0 / float(HEAD) ** 0.5
    GROUP = P // HEAD
    with ExitStack() as ctx:
        def sb(name, shape):
            return ctx.enter_context(nc.sbuf_tensor(f"l3a_{name}", shape, F32))

        qk = sb("qk", [P, TILES, (HEADS + KV3) * HEAD])
        v = sb("v", [P, TILES, KV3, HEAD])
        qT = sb("qT", [P, KC, TOKENS])
        oT = sb("oT", [P, KC, TOKENS])
        rope_qkv_stage(nc, core, "l3_qkv", weights, angles, HEADS + KV3, qk, KV3 * HEAD, lambda t: v[:, t, :, :])
        turn_stage(nc, core, "l3_turn", qk, KC, qT)
        with Stage(nc, "l3_heads") as st:
            taste = st.sb("taste", [P, 2, HEAD])
            rows = st.sb("rows", [P, GROUP])
            inside = st.sb("inside", [P, 2, P])
            diagonal = st.sb("diagonal", [P, P])
            term = [st.sb(f"term{b}", [P, 2, KV3, HEAD]) for b in range(2)]
            logit = st.sb("logit", [P, TILES, 2 * KV3])
            R = 2 * KV3
            NW = TOKENS // WIN
            peak = st.sb("peak", [R, NW])
            total = st.sb("total", [R, NW])
            share = st.sb("share", [R, TOKENS])
            both = st.sb("both", [P, TILES, 2, KV3])
            w = st.sb("w", [P, TILES, KV3])
            kw = st.sb("kw", [P, TILES, D])
            vw = st.sb("vw", [P, TILES, D])
            packed = st.sb("packed", [P, BATCH, KC, 2, P])
            z = [st.sb(f"z{b}", [P, D]) for b in range(2)]
            e = [st.sb(f"e{b}", [P, D]) for b in range(2)]
            prob = [st.sb(f"prob{b}", [P, D]) for b in range(2)]
            probT = [st.sb(f"probT{b}", [P, KC, P]) for b in range(2)]
            head_peak = st.sb("head_peak", [P, TILES, HEADS])
            head_total = st.sb("head_total", [P, TILES, HEADS])
            head_inverse = st.sb("head_inverse", [P, TILES, HEADS])
            ps_a = st.ps("ps_a", [P, HALVES, HALF])
            ps_w = st.ps("ps_w", [P, HALF])
            ps_s = [st.ps(f"ps_s{b}", [P, HALF]) for b in range(2)]
            ps_t = st.ps("ps_t", [P, HALF])
            ps_o = [st.ps(f"ps_o{b}", [P, HALF]) for b in range(2)]

            loaded = st.sem("loaded")
            rows_turned = st.sem("rows_turned")
            term_ready = st.sem("term_ready")
            logit_ready = st.sem("logit_ready")
            logit_turned = st.sem("logit_turned")
            step_done = st.sem("step_done")
            shifted = st.sem("shifted")
            exp_ready = st.sem("exp_ready")
            share_ready = st.sem("share_ready")
            share_turned = st.sem("share_turned")
            w_ready = st.sem("w_ready")
            kw_ready = st.sem("kw_ready")
            vw_ready = st.sem("vw_ready")
            block_summed = st.sem("block_summed")
            packed_ready = st.sem("packed_ready")
            scored = st.sem("scored")
            peak_ready = st.sem("peak_ready")
            z_ready = st.sem("z_ready")
            e_ready = st.sem("e_ready")
            total_ready = st.sem("total_ready")
            inverse_ready = st.sem("inverse_ready")
            prob_ready = st.sem("prob_ready")
            prob_turned = st.sem("prob_turned")
            probT_ready = st.sem("probT_ready")
            summed = st.sem("summed")
            o_copied = st.sem("o_copied")
            block = st.block()

            def keys(t):
                return qk[:, t, D:D + KV3 * HEAD].rearrange("p (h d) -> p h d", d=HEAD)

            def windows(ap):
                return ap.rearrange("p (n r) -> p n r", r=WIN)

            def repeated(ap):
                return ap.unsqueeze(2).broadcast_to([P, KV3, REP3, HEAD])

            def spread(t):
                return w[:, t, :].unsqueeze(2).unsqueeze(3).broadcast_to([P, KV3, REP3, HEAD])

            def wide(ap):
                return ap.rearrange("p (j r d) -> p j r d", j=KV3, r=REP3)

            def per_head(ap):
                return ap.rearrange("p (h s) -> p h s", h=HEADS)

            def across(ap, n, m):
                return ap.unsqueeze(2).broadcast_to([ap.shape[0], n, m])

            @block.sync
            def _(sp):
                sp.dma_start(taste[:], pool_w.partition_broadcast(P)).then_inc(loaded, 16)
                sp.dma_start(rows[:], head_rows).then_inc(loaded, 16)
                sp.dma_start(inside[:], window).then_inc(loaded, 16)

            @block.tensor
            def _(pe):
                pe.wait_ge(logit_ready, TILES)
                for t in range(TILES):
                    tr = pe.transpose(ps_a[0:R, t // 4, (t % 4) * P:(t % 4 + 1) * P], logit[:, t, :], core.ident[:])
                tr.then_inc(logit_turned, 1)
                pe.wait_ge(share_ready, 1)
                for t in range(TILES):
                    tr = pe.transpose(ps_w[:, t * R:(t + 1) * R], share[:, t * P:(t + 1) * P],
                                      core.ident[0:R, 0:R])
                tr.then_inc(share_turned, 1)
                for b in range(BATCH):
                    pe.wait_ge(kw_ready, 2 * b + 2)
                    pe.wait_ge(vw_ready, 2 * b + 2)
                    if b >= 2:
                        pe.wait_ge(packed_ready, b - 1)
                    for g in range(KC):
                        for j in range(2):
                            out = ps_a[:, b % 2, (2 * g + j) * P:(2 * g + j + 1) * P]
                            for par in range(2):
                                t = 2 * b + par
                                lhsT = kw[:, t, g * P:(g + 1) * P] if j == 0 else inside[:, par, :]
                                rhs = inside[:, par, :] if j == 0 else vw[:, t, g * P:(g + 1) * P]
                                mm = pe.matmul(out, lhsT, rhs, start=(par == 0), stop=(par == 1))
                    mm.then_inc(block_summed, 1)

                def scores(t):
                    pe.wait_ge(packed_ready, t // 2 + 1)
                    if t >= 2:
                        pe.wait_ge(z_ready, t - 1)
                    for g in range(KC):
                        mm = pe.matmul(ps_s[t % 2][:, g * P:(g + 1) * P], qT[:, g, t * P:(t + 1) * P],
                                       packed[:, t // 2, g, 0, :], start=True, stop=True)
                    mm.then_inc(scored, 1)

                def turn(t):
                    pe.wait_ge(prob_ready, t + 1)
                    if t >= 1:
                        pe.wait_ge(probT_ready, t)
                    for g in range(KC):
                        tr = pe.transpose(ps_t[:, g * P:(g + 1) * P], prob[t % 2][:, g * P:(g + 1) * P],
                                          core.ident[:])
                    tr.then_inc(prob_turned, 1)

                def values(t):
                    pe.wait_ge(probT_ready, t + 1)
                    if t >= 2:
                        pe.wait_ge(o_copied, t - 1)
                    for g in range(KC):
                        mm = pe.matmul(ps_o[t % 2][:, g * P:(g + 1) * P], packed[:, t // 2, g, 1, :],
                                       probT[t % 2][:, g, :], start=True, stop=True)
                    mm.then_inc(summed, 1)

                for t in range(TILES + 2):
                    if t < TILES:
                        scores(t)
                    if 1 <= t <= TILES:
                        turn(t - 1)
                    if t >= 2:
                        values(t - 2)

            @block.scalar
            def _(act):
                act.wait_ge(shifted, 1)
                act.activation(share[:], share[:], ACT.Exp).then_inc(exp_ready, 1)

                def copy_o(t):
                    act.wait_ge(summed, t + 1)
                    act.copy(oT[:, :, t * P:(t + 1) * P], ps_o[t % 2][:, 0:D].rearrange("p (c n) -> p c n", c=KC))\
                        .then_inc(o_copied, 1)

                for t in range(TILES):
                    act.wait_ge(z_ready, t + 1)
                    if t >= 2:
                        act.wait_ge(prob_ready, t - 1)
                    act.activation(e[t % 2][:], z[t % 2][:], ACT.Exp, scale=SCALE).then_inc(e_ready, 1)
                    if t >= 1:
                        act.wait_ge(prob_turned, t)
                        if t >= 3:
                            act.wait_ge(summed, t - 2)
                        act.copy(probT[(t - 1) % 2][:].rearrange("p c n -> p (c n)"), ps_t[:, 0:D])\
                            .then_inc(probT_ready, 1)
                    if t >= 2:
                        copy_o(t - 2)
                act.wait_ge(prob_turned, TILES)
                act.copy(probT[(TILES - 1) % 2][:].rearrange("p c n -> p (c n)"), ps_t[:, 0:D])\
                    .then_inc(probT_ready, 1)
                copy_o(TILES - 2)
                copy_o(TILES - 1)

            @block.gpsimd
            def _(pool):
                pool.wait_ge(loaded, 48)
                pool.tensor_copy(diagonal[:].rearrange("p (h d) -> p h d", d=HEAD), across(rows[:], GROUP, HEAD))\
                    .then_inc(rows_turned, 1)
                for t in range(TILES):
                    pool.wait_ge(w_ready, 1)
                    pool.tensor_tensor(wide(vw[:, t, :]), repeated(v[:, t, :, :]), spread(t), ALU.mult)\
                        .then_inc(vw_ready, 1)

            @block.vector
            def _(dve):
                steps = [0]

                def link(ins):
                    steps[0] += 1
                    ins.then_inc(step_done, 1)
                    dve.wait_ge(step_done, steps[0])

                dve.wait_ge(loaded, 48)
                for t in range(TILES):
                    if t >= 2:
                        dve.wait_ge(logit_ready, t - 1)
                    dve.tensor_tensor(term[t % 2][:], keys(t).unsqueeze(1).broadcast_to([P, 2, KV3, HEAD]),
                                      taste[:].unsqueeze(2).broadcast_to([P, 2, KV3, HEAD]), ALU.mult)\
                        .then_inc(term_ready, 1)
                    dve.wait_ge(term_ready, t + 1)
                    dve.tensor_reduce(logit[:, t, :].rearrange("p (a h) -> p a h", a=2), term[t % 2][:], AX_X,
                                      ALU.add).then_inc(logit_ready, 1)
                dve.wait_ge(logit_turned, 1)
                turned = ps_a[0:R, :, :].rearrange("p h n -> p (h n)")
                link(dve.tensor_reduce(peak[:], windows(turned), AX_X, ALU.max))
                dve.tensor_tensor(windows(share[:]), windows(turned), across(peak[:], NW, WIN), ALU.subtract)\
                    .then_inc(shifted, 1)
                dve.wait_ge(exp_ready, 1)
                link(dve.tensor_reduce(total[:], windows(share[:]), AX_X, ALU.add))
                link(dve.reciprocal(total[:], total[:]))
                dve.tensor_tensor(windows(share[:]), windows(share[:]), across(total[:], NW, WIN), ALU.mult)\
                    .then_inc(share_ready, 1)
                dve.wait_ge(share_turned, 1)
                link(dve.tensor_copy(both[:].rearrange("p t a h -> p (t a h)"), ps_w[:, 0:TILES * R]))
                link(dve.tensor_tensor(w[:], both[:, :, 0, :], both[:, :, 1, :], ALU.add))
                dve.tensor_scalar(w[:], w[:], 0.5, None, ALU.mult).then_inc(w_ready, 1)
                dve.wait_ge(w_ready, 1)
                for t in range(TILES):
                    dve.tensor_tensor(wide(kw[:, t, :]), repeated(keys(t)), spread(t), ALU.mult)\
                        .then_inc(kw_ready, 1)
                dve.wait_ge(rows_turned, 1)
                for b in range(BATCH):
                    dve.wait_ge(block_summed, b + 1)
                    dve.tensor_tensor(packed[:, b].rearrange("p g j n -> p (g j) n"),
                                      ps_a[:, b % 2, :].rearrange("p (g n) -> p g n", n=P),
                                      diagonal[:].unsqueeze(1).broadcast_to([P, 2 * KC, P]), ALU.mult)\
                        .then_inc(packed_ready, 1)

                def shift(t):
                    dve.wait_ge(scored, t + 1)
                    dve.tensor_reduce(head_peak[:, t, :], per_head(ps_s[t % 2][:, 0:D]), AX_X, ALU.max)\
                        .then_inc(peak_ready, 1)
                    dve.wait_ge(peak_ready, t + 1)
                    if t >= 2:
                        dve.wait_ge(e_ready, t - 1)
                    dve.tensor_tensor(per_head(z[t % 2][:]), per_head(ps_s[t % 2][:, 0:D]),
                                      across(head_peak[:, t, :], HEADS, BLOCKS3), ALU.subtract).then_inc(z_ready, 1)

                def normalise(t):
                    dve.wait_ge(e_ready, t + 1)
                    dve.tensor_reduce(head_total[:, t, :], per_head(e[t % 2][:]), AX_X, ALU.add)\
                        .then_inc(total_ready, 1)
                    dve.wait_ge(total_ready, t + 1)
                    dve.reciprocal(head_inverse[:, t, :], head_total[:, t, :]).then_inc(inverse_ready, 1)
                    dve.wait_ge(inverse_ready, t + 1)
                    if t >= 2:
                        dve.wait_ge(prob_turned, t - 1)
                    dve.tensor_tensor(per_head(prob[t % 2][:]), per_head(e[t % 2][:]),
                                      across(head_inverse[:, t, :], HEADS, BLOCKS3), ALU.mult).then_inc(prob_ready, 1)

                shift(0)
                for t in range(TILES):
                    if t + 1 < TILES:
                        shift(t + 1)
                    normalise(t)

        project_stage(nc, core, "l3_project", oT, w_out)


def build(nc, t, out):
    with ExitStack() as ctx:
        core = Core(nc, ctx)
        start_stage(nc, core, t["x"])

        with nc.sbuf_tensor("l0_w", [P, UNITS0, IN0 + D], F32) as w:
            norm_stage(nc, core)
            l0_ffn_stage(nc, core, "l0_ffn_a", w, (t["lut"], t["l0_in_idx"], t["l0_out_idx"]))
            norm_stage(nc, core)
            l0_attention(nc, core, t["l0_qkv"], t["angles"], t["head_rows"], t["l0_affine"], t["l0_wo"])
            norm_stage(nc, core)
            l0_ffn_stage(nc, core, "l0_ffn_b", w)

        norm_stage(nc, core)
        l1_ffn(nc, core, "l1_ffn_a", t)
        norm_stage(nc, core)
        l1_attention(nc, core, t["l1_wkv_a"], t["l1_norm_w"], t["l1_wq"], t["l1_wkv"], t["l1_columns"],
                     t["l1_sign"], t["l1_wo"], t["l1_bo"])
        norm_stage(nc, core)
        l1_ffn(nc, core, "l1_ffn_b", t)

        def l2_feed_forward(name):
            with nc.sbuf_tensor(f"{name}_xn", [P, TILES, D], F32) as xn:
                norm_stage(nc, core, xn)
                l2_ffn(nc, core, name, xn, t)

        l2_feed_forward("l2_ffn_a")
        norm_stage(nc, core)
        l2_attention(nc, core, t["l2_table"], t["l2_w_gates"], t["l2_b_gates"], t["l2_w_heads"], t["l2_conv"],
                     t["l2_ln_w"], t["l2_ln_b"], t["l2_wo"])
        l2_feed_forward("l2_ffn_b")

        w_up = ctx.enter_context(nc.sbuf_tensor("l3_w_up", [P, KC, HIDDEN3], F32))
        w_down = ctx.enter_context(nc.sbuf_tensor("l3_w_down", [P, CHUNKS3, D], F32))
        l3_decode_stage(nc, core, w_up, w_down, *(t[f"l3_{k}"] for k in (
            "up_q", "up_scale", "up_a", "up_b", "down_q", "down_scale", "down_a", "down_b_rank")))
        norm_stage(nc, core)
        l3_ffn_stage(nc, core, "l3_ffn_a", w_up, w_down, t["l3_bias_up"], t["l3_bias_down"])
        norm_stage(nc, core)
        l3_attention(nc, core, t["l3_qkv"], t["angles"], t["head_rows"], t["l3_window"], t["l3_pool"], t["l3_wo"])
        norm_stage(nc, core)
        l3_ffn_stage(nc, core, "l3_ffn_b", w_up, w_down, t["l3_bias_up"], t["l3_bias_down"])
        end_stage(nc, core, out)


def kernel(**inputs):
    import numpy as np
    import concourse.bacc as bacc
    from concourse.bass_utils import run_bass_kernel_spmd

    def arr(name):
        return np.asarray(inputs[name])

    def in_units(gate, up, units, f):
        g = gate.reshape(KC, P, units, f)
        u = up.reshape(KC, P, units, f)
        return np.stack([g, u], axis=3).transpose(2, 1, 0, 3, 4)

    def filled_up(idx):
        return np.concatenate([idx, np.full((UNITS0 * F0 - INTER0, D), NO_ENTRY, idx.dtype)])

    a = {
        "x": arr("L0_attn_x").reshape(TOKENS, D),
        "lut": arr("L0_ffn_lut"),
        "l0_in_idx": in_units(filled_up(arr("L0_ffn_gate_idx")).T, filled_up(arr("L0_ffn_up_idx")).T, UNITS0, F0)
        .reshape(UNITS0, P, IN0),
        "l0_out_idx": filled_up(arr("L0_ffn_down_idx").T).reshape(UNITS0, F0, D),
    }
    inv = (1.0 / np.float32(10000.0) ** (np.arange(0, HEAD, 2, dtype=np.float32) / HEAD)).astype(np.float32)
    theta = np.arange(SEQ, dtype=np.float32)[:, None] * inv[None, :]
    a["angles"] = np.stack([np.cos(theta), np.sin(theta)], 1).astype(np.float32).reshape(2, P, 2, HALF_HEAD)\
        .transpose(1, 0, 2, 3)
    a["head_rows"] = np.kron(np.eye(P // HEAD), np.ones((HEAD, 1))).astype(np.float32)
    a["l0_qkv"] = arr("L0_attn_w_qkv")
    a["l0_affine"] = np.tile(np.stack([arr("L0_attn_ln_scale"), arr("L0_attn_ln_bias")], axis=1), (P // HEAD, 1))
    a["l0_wo"] = arr("L0_attn_w_out")
    def in_l1(w, shared):
        return np.concatenate([w.transpose(1, 0, 2).reshape(D, -1), shared,
                               np.zeros((D, UNITS1 * F1 - INTER1), w.dtype)], axis=1)

    a["l1_in_w"] = in_units(*(in_l1(arr(f"L1_ffn_We_{k}"), arr(f"L1_ffn_Ws_{k}")) for k in ("gate", "up")),
                            UNITS1, F1)
    down = arr("L1_ffn_We_down")
    a["l1_out_w"] = np.concatenate([down.reshape(-1, D), arr("L1_ffn_Ws_down"),
                                    np.zeros((UNITS1 * F1 - INTER1, D), down.dtype)]).reshape(UNITS1, F1, D)
    owner = np.minimum(np.arange(UNITS1 * F1) // EXPERT1, EXPERTS1)
    a["l1_select"] = np.tile((owner == np.arange(OWNERS1)[:, None]).astype(np.float32), (3, 1))\
        .reshape(3 * OWNERS1, UNITS1, F1)
    a["l1_router"] = arr("L1_ffn_W_router")
    order = np.concatenate([np.arange(DH1 - ROPE1), DH1 - ROPE1 + np.arange(0, ROPE1, 2),
                            DH1 - ROPE1 + np.arange(1, ROPE1, 2)])
    wq = arr("L1_attn_wq_w").reshape(HEADS1, DH1, KC, P)[:, order]
    a["l1_wq"] = wq.transpose(0, 3, 2, 1)
    wkv = arr("L1_attn_wkv_b_w").reshape(2, HEADS1, DH1, LATENT)
    a["l1_wkv"] = np.concatenate([wkv[0][:, order], wkv[1]], axis=1).transpose(0, 2, 1)
    freqs = arr("L1_attn_freqs")[:HEADS1]
    one = np.ones((HEADS1, DH1 - ROPE1), np.float32)
    a["l1_columns"] = np.stack([arr("L1_attn_wq_b").reshape(HEADS1, DH1)[:, order]] +
                               [np.concatenate([one, freqs[:, :, k], freqs[:, :, k]], axis=1) for k in (0, 1)],
                               axis=2)
    a["l1_sign"] = np.concatenate([np.ones(P - ROPE1 // 2), -np.ones(ROPE1 // 2)]).astype(np.float32)[:, None]
    a["l1_wkv_a"] = arr("L1_attn_wkv_a_w").T
    a["l1_norm_w"] = arr("L1_attn_norm_w")
    a["l1_wo"] = arr("L1_attn_out_w").T.reshape(HEADS1, P, D)
    a["l1_bo"] = arr("L1_attn_out_b")
    a["l2_in_w"] = arr("L2_ffn_gate_up_proj").reshape(EXPERTS2, KC, P, 2, F2).transpose(0, 2, 1, 3, 4)
    a["l2_out_w"] = arr("L2_ffn_down_proj")
    a["l2_shared_in_w"] = in_units(*(arr(f"L2_ffn_shared_{k}_w").T for k in ("gate", "up")), SHARED2, F2)
    a["l2_shared_out_w"] = arr("L2_ffn_shared_down_w").T.reshape(SHARED2, F2, D)
    a["l2_router"] = arr("L2_ffn_gate_w").T
    a["l2_w_gates"] = np.concatenate([arr("L2_attn_Wa"), arr("L2_attn_Wb")], axis=1)
    a["l2_b_gates"] = np.concatenate([arr("L2_attn_ba"), arr("L2_attn_bb")])
    a["l2_w_heads"] = np.stack([arr(f"L2_attn_W{k}").reshape(KC, P, HEADS2, DH2) for k in "qkvg"])\
        .transpose(3, 2, 0, 1, 4)
    a["l2_conv"] = np.stack([
        np.concatenate([arr(f"L2_attn_{k}cw"), arr(f"L2_attn_{k}cb")[:, None]], axis=1)
        .reshape(HEADS2, DH2, TAPS + 1) for k in "qkv"], axis=2)
    a["l2_ln_w"], a["l2_ln_b"] = arr("L2_attn_ln_w"), arr("L2_attn_ln_b")
    a["l2_wo"] = arr("L2_attn_Wo").reshape(HEADS2, P, D)
    a["l3_up_q"] = arr("L3_ffn_w_up_q").T
    a["l3_up_scale"] = arr("L3_ffn_w_up_scale").T
    a["l3_up_a"] = arr("L3_ffn_w_up_lora_a").T
    a["l3_up_b"] = arr("L3_ffn_w_up_lora_b")
    a["l3_down_q"] = arr("L3_ffn_w_down_q").T
    a["l3_down_scale"] = arr("L3_ffn_w_down_scale").T
    a["l3_down_a"] = arr("L3_ffn_w_down_lora_a").T
    a["l3_down_b_rank"] = arr("L3_ffn_w_down_lora_b")
    a["l3_bias_up"] = arr("L3_ffn_b_up").reshape(CHUNKS3, P).T
    a["l3_bias_down"] = arr("L3_ffn_b_down")
    halves = np.concatenate([np.arange(0, HEAD, 2), np.arange(1, HEAD, 2)])
    a["l3_qkv"] = np.concatenate([
        arr("L3_attn_wq").reshape(D, HEADS, HEAD)[:, :, halves].reshape(D, D),
        arr("L3_attn_wk").reshape(D, KV3, HEAD)[:, :, halves].reshape(D, KV3 * HEAD),
        arr("L3_attn_wv")], axis=1)
    a["l3_pool"] = np.stack([arr("L3_attn_cwa")[halves], arr("L3_attn_cwb")[halves]])
    a["l3_wo"] = arr("L3_attn_wo")
    token, blocks = np.arange(P)[:, None, None], np.arange(P)[None, None, :] % BLOCKS3
    a["l3_window"] = (blocks == token // WIN + PER3 * np.arange(2)[None, :, None]).astype(np.float32)
    nc = bacc.Bacc("TRN2", target_bir_lowering=False, num_devices=1)
    arrays, t = {}, {}
    for name, v in a.items():
        v = np.ascontiguousarray(v)
        arrays[f"in_{name}"] = v
        t[name] = nc.dram_tensor(f"in_{name}", v.shape, mybir.dt.from_np(v.dtype), kind="ExternalInput").ap()
    t["l2_table"] = nc.dram_tensor("l2_table", [P, HEADS2, COLUMNS, TILES], F32, kind="Internal").ap()
    out = nc.dram_tensor("out", [TOKENS, D], F32, kind="ExternalOutput").ap()
    build(nc, t, out)
    r = run_bass_kernel_spmd(nc, [arrays], core_ids=[0])
    return np.asarray(r.results[0]["out"]).reshape(BATCH, SEQ, D)
```
